# Optimizing a Trainium2 kernel written in Bass

```python
import numpy as np
import jax
import jax.numpy as jnp

def _softmax(x, axis=-1):
    return jax.nn.softmax(x, axis=axis)

def _gelu(x):
    return jax.nn.gelu(x, approximate=True)

def _silu(x):
    return jax.nn.silu(x)

def _sigmoid(x):
    return jax.nn.sigmoid(x)

def _layernorm(x, axis=-1, eps=1e-05):
    m = jnp.mean(x, axis=axis, keepdims=True)
    v = jnp.var(x, axis=axis, keepdims=True)
    return (x - m) / jnp.sqrt(v + eps)

def _scatter_add(tgt, idx, src, axis=0):
    return tgt.at[idx].add(src)

def _segment_sum(src, seg, n):
    return jax.ops.segment_sum(src, seg, n)
kernel_name = 'mk_gnn_ffn_d2_gnn_r8_32e7d8'

def setup_inputs(seed: int=0):
    np.random.seed(seed)
    _w = jnp.asarray

    def _rec_inputs():
        import jax
        import jax.numpy as jnp
        _gk = jax.random.key(seed)
        x = -0.0005963 + 1.001 * jax.random.normal(jax.random.fold_in(_gk, 1), (512, 768), jnp.float32)
        src = jax.random.randint(jax.random.fold_in(_gk, 2), (8192,), 0, 512, jnp.int32)
        dst = jax.random.randint(jax.random.fold_in(_gk, 3), (8192,), 0, 512, jnp.int32)
        _o = jnp.argsort(dst, stable=True)
        src = src[_o]
        dst = dst[_o]
        edge_attr_256 = 0.000121155 + 1.00018 * jax.random.normal(jax.random.fold_in(_gk, 11), (8192, 256), jnp.float32)
        return (x, src, dst, edge_attr_256)
    x, src, dst, edge_attr_256 = _rec_inputs()

    def _L0_gnn_setup():
        import jax, jax.numpy as jnp
        import numpy as np
        N_NODES = 512
        N_EDGES = 16384
        D = 768
        DE = 256
        L = 3
        H = 8
        DH = D // H
        EPS = 1e-05

        def _layernorm(x, g, b):
            mu = jnp.mean(x, axis=-1, keepdims=True)
            var = jnp.var(x, axis=-1, keepdims=True)
            return (x - mu) * jax.lax.rsqrt(var + EPS) * g + b
        key = jax.random.key(seed)
        ks = jax.random.split(key, 20)
        s = 0.02
        inp = {'node_features': jax.random.normal(ks[0], (N_NODES, D), jnp.float32), 'edge_index': jax.random.randint(ks[1], (2, N_EDGES), 0, N_NODES, jnp.int64 if jax.config.x64_enabled else jnp.int32), 'edge_features': jax.random.normal(ks[2], (N_EDGES, DE), jnp.float32), 'Wn': jax.random.normal(ks[3], (D, D), jnp.float32) * s, 'bn': jnp.zeros((D,), jnp.float32), 'We': jax.random.normal(ks[4], (D, DE), jnp.float32) * s, 'be': jnp.zeros((D,), jnp.float32), 'W1': jax.random.normal(ks[5], (L, D, 2 * D), jnp.float32) * s, 'b1': jnp.zeros((L, D), jnp.float32), 'ln_g': jnp.ones((L, D), jnp.float32), 'ln_b': jnp.zeros((L, D), jnp.float32), 'W2': jax.random.normal(ks[6], (L, D, D), jnp.float32) * s, 'b2': jnp.zeros((L, D), jnp.float32), 'Wqkv': jax.random.normal(ks[7], (3 * D, D), jnp.float32) * s, 'bqkv': jnp.zeros((3 * D,), jnp.float32), 'Wo': jax.random.normal(ks[8], (D, D), jnp.float32) * s, 'bo': jnp.zeros((D,), jnp.float32)}
        return inp
    _L0_gnn_all = _L0_gnn_setup()
    _L0_gnn_in = {k: v for k, v in _L0_gnn_all.items() if k in ('Wn', 'bn', 'We', 'be', 'W1', 'b1', 'ln_g', 'ln_b', 'W2', 'b2', 'Wqkv', 'bqkv', 'Wo', 'bo')}
    del _L0_gnn_all

    def _L0_ffn_setup():
        import jax, jax.numpy as jnp
        import numpy as np
        B, N, C, E = (8, 1024, 768, 8)
        H = 2 * C
        key = jax.random.key(seed)
        ks = jax.random.split(key, 7)
        s = 0.02
        return {'x': jax.random.normal(ks[0], (B, N, C), dtype=jnp.float32), 'Wg': jax.random.normal(ks[1], (C, E), dtype=jnp.float32) * s, 'bg': jnp.zeros((E,), dtype=jnp.float32), 'W1': jax.random.normal(ks[2], (E, C, H), dtype=jnp.float32) * s, 'b1': jnp.zeros((E, H), dtype=jnp.float32), 'W2': jax.random.normal(ks[3], (E, H, C), dtype=jnp.float32) * s, 'b2': jnp.zeros((E, C), dtype=jnp.float32)}
    _L0_ffn_all = _L0_ffn_setup()
    _L0_ffn_in = {k: v for k, v in _L0_ffn_all.items() if k in ('Wg', 'bg', 'W1', 'b1', 'W2', 'b2')}
    del _L0_ffn_all

    def _L1_gnn_setup():
        import jax, jax.numpy as jnp
        import numpy as np
        N_NODES = 1250
        NEG_SLOPE = 0.2
        EPS = 1e-16

        def gat_layer(x, W, att_src, att_dst, bias, src, dst, heads, out_ch, concat):
            n = x.shape[0]
            h = (x @ W.T).reshape(n, heads, out_ch)
            a_src = jnp.einsum('nhc,hc->nh', h, att_src)
            a_dst = jnp.einsum('nhc,hc->nh', h, att_dst)
            e = a_src[src] + a_dst[dst]
            e = jax.nn.leaky_relu(e, NEG_SLOPE)
            m = jax.ops.segment_max(e, dst, num_segments=n)
            ex = jnp.exp(e - m[dst])
            denom = jax.ops.segment_sum(ex, dst, num_segments=n)
            alpha = ex / (denom[dst] + EPS)
            msg = alpha[:, :, None] * h[src]
            out = jax.ops.segment_sum(msg, dst, num_segments=n)
            if concat:
                out = out.reshape(n, heads * out_ch)
            else:
                out = out.mean(axis=1)
            return out + bias
        key = jax.random.key(seed)
        ks = jax.random.split(key, 12)
        x = jax.random.normal(ks[0], (N_NODES, 768), dtype=jnp.float32)
        edge_index = jax.random.randint(ks[1], (2, 20000), 0, N_NODES, dtype=jnp.int64)
        s1 = 1.0 / np.sqrt(768.0)
        W1 = jax.random.normal(ks[2], (8 * 128, 768), dtype=jnp.float32) * s1
        att_src1 = jax.random.normal(ks[3], (8, 128), dtype=jnp.float32) * (1.0 / np.sqrt(128.0))
        att_dst1 = jax.random.normal(ks[4], (8, 128), dtype=jnp.float32) * (1.0 / np.sqrt(128.0))
        b1 = jnp.zeros((8 * 128,), dtype=jnp.float32)
        s2 = 1.0 / np.sqrt(1024.0)
        W2 = jax.random.normal(ks[5], (1 * 768, 1024), dtype=jnp.float32) * s2
        att_src2 = jax.random.normal(ks[6], (1, 768), dtype=jnp.float32) * (1.0 / np.sqrt(768.0))
        att_dst2 = jax.random.normal(ks[7], (1, 768), dtype=jnp.float32) * (1.0 / np.sqrt(768.0))
        b2 = jnp.zeros((768,), dtype=jnp.float32)
        return {'x': x, 'edge_index': edge_index, 'W1': W1, 'att_src1': att_src1, 'att_dst1': att_dst1, 'b1': b1, 'W2': W2, 'att_src2': att_src2, 'att_dst2': att_dst2, 'b2': b2}
    _L1_gnn_all = _L1_gnn_setup()
    _L1_gnn_in = {k: v for k, v in _L1_gnn_all.items() if k in ('W1', 'att_src1', 'att_dst1', 'b1', 'W2', 'att_src2', 'att_dst2', 'b2')}
    del _L1_gnn_all

    def _L1_ffn_setup():
        import jax, jax.numpy as jnp
        import numpy as np
        B, T, E = (2, 1024, 768)
        H = 384
        N_EXP = 4
        key = jax.random.key(seed)
        ks = jax.random.split(key, 8)
        s_e = 1.0 / np.sqrt(E)
        s_h = 1.0 / np.sqrt(H)
        return {'x': jax.random.normal(ks[0], (B, T, E), dtype=jnp.float32), 'Wg': jax.random.uniform(ks[1], (E, N_EXP), minval=-s_e, maxval=s_e, dtype=jnp.float32), 'bg': jax.random.uniform(ks[2], (N_EXP,), minval=-s_e, maxval=s_e, dtype=jnp.float32), 'W1': jax.random.uniform(ks[3], (N_EXP, E, H), minval=-s_e, maxval=s_e, dtype=jnp.float32), 'b1': jax.random.uniform(ks[4], (N_EXP, H), minval=-s_e, maxval=s_e, dtype=jnp.float32), 'W2': jax.random.uniform(ks[5], (N_EXP, H, E), minval=-s_h, maxval=s_h, dtype=jnp.float32), 'b2': jax.random.uniform(ks[6], (N_EXP, E), minval=-s_h, maxval=s_h, dtype=jnp.float32)}
    _L1_ffn_all = _L1_ffn_setup()
    _L1_ffn_in = {k: v for k, v in _L1_ffn_all.items() if k in ('Wg', 'bg', 'W1', 'b1', 'W2', 'b2')}
    del _L1_ffn_all
    return {'x': x, 'src': src, 'dst': dst, 'edge_attr_256': edge_attr_256, 'L0_gnn_Wn': _L0_gnn_in['Wn'], 'L0_gnn_bn': _L0_gnn_in['bn'], 'L0_gnn_We': _L0_gnn_in['We'], 'L0_gnn_be': _L0_gnn_in['be'], 'L0_gnn_W1': _L0_gnn_in['W1'], 'L0_gnn_b1': _L0_gnn_in['b1'], 'L0_gnn_ln_g': _L0_gnn_in['ln_g'], 'L0_gnn_ln_b': _L0_gnn_in['ln_b'], 'L0_gnn_W2': _L0_gnn_in['W2'], 'L0_gnn_b2': _L0_gnn_in['b2'], 'L0_gnn_Wqkv': _L0_gnn_in['Wqkv'], 'L0_gnn_bqkv': _L0_gnn_in['bqkv'], 'L0_gnn_Wo': _L0_gnn_in['Wo'], 'L0_gnn_bo': _L0_gnn_in['bo'], 'L0_ffn_Wg': _L0_ffn_in['Wg'], 'L0_ffn_bg': _L0_ffn_in['bg'], 'L0_ffn_W1': _L0_ffn_in['W1'], 'L0_ffn_b1': _L0_ffn_in['b1'], 'L0_ffn_W2': _L0_ffn_in['W2'], 'L0_ffn_b2': _L0_ffn_in['b2'], 'L1_gnn_W1': _L1_gnn_in['W1'], 'L1_gnn_att_src1': _L1_gnn_in['att_src1'], 'L1_gnn_att_dst1': _L1_gnn_in['att_dst1'], 'L1_gnn_b1': _L1_gnn_in['b1'], 'L1_gnn_W2': _L1_gnn_in['W2'], 'L1_gnn_att_src2': _L1_gnn_in['att_src2'], 'L1_gnn_att_dst2': _L1_gnn_in['att_dst2'], 'L1_gnn_b2': _L1_gnn_in['b2'], 'L1_ffn_Wg': _L1_ffn_in['Wg'], 'L1_ffn_bg': _L1_ffn_in['bg'], 'L1_ffn_W1': _L1_ffn_in['W1'], 'L1_ffn_b1': _L1_ffn_in['b1'], 'L1_ffn_W2': _L1_ffn_in['W2'], 'L1_ffn_b2': _L1_ffn_in['b2']}

def reference(x, src, dst, edge_attr_256, L0_gnn_Wn, L0_gnn_bn, L0_gnn_We, L0_gnn_be, L0_gnn_W1, L0_gnn_b1, L0_gnn_ln_g, L0_gnn_ln_b, L0_gnn_W2, L0_gnn_b2, L0_gnn_Wqkv, L0_gnn_bqkv, L0_gnn_Wo, L0_gnn_bo, L0_ffn_Wg, L0_ffn_bg, L0_ffn_W1, L0_ffn_b1, L0_ffn_W2, L0_ffn_b2, L1_gnn_W1, L1_gnn_att_src1, L1_gnn_att_dst1, L1_gnn_b1, L1_gnn_W2, L1_gnn_att_src2, L1_gnn_att_dst2, L1_gnn_b2, L1_ffn_Wg, L1_ffn_bg, L1_ffn_W1, L1_ffn_b1, L1_ffn_W2, L1_ffn_b2):
    import jax
    import jax.numpy as jnp

    def _L0_gnn_ref(node_features, edge_index, edge_features, Wn, bn, We, be, W1, b1, ln_g, ln_b, W2, b2, Wqkv, bqkv, Wo, bo):
        import jax, jax.numpy as jnp
        import numpy as np
        N_NODES = 512
        N_EDGES = 16384
        D = 768
        DE = 256
        L = 3
        H = 8
        DH = D // H
        EPS = 1e-05

        def _layernorm(x, g, b):
            mu = jnp.mean(x, axis=-1, keepdims=True)
            var = jnp.var(x, axis=-1, keepdims=True)
            return (x - mu) * jax.lax.rsqrt(var + EPS) * g + b
        n = node_features.shape[0]
        nodes = node_features @ Wn.T + bn
        edge_proj = edge_features @ We.T + be
        src, dst = (edge_index[0], edge_index[1])
        for l in range(L):
            msgs = nodes[src] + nodes[dst] + edge_proj
            agg = jax.ops.segment_sum(msgs, dst, num_segments=n)
            combined = jnp.concatenate([nodes, agg], axis=-1)
            h = combined @ W1[l].T + b1[l]
            h = _layernorm(h, ln_g[l], ln_b[l])
            h = jax.nn.relu(h)
            h = h @ W2[l].T + b2[l]
            nodes = h + nodes
        qkv = nodes @ Wqkv.T + bqkv
        q, k, v = jnp.split(qkv, 3, axis=-1)
        q = q.reshape(n, H, DH) * DH ** (-0.5)
        k = k.reshape(n, H, DH)
        v = v.reshape(n, H, DH)
        scores = jnp.einsum('nhd,mhd->hnm', q, k)
        probs = jax.nn.softmax(scores, axis=-1)
        attn = jnp.einsum('hnm,mhd->nhd', probs, v).reshape(n, D)
        attended = attn @ Wo.T + bo
        return nodes + attended

    def _L0_ffn_ref(x, Wg, bg, W1, b1, W2, b2):
        import jax, jax.numpy as jnp
        import numpy as np
        B, N, C, E = (8, 1024, 768, 8)
        H = 2 * C
        gates = jax.nn.softmax(x @ Wg + bg, axis=-1)
        topg, topi = jax.lax.top_k(gates, 2)
        topg = topg / jnp.sum(topg, axis=-1, keepdims=True)
        h = jnp.einsum('bnc,ech->ebnh', x, W1) + b1[:, None, None, :]
        h = jax.nn.gelu(h, approximate=False)
        y = jnp.einsum('ebnh,ehc->bnec', h, W2) + b2[None, None, :, :]
        sel = jnp.take_along_axis(y, topi[..., :, None], axis=2)
        out = jnp.sum(sel * topg[..., None], axis=2)
        return out

    def _L1_gnn_ref(x, edge_index, W1, att_src1, att_dst1, b1, W2, att_src2, att_dst2, b2):
        import jax, jax.numpy as jnp
        import numpy as np
        N_NODES = 1250
        NEG_SLOPE = 0.2
        EPS = 1e-16

        def gat_layer(x, W, att_src, att_dst, bias, src, dst, heads, out_ch, concat):
            n = x.shape[0]
            h = (x @ W.T).reshape(n, heads, out_ch)
            a_src = jnp.einsum('nhc,hc->nh', h, att_src)
            a_dst = jnp.einsum('nhc,hc->nh', h, att_dst)
            e = a_src[src] + a_dst[dst]
            e = jax.nn.leaky_relu(e, NEG_SLOPE)
            m = jax.ops.segment_max(e, dst, num_segments=n)
            ex = jnp.exp(e - m[dst])
            denom = jax.ops.segment_sum(ex, dst, num_segments=n)
            alpha = ex / (denom[dst] + EPS)
            msg = alpha[:, :, None] * h[src]
            out = jax.ops.segment_sum(msg, dst, num_segments=n)
            if concat:
                out = out.reshape(n, heads * out_ch)
            else:
                out = out.mean(axis=1)
            return out + bias
        src, dst = (edge_index[0], edge_index[1])
        h = gat_layer(x, W1, att_src1, att_dst1, b1, src, dst, heads=8, out_ch=128, concat=True)
        h = jax.nn.relu(h)
        out = gat_layer(h, W2, att_src2, att_dst2, b2, src, dst, heads=1, out_ch=768, concat=True)
        return out

    def _L1_ffn_ref(x, Wg, bg, W1, b1, W2, b2):
        import jax, jax.numpy as jnp
        import numpy as np
        B, T, E = (2, 1024, 768)
        H = 384
        N_EXP = 4
        gate_logits = jnp.einsum('bte,en->btn', x, Wg) + bg
        top = jnp.argmax(gate_logits, axis=-1)
        h = jax.nn.gelu(jnp.einsum('bte,neh->nbth', x, W1) + b1[:, None, None, :], approximate=False)
        y = jnp.einsum('nbth,nhe->nbte', h, W2) + b2[:, None, None, :]
        onehot = jax.nn.one_hot(top, N_EXP, dtype=x.dtype)
        out = jnp.einsum('nbte,btn->bte', y, onehot)
        return out
    edge_index = jnp.stack([src, dst])
    x = x + _L0_gnn_ref(_layernorm(x, axis=-1), edge_index, edge_attr_256, L0_gnn_Wn, L0_gnn_bn, L0_gnn_We, L0_gnn_be, L0_gnn_W1, L0_gnn_b1, L0_gnn_ln_g, L0_gnn_ln_b, L0_gnn_W2, L0_gnn_b2, L0_gnn_Wqkv, L0_gnn_bqkv, L0_gnn_Wo, L0_gnn_bo)
    x = x + _L0_ffn_ref(_layernorm(x, axis=-1)[None], L0_ffn_Wg, L0_ffn_bg, L0_ffn_W1, L0_ffn_b1, L0_ffn_W2, L0_ffn_b2)[0]
    x = x + _L1_gnn_ref(_layernorm(x, axis=-1), edge_index, L1_gnn_W1, L1_gnn_att_src1, L1_gnn_att_dst1, L1_gnn_b1, L1_gnn_W2, L1_gnn_att_src2, L1_gnn_att_dst2, L1_gnn_b2)
    x = x + _L1_ffn_ref(_layernorm(x, axis=-1)[None], L1_ffn_Wg, L1_ffn_bg, L1_ffn_W1, L1_ffn_b1, L1_ffn_W2, L1_ffn_b2)[0]
    return x

_drawn_inputs = setup_inputs


def setup_inputs(seed=0):
    import zlib

    import numpy as np

    out = dict(_drawn_inputs(seed))
    spreads = {'L0_gnn_bn': (0.0, 0.1),
     'L0_gnn_be': (0.0, 0.1),
     'L0_gnn_b1': (0.0, 0.289),
     'L0_gnn_ln_g': (1.0, 0.2),
     'L0_gnn_ln_b': (0.0, 0.1),
     'L0_gnn_b2': (0.0, 0.1),
     'L0_gnn_bqkv': (0.0, 0.1),
     'L0_gnn_bo': (0.0, 0.1),
     'L0_ffn_bg': (0.0, 0.1),
     'L0_ffn_b1': (0.0, 0.279),
     'L0_ffn_b2': (0.0, 0.1),
     'L1_gnn_b1': (0.0, 0.1),
     'L1_gnn_b2': (0.0, 0.1)}
    factors = {'L1_gnn_att_dst1': 3.347,
     'L1_gnn_att_src2': 7.316,
     'L1_gnn_att_dst2': 28.778,
     'L1_ffn_b1': 8.0,
     'L1_ffn_b2': 2.808}
    for name, (base, spread) in spreads.items():
        noise = np.random.default_rng([zlib.crc32(name.encode()), seed]).standard_normal(out[name].shape)
        drawn = base * np.exp(spread * noise) if base else spread * noise
        out[name] = jnp.asarray(drawn.astype(out[name].dtype))
    for name, factor in factors.items():
        out[name] = (out[name] * factor).astype(out[name].dtype)
    return out
```

```python
from contextlib import ExitStack

import concourse.bass as bass
from concourse import mybir

P = 128
F32 = mybir.dt.float32
F32R = mybir.dt.float32r
I32 = mybir.dt.int32
ALU = mybir.AluOpType
ACT = mybir.ActivationFunctionType
AX_X = mybir.AxisListType.X

N = 512
NT = N // P
D = 768
DC = D // P
HALF = D // 2
DE = 256
E = 8192
L = 3
NH, DH = 8, 96
NE0, H0 = 8, 1536
NE1, H1 = 4, 384
GH, GC = 8, 128
GD = GH * GC
EPS = 1e-5
DEN_EPS = 1e-16
NONE = -1e30
FLOOR = -1e25

NEWTON = 4

RING = 4
STATS_STEPS = 3 * NT + 3 + 3 * NEWTON
GROUP = 8
GROUPS = E // P // GROUP

STAGES = [
    ("xt0", 3, 3), ("wn", 3, 3), ("tok0", 4, 4), ("edges", 4, 2), ("deg", 0, 1), ("base", 0, DC),
    ("rounds", L * 10, L * 24), ("v", 0, 8), ("heads", NH * 7, NH * 4), ("wo", 0, 8),
    ("xt1", 3, 3), ("gate0", 0, 2), ("bias0", 0, 8), ("experts0", NE0 * 12, NE0 * 8),
    ("xt2", 3, 3), ("h1", 4, 4), ("mask", 0, 4), ("gat1", 0, GH * 7), ("o1t", 4, 4), ("h2", 4, 4),
    ("gat2", 0, 13), ("xt3", 3, 3), ("gate1", 0, 2), ("bias1", 0, 8), ("experts1", NE1 * 3, NE1 * 8),
]
ACT0, DVE0 = {}, {}
_a = _v = 0
for _name, _da, _dv in STAGES:
    ACT0[_name], DVE0[_name] = _a, _v
    _a, _v = _a + _da, _v + _dv
ACT0["end"], DVE0["end"] = _a, _v

COLS = {}
_c = 0
for _name, _w in [("bn", DC), ("be", DC), ("ln_g", L * DC), ("ln_b", L * DC), ("b2", L * DC),
                  ("bq", NH), ("bk", NH), ("e0b1", NE0 * H0 // P), ("e1b1", NE1 * H1 // P),
                  ("prio", NT * 8)]:
    COLS[_name] = _c
    _c += _w
NCOLS = _c
ROWS = {}
_c = 0
for _name, _w in [("b1", L * D), ("bv", D), ("bo", D), ("g_b1", GD), ("g_src1", GD), ("g_dst1", GD),
                  ("g_b2", D), ("g_src2", D), ("g_dst2", D), ("bg0", NE0), ("bg1", NE1)]:
    ROWS[_name] = _c
    _c += _w
NROWS = _c


def wait(eng, sem, value):
    if not isinstance(value, int) or value > 0:
        eng.wait_ge(sem, value)


def build(nc, x, src, dst, edge, cols, rows, ident_d, iota_d, wn, we, w1, w2, wqkv, wo, wg0, e0w1,
          e0w2, e0b2, gw1, gw2, wg1, e1w1, e1w2, e1b2, out):
    ctx = ExitStack()
    with ctx:
        start = (nc.sbuf_base + 63) // 64 * 64
        top = [0]

        def place(name, shape, dt, at=None):
            size = 1
            for s in shape[1:]:
                size *= s
            if at is None:
                at = top[0]
                top[0] += (size + 7) // 8 * 8
            return nc.alloc_sbuf_tensor_at(name, shape, dt, offset=start + 4 * at)

        def sem(name):
            return ctx.enter_context(nc.semaphore(name))

        slot = [place(f"slot{s}", [P, 4608], F32) for s in range(4)]
        ident = place("ident", [P, P], F32)
        ones = place("ones", [P, P], F32)
        par = place("par", [P, NCOLS], F32)
        xres = place("xres", [P, NT, D], F32)
        ct = place("ct", [P, NT, N], F32)
        cpt_at = top[0]
        cpt = place("cpt", [P, NT, N], F32)
        mask = place("mask", [P, NT, N], F32, cpt_at)
        bc_at = top[0]
        brow = place("brow", [P, 2, D], F32)
        bns = place("bns", [P, NT, 2, 6], F32)
        mv = place("mv", [P, NT, 2], F32)
        rstd = place("rstd", [P, NT], F32)
        root = place("root", [P, 2, NT], F32)
        nbias = place("nbias", [P, 2, NT], F32)
        rsum = place("rsum", [P, 2, NT], F32)
        rinv = place("rinv", [P, 2, NT], F32)
        logit = place("logit", [P, NT, 8], F32)
        prob = place("prob", [P, NT, 8], F32)
        pick = [place(f"pick{i}", [P, NT, 8], F32) for i in range(4)]
        top4 = place("top4", [P, NT], F32)
        gate = place("gate", [P, NT, 8], F32)
        gate_t = place("gate_t", [8, N], F32)
        wg = place("wg", [P, DC, 8], F32)
        bg = place("bg", [P, 12], F32)
        att = place("att", [P, 2, NT, GH], F32)
        gmax = place("gmax", [P, 2, NT], F32)
        gdec = place("gdec", [P, 2, 4, NT], F32)
        area = top[0]

        def over(name, shape, at, dt=F32):
            return place(name, shape, dt, area + at)

        nodes = over("nodes", [P, NT, D], 0)
        nodes_t = over("nodes_t", [P, DC, N], 3072)
        xn = over("xn", [P, NT, D], 0)
        xn_t = over("xn_t", [P, DC, N], 6144)
        ea_raw = over("ea_raw", [P, 2, GROUP, DE], 6144)
        ea_hi = over("ea_hi", [P, 2, GROUP, DE], 10240, F32R)
        ea_lo = over("ea_lo", [P, 2, GROUP, DE], 14336, F32R)
        hot_d = over("hot_d", [P, 2, N], 18432, F32R)
        hot_s = over("hot_s", [P, 2, N], 19456, F32R)
        iota = over("iota", [P, N], 20480)
        ends_i = over("ends_i", [P, 2, E // P], 20992, I32)
        ends = over("ends", [P, 2, E // P], 21120)
        sea_t = over("sea_t", [P, DE // P, N], 21248)
        zero = over("zero", [P, N], 22272, F32R)
        deg = over("deg", [P, N], 22784)
        agg_t = over("agg_t", [P, DC, N], 6144)
        base_t = over("base_t", [P, DC, N], 9216)
        h = over("h", [P, NT, D], 12288)
        h_t = over("h_t", [P, DC, N], 15360)
        v = over("v", [P, NT, D], 12288)
        attn_t = over("attn_t", [DH, NH, N], 6144)
        q_t = over("q_t", [DH, 2, N], 10240)
        k_t = over("k_t", [DH, 2, N], 11264)
        prb = over("prb", [P, 2, NT, N], 15360)
        prb_t = over("prb_t", [P, NT, N], 19456)
        xn1 = over("xn1", [P, NT, D], 0)
        xn1_t = over("xn1_t", [P, DC, N], 3072)
        eh_t = over("eh_t", [P, H0 // P, N], 6144)
        e0b2_s = over("e0b2_s", [NE0, D], 12288)
        xn2 = over("xn2", [P, NT, D], 0)
        xn2_t = over("xn2_t", [P, DC, N], 3072)
        h1x = over("h1x", [P, NT, GH, GC + 2], 6144)
        out1 = over("out1", [P, NT, GD], 0)
        g_b1 = over("g_b1", [P, GD], 4096)
        g_b2 = over("g_b2", [P, D], 5120)
        h2x = over("h2x", [P, NT, D + 2], 6144)
        att1 = over("att1", [P, 2, GD], 10304)
        scr = over("scr", [P, GD], 12352)
        arg = over("arg", [P, 2, NT, N], 10304)
        arg2 = over("arg2", [P, NT, N], 14400)
        gp = over("gp", [P, NT, N], 16448)
        gp_t = over("gp_t", [P, NT, N], 18496)
        out1_t = over("out1_t", [P, GD // P, N], 10304)
        xn3 = over("xn3", [P, NT, D], 0)
        xn3_t = over("xn3_t", [P, DC, N], 3072)
        eh1_t = over("eh1_t", [P, 2, H1 // P, N], 6144)
        e1b2_s = over("e1b2_s", [NE1, D], 12288)

        act_ps = [ctx.enter_context(nc.psum_tensor(f"act_ps{i}", [P, N], F32)) for i in range(RING)]
        dve_ps = [ctx.enter_context(nc.psum_tensor(f"dve_ps{i}", [P, N], F32)) for i in range(RING)]

        pe_to_act = sem("pe_to_act")
        pe_to_dve = sem("pe_to_dve")
        act_freed = sem("act_freed")
        dve_freed = sem("dve_freed")
        slot_in = [sem(f"slot_in{s}") for s in range(4)]
        in_x = sem("in_x")
        in_par = sem("in_par")
        in_ends = sem("in_ends")
        in_edge = [sem("in_edge0"), sem("in_edge1")]
        in_row = [sem("in_row0"), sem("in_row1")]
        in_gate = sem("in_gate")
        in_eb2 = sem("in_eb2")
        in_att1 = sem("in_att1")
        in_gb = sem("in_gb")
        in_gate1 = sem("in_gate1")
        out_done = sem("out_done")
        dve_step = sem("dve_step")
        act_step = sem("act_step")
        normed = sem("normed")
        const_set = sem("const_set")
        ea_split = sem("ea_split")
        ea_high = sem("ea_high")
        hots = sem("hots")
        chunk_done = sem("chunk_done")
        cpt_set = sem("cpt_set")
        row_max = sem("row_max")
        exp_done = sem("exp_done")
        prob_set = sem("prob_set")
        logit_set = sem("logit_set")
        prob_exp = sem("prob_exp")
        gate_set = sem("gate_set")
        att_set = sem("att_set")
        g_max = sem("g_max")
        g_low = sem("g_low")
        g_arg = sem("g_arg")
        g_exp = sem("g_exp")

        block = ctx.enter_context(nc.Block())

        def bview(name, width):
            return rows[ROWS[name]:ROWS[name] + width].partition_broadcast(P)

        def col(name, i, n=1):
            return par[:, COLS[name] + i:COLS[name] + i + n]

        def k_unit(hd):
            return 0 if hd == 0 else 1 + 7 * (hd - 1) + 4

        def score_unit(hd):
            return 1 + 7 * hd

        def turn_unit_a(hd):
            return 1 + 7 * hd + 4 + (1 if hd < NH - 1 else 0)

        def q_unit(hd):
            return 0 if hd == 0 else 1 + 4 * (hd - 1)

        def turn_unit_v(hd):
            return 1 + 4 * hd + (1 if hd < NH - 1 else 0)

        def pv_unit(hd):
            return turn_unit_v(hd) + 2

        @block.sync
        def _(sp):
            def load(s, dst, source):
                sp.dma_start(dst, source).then_inc(slot_in[s], 16)

            def kview(ap):
                return ap.rearrange("(k p) n -> p k n", p=P)

            def sview(s, k, n):
                return slot[s][:, 0:k * n].rearrange("p (k n) -> p k n", k=k)

            sp.dma_start(xres[:, :, :], x.rearrange("(t p) d -> p t d", p=P)).then_inc(in_x, 16)
            sp.dma_start(ident[:, :], ident_d).then_inc(in_par, 16)
            sp.dma_start(par[:, :], cols).then_inc(in_par, 16)
            load(0, sview(0, DC, D), kview(wn))
            sp.dma_start(iota[:, :], iota_d.partition_broadcast(P)).then_inc(in_ends, 16)
            sp.dma_start(ends_i[:, 0, :], src).then_inc(in_ends, 16)
            sp.dma_start(ends_i[:, 1, :], dst).then_inc(in_ends, 16)
            wait(sp, pe_to_act, ACT0["tok0"])
            wait(sp, pe_to_dve, DVE0["tok0"])

            def load_edges(g, b):
                sp.dma_start(ea_raw[:, b, :, :],
                             edge[bass.ds(g * GROUP * P, GROUP * P), :].rearrange("(c p) d -> p c d", p=P)
                             ).then_inc(in_edge[b], 16)

            for b in range(2):
                load_edges(b, b)
            load(1, sview(1, DE // P, D), kview(we))
            load(2, sview(2, DC, D), kview(w1[0, 0:D, :]))
            load(3, sview(3, DC, D), kview(w1[0, D:2 * D, :]))
            load(0, sview(0, DC, D), kview(w2[0]))
            sp.dma_start(brow[:, 0, :], bview("b1", D)).then_inc(in_row[0], 16)
            sp.dma_start(brow[:, 1, :], bview("bv", D)).then_inc(in_row[1], 16)
            with sp.Fori(1, GROUPS // 2) as i:
                for b in range(2):
                    sp.wait_ge(ea_split, 2 * i - 1 + b)
                    load_edges(2 * i + b, b)
            with sp.Fori(1, L) as l:
                sp.wait_ge(pe_to_dve, DVE0["rounds"] + 24 * (l - 1) + 14)
                load(2, sview(2, DC, D), kview(w1[bass.ds(l, 1), 0:D, :].rearrange("a k n -> (a k) n")))
                load(3, sview(3, DC, D), kview(w1[bass.ds(l, 1), D:2 * D, :].rearrange("a k n -> (a k) n")))
                sp.wait_ge(dve_freed, DVE0["rounds"] + 24 * (l - 1) + 14)
                sp.dma_start(brow[:, 0, :], rows[bass.ds(ROWS["b1"] + l * D, D)].partition_broadcast(P)
                             ).then_inc(in_row[0], 16)
                sp.wait_ge(pe_to_dve, DVE0["rounds"] + 24 * (l - 1) + 20)
                load(0, sview(0, DC, D), kview(w2[bass.ds(l, 1), :, :].rearrange("a k n -> (a k) n")))
            last = DVE0["rounds"] + 24 * (L - 1)
            load(1, sview(1, DC, D), kview(wqkv[:, 0:D]))
            sp.wait_ge(pe_to_dve, last + 14)
            load(2, sview(2, DC, D), kview(wqkv[:, D:2 * D]))
            load(3, sview(3, DC, D), kview(wqkv[:, 2 * D:3 * D]))
            sp.wait_ge(dve_freed, last + 14)
            sp.dma_start(brow[:, 0, :], bview("bo", D)).then_inc(in_row[0], 16)
            sp.wait_ge(pe_to_dve, last + 20)
            load(0, slot[0][0:DH, 0:4 * D].rearrange("p (k n) -> p k n", k=4),
                 wo[0:4 * DH, :].rearrange("(k p) n -> p k n", p=DH))
            sp.dma_start(wg[:, :, :], wg0.rearrange("(k p) n -> p k n", p=P)).then_inc(in_gate, 16)
            sp.dma_start(bg[:, 0:NE0], bview("bg0", NE0)).then_inc(in_gate, 16)
            sp.dma_start(bg[:, 8:8 + NE1], bview("bg1", NE1)).then_inc(in_gate, 16)
            sp.wait_ge(pe_to_act, ACT0["heads"] + k_unit(NH - 1) + 1)
            sp.wait_ge(pe_to_dve, DVE0["heads"] + q_unit(NH - 1) + 1)
            load(1, slot[1][0:DH, 0:4 * D].rearrange("p (k n) -> p k n", k=4),
                 wo[4 * DH:8 * DH, :].rearrange("(k p) n -> p k n", p=DH))

            def expert0(e, wait_up, wait_down):
                wait_up()
                up = e0w1[bass.ds(e, 1), :, :].rearrange("a k n -> (a k) n")
                down = e0w2[bass.ds(e, 1), :, :].rearrange("a k n -> (a k) n")
                load(2, sview(2, DC, D), kview(up[:, 0:D]))
                load(3, sview(3, DC, D), kview(up[:, D:2 * D]))
                wait_down()
                load(0, sview(0, DC, D), kview(down[0:D, :]))
                load(1, sview(1, DC, D), kview(down[D:2 * D, :]))

            expert0(0, lambda: None, lambda: sp.wait_ge(pe_to_dve, DVE0["xt1"]))
            sp.dma_start(e0b2_s[:, :], e0b2).then_inc(in_eb2, 16)
            with sp.Fori(1, NE0) as e:
                expert0(e, lambda: sp.wait_ge(pe_to_act, ACT0["experts0"] + 12 * e),
                        lambda: sp.wait_ge(pe_to_dve, DVE0["experts0"] + 8 * e))
            sp.wait_ge(pe_to_act, ACT0["xt2"])
            load(2, sview(2, DC, N), kview(gw1[:, 0:N]))
            load(3, sview(3, DC, N), kview(gw1[:, N:2 * N]))
            sp.wait_ge(pe_to_dve, DVE0["xt2"])
            load(0, sview(0, 4, D), kview(gw2[0:N, :]))
            load(1, sview(1, 4, D), kview(gw2[N:2 * N, :]))
            sp.dma_start(att1[:, :, :], rows[ROWS["g_src1"]:ROWS["g_src1"] + 2 * GD]
                         .rearrange("(a n) -> a n", a=2).partition_broadcast(P)).then_inc(in_att1, 16)
            sp.dma_start(brow[:, :, :], rows[ROWS["g_src2"]:ROWS["g_src2"] + 2 * D]
                         .rearrange("(a n) -> a n", a=2).partition_broadcast(P)).then_inc(in_row[0], 16)
            sp.wait_ge(pe_to_act, ACT0["mask"])
            sp.wait_ge(pe_to_dve, DVE0["mask"])
            sp.dma_start(g_b1[:, :], bview("g_b1", GD)).then_inc(in_gb, 16)
            sp.dma_start(g_b2[:, :], bview("g_b2", D)).then_inc(in_gb, 16)

            def expert1(n, s):
                load(s, slot[s][:, 0:DC * H1].rearrange("p (k n) -> p k n", k=DC),
                     kview(e1w1[bass.ds(n, 1), :, :].rearrange("a k n -> (a k) n")))
                load(s, slot[s][:, DC * H1:DC * H1 + 3 * D].rearrange("p (k n) -> p k n", k=3),
                     kview(e1w2[bass.ds(n, 1), :, :].rearrange("a k n -> (a k) n")))

            expert1(0, 2)
            expert1(1, 3)
            sp.dma_start(wg[:, :, 0:NE1], wg1.rearrange("(k p) n -> p k n", p=P)).then_inc(in_gate1, 16)
            sp.wait_ge(pe_to_dve, DVE0["gat1"] + GH * 7)
            sp.wait_ge(pe_to_dve, DVE0["xt3"])
            sp.dma_start(e1b2_s[:, :], e1b2).then_inc(in_eb2, 16)
            for n in range(2, NE1):
                sp.wait_ge(pe_to_dve, DVE0["experts1"] + 8 * (n - 1))
                expert1(n, 2 + n % 2)
            for t in range(NT):
                sp.wait_ge(dve_freed, DVE0["end"] - 8 + 2 * (t + 1))
                sp.dma_start(out[t * P:(t + 1) * P, :], xres[:, t, :]).then_inc(out_done, 16)
            sp.wait_ge(out_done, 16 * NT)

        @block.tensor
        def _(pe):
            mm = nc.tensor.matmul

            def act_bank(j, before):
                wait(pe, act_freed, before + max(0, j - RING + 1))
                return act_ps[j % RING]

            def dve_bank(j, before):
                wait(pe, dve_freed, before + max(0, j - RING + 1))
                return dve_ps[j % RING]

            def turn_features(source, a0, v0, normed_by=None):
                for c in range(DC):
                    bank = act_bank(c // 2, a0) if c % 2 == 0 else dve_bank(c // 2, v0)
                    for t in range(NT):
                        last = nc.tensor.transpose(bank[:, t * P:(t + 1) * P], source[:, t, c * P:(c + 1) * P], ident[:, :])
                    last.then_inc(pe_to_act if c % 2 == 0 else pe_to_dve, 1)

            def turn_tokens(source, a0, v0):
                for t in range(NT):
                    for half in range(2):
                        bank = act_bank(t, a0) if half == 0 else dve_bank(t, v0)
                        for j in range(3):
                            last = nc.tensor.transpose(bank[:, j * P:(j + 1) * P],
                                                       source[:, half * 3 + j, t * P:(t + 1) * P], ident[:, :])
                        last.then_inc(pe_to_act if half == 0 else pe_to_dve, 1)

            def kslot(s, n):
                return slot[s][:, 0:4608 // n * n].rearrange("p (k n) -> p k n", n=n)

            pe.wait_ge(in_par, 32)
            pe.wait_ge(normed, NT)
            turn_features(xn, ACT0["xt0"], DVE0["xt0"])
            pe.wait_ge(slot_in[0], 16)
            pe.wait_ge(act_freed, ACT0["wn"])
            pe.wait_ge(dve_freed, DVE0["wn"])
            wn_s = kslot(0, D)
            for c in range(DC):
                bank = act_bank(c // 2, ACT0["wn"]) if c % 2 == 0 else dve_bank(c // 2, DVE0["wn"])
                for k in range(DC):
                    last = mm(bank[:, :], wn_s[:, k, c * P:(c + 1) * P], xn_t[:, k, :], start=(k == 0), stop=(k == DC - 1))
                last.then_inc(pe_to_act if c % 2 == 0 else pe_to_dve, 1)
            pe.wait_ge(act_freed, ACT0["tok0"])
            pe.wait_ge(dve_freed, DVE0["tok0"])
            turn_tokens(nodes_t, ACT0["tok0"], DVE0["tok0"])

            pe.wait_ge(act_freed, ACT0["edges"])
            pe.wait_ge(dve_freed, DVE0["edges"])
            pe.wait_ge(const_set, 2)
            sums = act_ps + dve_ps[0:2]
            for bank in sums:
                mm(bank[:, :], zero[:, 0:P], zero[:, :], start=True, stop=False)
            with pe.Fori(0, GROUPS // 2) as i:
                for b in range(2):
                    pe.wait_ge(ea_split, 2 * i + b + 1)
                    pe.wait_ge(ea_high, 2 * i + b + 1)
                    for c in range(GROUP):
                        pe.wait_ge(hots, (2 * i + b) * GROUP + c + 1)
                        hd, hs = hot_d[:, c % 2, :], hot_s[:, c % 2, :]
                        for m in range(NT):
                            mm(act_ps[m][:, :], hs[:, m * P:(m + 1) * P], hd, start=False, stop=False)
                        for m in range(DE // P):
                            for part in (ea_hi, ea_lo):
                                last = mm(dve_ps[m][:, :], part[:, b, c, m * P:(m + 1) * P], hd, start=False, stop=False)
                        last.then_inc(chunk_done, 1)
            for n, bank in enumerate(sums):
                mm(bank[:, :], zero[:, 0:P], zero[:, :], start=False, stop=True).then_inc(
                    pe_to_act if n < NT else pe_to_dve, 1)

            pe.wait_ge(act_freed, ACT0["deg"])
            bank = dve_bank(0, DVE0["deg"])
            for m in range(NT):
                last = mm(bank[:, :], ones[:, :], ct[:, m, :], start=(m == 0), stop=(m == NT - 1))
            last.then_inc(pe_to_dve, 1)
            pe.wait_ge(slot_in[1], 16)
            pe.wait_ge(dve_freed, DVE0["base"])
            for c in range(DC):
                bank = dve_bank(c, DVE0["base"])
                for k in range(DE // P):
                    last = mm(bank[:, :], kslot(1, D)[:, k, c * P:(c + 1) * P], sea_t[:, k, :],
                              start=(k == 0), stop=(k == DE // P - 1))
                last.then_inc(pe_to_dve, 1)

            pe.wait_ge(cpt_set, 1)
            with pe.Fori(0, L) as l:
                a0, v0 = ACT0["rounds"] + 10 * l, DVE0["rounds"] + 24 * l
                pe.wait_ge(act_freed, a0)
                for c in range(DC):
                    bank = dve_bank(c, v0)
                    for k in range(NT):
                        last = mm(bank[:, :], nodes[:, k, c * P:(c + 1) * P], cpt[:, k, :], start=(k == 0), stop=(k == NT - 1))
                    last.then_inc(pe_to_dve, 1)
                pe.wait_ge(slot_in[2], 16 * (l + 1))
                pe.wait_ge(slot_in[3], 16 * (l + 1))
                pe.wait_ge(dve_freed, v0 + DC)
                for u in range(8):
                    t, half = u // 2, u % 2
                    bank = dve_bank(u, v0 + 6)
                    for k in range(2 * DC):
                        act_t = nodes_t[:, k, :] if k < DC else agg_t[:, k - DC, :]
                        w = kslot(2 if k < DC else 3, D)[:, k % DC, half * HALF:(half + 1) * HALF]
                        last = mm(bank[:, 0:HALF], act_t[:, t * P:(t + 1) * P], w, start=(k == 0), stop=(k == 2 * DC - 1))
                    last.then_inc(pe_to_dve, 1)
                pe.wait_ge(normed, NT * (l + 2))
                for c in range(DC):
                    bank = act_bank(c, a0)
                    for t in range(NT):
                        last = nc.tensor.transpose(bank[:, t * P:(t + 1) * P], h[:, t, c * P:(c + 1) * P], ident[:, :])
                    last.then_inc(pe_to_act, 1)
                pe.wait_ge(slot_in[0], 16 * (l + 2))
                pe.wait_ge(act_freed, a0 + DC)
                for c in range(DC):
                    bank = dve_bank(c, v0 + 14)
                    for k in range(DC):
                        last = mm(bank[:, :], kslot(0, D)[:, k, c * P:(c + 1) * P], h_t[:, k, :], start=(k == 0), stop=(k == DC - 1))
                    last.then_inc(pe_to_dve, 1)
                pe.wait_ge(dve_freed, v0 + 20)
                turn_tokens(nodes_t, a0 + 6, v0 + 20)

            pe.wait_ge(slot_in[3], 16 * (L + 1))
            for u in range(8):
                t, half = u // 2, u % 2
                bank = dve_bank(u, DVE0["v"])
                for k in range(DC):
                    last = mm(bank[:, 0:HALF], nodes_t[:, k, t * P:(t + 1) * P],
                              kslot(3, D)[:, k, half * HALF:(half + 1) * HALF], start=(k == 0), stop=(k == DC - 1))
                last.then_inc(pe_to_dve, 1)

            a0, v0 = ACT0["heads"], DVE0["heads"]

            def project(hd):
                for bank, s, signal in ((dve_bank(q_unit(hd), v0), 1, pe_to_dve), (act_bank(k_unit(hd), a0), 2, pe_to_act)):
                    for k in range(DC):
                        last = mm(bank[0:DH, :], kslot(s, D)[:, k, hd * DH:(hd + 1) * DH], nodes_t[:, k, :],
                                  start=(k == 0), stop=(k == DC - 1))
                    last.then_inc(signal, 1)

            def scores(hd):
                pe.wait_ge(dve_freed, v0 + q_unit(hd) + 1)
                pe.wait_ge(act_freed, a0 + k_unit(hd) + 1)
                for t in range(NT):
                    bank = act_bank(score_unit(hd) + t, a0)
                    mm(bank[:, :], q_t[:, hd % 2, t * P:(t + 1) * P], k_t[:, hd % 2, :], start=True, stop=True
                       ).then_inc(pe_to_act, 1)

            def turn_probs(hd):
                pe.wait_ge(prob_set, NT * (hd + 1))
                for m in range(NT):
                    bank = act_bank(turn_unit_a(hd) + m // 2, a0) if m % 2 == 0 else dve_bank(turn_unit_v(hd) + m // 2, v0)
                    for t in range(NT):
                        last = nc.tensor.transpose(bank[:, t * P:(t + 1) * P], prb[:, hd % 2, t, m * P:(m + 1) * P], ident[:, :])
                    last.then_inc(pe_to_act if m % 2 == 0 else pe_to_dve, 1)

            def weigh(hd):
                pe.wait_ge(act_freed, a0 + turn_unit_a(hd) + 2)
                pe.wait_ge(dve_freed, v0 + turn_unit_v(hd) + 2)
                bank = dve_bank(pv_unit(hd), v0)
                for m in range(NT):
                    last = mm(bank[0:DH, :], v[:, m, hd * DH:(hd + 1) * DH], prb_t[:, m, :], start=(m == 0), stop=(m == NT - 1))
                last.then_inc(pe_to_dve, 1)

            pe.wait_ge(slot_in[1], 32)
            pe.wait_ge(slot_in[2], 16 * (L + 1))
            project(0)
            scores(0)
            for hd in range(NH):
                if hd + 1 < NH:
                    project(hd + 1)
                turn_probs(hd)
                if hd + 1 < NH:
                    scores(hd + 1)
                weigh(hd)
            pe.wait_ge(slot_in[0], 16 * (L + 2))
            pe.wait_ge(slot_in[1], 48)
            pe.wait_ge(dve_freed, DVE0["wo"])
            for u in range(8):
                t, half = u // 2, u % 2
                bank = dve_bank(u, DVE0["wo"])
                for hd in range(NH):
                    w = slot[hd // 4][0:DH, 0:4 * D].rearrange("p (k n) -> p k n", k=4)[:, hd % 4, half * HALF:(half + 1) * HALF]
                    last = mm(bank[:, 0:HALF], attn_t[:, hd, t * P:(t + 1) * P], w, start=(hd == 0), stop=(hd == NH - 1))
                last.then_inc(pe_to_dve, 1)

            def gates(xt, ne, stage, bias_stage, b2, k_in):
                pe.wait_ge(*k_in)
                bank = dve_bank(0, DVE0[stage])
                for t in range(NT):
                    for k in range(DC):
                        last = mm(bank[:, t * ne:(t + 1) * ne], xt[:, k, t * P:(t + 1) * P], wg[:, k, 0:ne],
                                  start=(k == 0), stop=(k == DC - 1))
                last.then_inc(pe_to_dve, 1)
                pe.wait_ge(gate_set, 1 if ne == NE0 else 2)
                bank = dve_bank(1, DVE0[stage])
                for t in range(NT):
                    last = nc.tensor.transpose(bank[0:ne, t * P:(t + 1) * P], gate[:, t, 0:ne], ident[:, :])
                last.then_inc(pe_to_dve, 1)
                pe.wait_ge(in_eb2, 16 if ne == NE0 else 32)
                pe.wait_ge(dve_freed, DVE0[bias_stage])
                for u in range(8):
                    t, half = u // 2, u % 2
                    bank = dve_bank(u, DVE0[bias_stage])
                    mm(bank[:, 0:HALF], gate_t[0:ne, t * P:(t + 1) * P], b2[:, half * HALF:(half + 1) * HALF],
                       start=True, stop=True).then_inc(pe_to_dve, 1)

            pe.wait_ge(normed, NT * (L + 2))
            turn_features(xn1, ACT0["xt1"], DVE0["xt1"])
            pe.wait_ge(act_freed, ACT0["gate0"])
            pe.wait_ge(dve_freed, DVE0["gate0"])
            gates(xn1_t, NE0, "gate0", "bias0", e0b2_s, (in_gate, 48))
            with pe.Fori(0, NE0) as e:
                a0, v0 = ACT0["experts0"] + 12 * e, DVE0["experts0"] + 8 * e
                pe.wait_ge(slot_in[2], 16 * (L + 2) + 16 * e)
                pe.wait_ge(slot_in[3], 16 * (L + 2) + 16 * e)
                for c in range(H0 // P):
                    bank = act_bank(c, a0)
                    for k in range(DC):
                        w = kslot(2 + c // DC, D)[:, k, (c % DC) * P:(c % DC + 1) * P]
                        last = mm(bank[:, :], w, xn1_t[:, k, :], start=(k == 0), stop=(k == DC - 1))
                    last.then_inc(pe_to_act, 1)
                pe.wait_ge(slot_in[0], 16 * (L + 3) + 16 * e)
                pe.wait_ge(slot_in[1], 64 + 16 * e)
                pe.wait_ge(act_freed, a0 + 12)
                for u in range(8):
                    t, half = u // 2, u % 2
                    bank = dve_bank(u, v0)
                    for k in range(H0 // P):
                        w = kslot(k // DC, D)[:, k % DC, half * HALF:(half + 1) * HALF]
                        last = mm(bank[:, 0:HALF], eh_t[:, k, t * P:(t + 1) * P], w, start=(k == 0), stop=(k == H0 // P - 1))
                    last.then_inc(pe_to_dve, 1)

            pe.wait_ge(normed, NT * (L + 3))
            turn_features(xn2, ACT0["xt2"], DVE0["xt2"])
            pe.wait_ge(act_freed, ACT0["h1"])
            pe.wait_ge(dve_freed, DVE0["h1"])
            for s in (2, 3):
                pe.wait_ge(slot_in[s], 16 * (L + 1) + 16 * NE0 + 16)
            for u in range(8):
                t, half = u // 2, u % 2
                bank = act_bank(t, ACT0["h1"]) if half == 0 else dve_bank(t, DVE0["h1"])
                for k in range(DC):
                    last = mm(bank[:, :], xn2_t[:, k, t * P:(t + 1) * P], kslot(2 + half, N)[:, k, :], start=(k == 0), stop=(k == DC - 1))
                last.then_inc(pe_to_act if half == 0 else pe_to_dve, 1)
            for t in range(NT):
                bank = dve_bank(t, DVE0["mask"])
                for m in range(NT):
                    last = nc.tensor.transpose(bank[:, m * P:(m + 1) * P], ct[:, m, t * P:(t + 1) * P], ident[:, :])
                last.then_inc(pe_to_dve, 1)

            def spread(a_src, unit, v0):
                bank = dve_bank(unit, v0)
                for t in range(NT):
                    last = mm(bank[:, t * P:(t + 1) * P], a_src(t).to_broadcast([P, P]), ident[:, :], start=True, stop=True)
                last.then_inc(pe_to_dve, 1)

            def turn_graph(unit, v0, g):
                pe.wait_ge(g_exp, g + 1)
                for m in range(NT):
                    bank = dve_bank(unit + m, v0)
                    for t in range(NT):
                        last = nc.tensor.transpose(bank[:, t * P:(t + 1) * P], gp[:, t, m * P:(m + 1) * P], ident[:, :])
                    last.then_inc(pe_to_dve, 1)
                pe.wait_ge(dve_freed, v0 + unit + 4)

            pe.wait_ge(att_set, 1)
            v0 = DVE0["gat1"]
            spread(lambda t: att[:, 0, t, 0:1], 0, v0)
            unit = 1
            for hd in range(GH):
                if hd + 1 < GH:
                    spread(lambda t: att[:, 0, t, hd + 1:hd + 2], unit, v0)
                    unit += 1
                turn_graph(unit, v0, hd)
                unit += NT
                for pair in range(2):
                    bank = dve_bank(unit, v0)
                    for t in (2 * pair, 2 * pair + 1):
                        w = GC + 2
                        for m in range(NT):
                            last = mm(bank[:, (t % 2) * w:(t % 2 + 1) * w], gp_t[:, m, t * P:(t + 1) * P], h1x[:, m, hd, :],
                                      start=(m == 0), stop=(m == NT - 1))
                    last.then_inc(pe_to_dve, 1)
                    unit += 1
            pe.wait_ge(dve_freed, DVE0["o1t"])
            for c in range(GD // P):
                bank = act_bank(c // 2, ACT0["o1t"]) if c % 2 == 0 else dve_bank(c // 2, DVE0["o1t"])
                for t in range(NT):
                    last = nc.tensor.transpose(bank[:, t * P:(t + 1) * P], out1[:, t, c * P:(c + 1) * P], ident[:, :])
                last.then_inc(pe_to_act if c % 2 == 0 else pe_to_dve, 1)
            pe.wait_ge(act_freed, ACT0["h2"])
            pe.wait_ge(dve_freed, DVE0["h2"])
            pe.wait_ge(slot_in[0], 16 * (L + 2) + 16 * NE0 + 16)
            pe.wait_ge(slot_in[1], 48 + 16 * NE0 + 16)
            for u in range(8):
                t, half = u // 2, u % 2
                bank = act_bank(t, ACT0["h2"]) if half == 0 else dve_bank(t, DVE0["h2"])
                for k in range(GD // P):
                    last = mm(bank[:, 0:HALF], out1_t[:, k, t * P:(t + 1) * P],
                              kslot(k // 4, D)[:, k % 4, half * HALF:(half + 1) * HALF], start=(k == 0), stop=(k == GD // P - 1))
                last.then_inc(pe_to_act if half == 0 else pe_to_dve, 1)
            pe.wait_ge(att_set, 2)
            v0 = DVE0["gat2"]
            spread(lambda t: att[:, 0, t, 0:1], 0, v0)
            turn_graph(1, v0, GH)
            for u in range(8):
                t, half = u // 2, 1 - u % 2
                bank = dve_bank(5 + u, v0)
                lo, hi = (0, HALF) if half == 0 else (HALF, D + 2)
                for m in range(NT):
                    last = mm(bank[:, 0:hi - lo], gp_t[:, m, t * P:(t + 1) * P], h2x[:, m, lo:hi], start=(m == 0), stop=(m == NT - 1))
                last.then_inc(pe_to_dve, 1)

            pe.wait_ge(normed, NT * (L + 4))
            turn_features(xn3, ACT0["xt3"], DVE0["xt3"])
            pe.wait_ge(act_freed, ACT0["gate1"])
            pe.wait_ge(dve_freed, DVE0["gate1"])
            gates(xn3_t, NE1, "gate1", "bias1", e1b2_s, (in_gate1, 16))
            for n in range(NE1):
                a0, v0, s = ACT0["experts1"] + 3 * n, DVE0["experts1"] + 8 * n, 2 + n % 2
                pe.wait_ge(slot_in[s], 16 * (L + 1) + 16 * NE0 + 16 + 32 * (n // 2 + 1))
                up = slot[s][:, 0:DC * H1].rearrange("p (k n) -> p k n", k=DC)
                down = slot[s][:, DC * H1:DC * H1 + 3 * D].rearrange("p (k n) -> p k n", k=3)
                wait(pe, pe_to_dve, v0 - 8 if n >= 2 else 0)
                for c in range(3):
                    bank = act_bank(c, a0)
                    for k in range(DC):
                        last = mm(bank[:, :], up[:, k, c * P:(c + 1) * P], xn3_t[:, k, :], start=(k == 0), stop=(k == DC - 1))
                    last.then_inc(pe_to_act, 1)
                pe.wait_ge(act_freed, a0 + 3)
                for u in range(8):
                    t, half = u // 2, u % 2
                    bank = dve_bank(u, v0)
                    for k in range(3):
                        last = mm(bank[:, 0:HALF], eh1_t[:, n % 2, k, t * P:(t + 1) * P], down[:, k, half * HALF:(half + 1) * HALF],
                                  start=(k == 0), stop=(k == 2))
                    last.then_inc(pe_to_dve, 1)

        @block.scalar
        def _(act):
            go = nc.scalar.activation

            def bank_of(j, before):
                act.wait_ge(pe_to_act, before + j + 1)
                return act_ps[j % RING]

            for c in range(0, DC, 2):
                bank = bank_of(c // 2, ACT0["xt0"])
                go(xn_t[:, c, :], bank[:, :], ACT.Copy).then_inc(act_freed, 1)
            act.wait_ge(in_par, 32)
            for c in range(0, DC, 2):
                bank = bank_of(c // 2, ACT0["wn"])
                go(nodes_t[:, c, :], bank[:, :], ACT.Identity, bias=col("bn", c)).then_inc(act_freed, 1)
            for t in range(NT):
                bank = bank_of(t, ACT0["tok0"])
                go(nodes[:, t, 0:HALF], bank[:, 0:HALF], ACT.Copy).then_inc(act_freed, 1)
            with act.Fori(0, GROUPS // 2) as i:
                for b in range(2):
                    act.wait_ge(in_edge[b], 16 * (i + 1))
                    act.wait_ge(chunk_done, 2 * GROUP * i - 0 if b == 0 else 2 * GROUP * i)
                    go(ea_hi[:, b, :, :], ea_raw[:, b, :, :], ACT.Copy).then_inc(ea_high, 1)
            for m in range(NT):
                bank = bank_of(m, ACT0["edges"])
                go(ct[:, m, :], bank[:, :], ACT.Copy).then_inc(act_freed, 1)
            with act.Fori(0, L) as l:
                a0 = ACT0["rounds"] + 10 * l
                for c in range(DC):
                    bank = bank_of(c, a0)
                    go(h_t[:, c, :], bank[:, :], ACT.Relu, bias=par[:, bass.ds(COLS["ln_b"] + DC * l + c, 1)],
                       scale=par[:, bass.ds(COLS["ln_g"] + DC * l + c, 1)]).then_inc(act_freed, 1)
                for t in range(NT):
                    bank = bank_of(t, a0 + 6)
                    go(nodes[:, t, 0:HALF], bank[:, 0:HALF], ACT.Copy).then_inc(act_freed, 1)
            a0 = ACT0["heads"]

            def key(hd):
                bank = bank_of(k_unit(hd), a0)
                go(k_t[:, hd % 2, :], bank[0:DH, :], ACT.Identity, bias=par[0:DH, COLS["bk"] + hd:COLS["bk"] + hd + 1]).then_inc(act_freed, 1)

            key(0)
            for hd in range(NH):
                wait(act, pe_to_dve, DVE0["heads"] + turn_unit_v(hd - 2) + 2 if hd >= 2 else 0)
                for t in range(NT):
                    act.wait_ge(row_max, NT * hd + t + 1)
                    go(prb[:, hd % 2, t, :], act_ps[(score_unit(hd) + t) % RING][:, :], ACT.Exp, bias=nbias[:, hd % 2, t:t + 1],
                       accum_out=rsum[:, hd % 2, t:t + 1]).then_inc(act_freed, 1)
                if hd + 1 < NH:
                    key(hd + 1)
                for j in range(2):
                    bank = bank_of(turn_unit_a(hd) + j, a0)
                    wait(act, pe_to_dve, DVE0["heads"] + pv_unit(hd - 1) + 1 if hd else 0)
                    go(prb_t[:, 2 * j, :], bank[:, :], ACT.Copy).then_inc(act_freed, 1)
            for c in range(0, DC, 2):
                bank = bank_of(c // 2, ACT0["xt1"])
                go(xn1_t[:, c, :], bank[:, :], ACT.Copy).then_inc(act_freed, 1)
            act.wait_ge(logit_set, 1)
            go(prob[:, :, :], logit[:, :, :], ACT.Exp).then_inc(prob_exp, 1)
            with act.Fori(0, NE0) as e:
                a0 = ACT0["experts0"] + 12 * e
                for c in range(H0 // P):
                    bank = bank_of(c, a0)
                    if c == 0:
                        act.wait_ge(pe_to_dve, DVE0["experts0"] + 8 * e)
                    go(eh_t[:, c, :], bank[:, :], ACT.Gelu, bias=par[:, bass.ds(COLS["e0b1"] + H0 // P * e + c, 1)]).then_inc(act_freed, 1)
            for c in range(0, DC, 2):
                bank = bank_of(c // 2, ACT0["xt2"])
                go(xn2_t[:, c, :], bank[:, :], ACT.Copy).then_inc(act_freed, 1)
            for t in range(NT):
                bank = bank_of(t, ACT0["h1"])
                go(h1x[:, t, 0:4, 0:GC], bank[:, :].rearrange("p (h c) -> p h c", h=4), ACT.Copy).then_inc(act_freed, 1)

            def graph(g):
                b = g % 2
                act.wait_ge(g_max, g + 1)
                wait(act, g_arg, g)
                for t in range(NT):
                    last = go(arg2[:, t, :], arg[:, b, t, :], ACT.Identity, bias=gdec[:, b, 3, t:t + 1], scale=0.2)
                last.then_inc(g_low, 1)

            def graph_exp(g):
                act.wait_ge(g_arg, g + 1)
                if g:
                    act.wait_ge(pe_to_dve, gp_free(g))
                go(gp[:, :, :], arg[:, g % 2, :, :], ACT.Exp).then_inc(g_exp, 1)

            def gp_free(g):
                return DVE0["gat1"] + 1 + 7 * (g - 1) + (1 if g < GH else 0) + NT

            graph(0)
            for g in range(GH):
                graph_exp(g)
                if g + 1 < GH:
                    graph(g + 1)
            for c in range(0, GD // P, 2):
                bank = bank_of(c // 2, ACT0["o1t"])
                go(out1_t[:, c, :], bank[:, :], ACT.Relu).then_inc(act_freed, 1)
            for t in range(NT):
                bank = bank_of(t, ACT0["h2"])
                go(h2x[:, t, 0:HALF], bank[:, 0:HALF], ACT.Copy).then_inc(act_freed, 1)
            graph(GH)
            graph_exp(GH)
            for c in range(0, DC, 2):
                bank = bank_of(c // 2, ACT0["xt3"])
                go(xn3_t[:, c, :], bank[:, :], ACT.Copy).then_inc(act_freed, 1)
            for n in range(NE1):
                for c in range(3):
                    bank = bank_of(c, ACT0["experts1"] + 3 * n)
                    wait(act, pe_to_dve, DVE0["experts1"] + 8 * (n - 1) if n >= 2 else 0)
                    go(eh1_t[:, n % 2, c, :], bank[:, :], ACT.Gelu, bias=col("e1b1", 3 * n + c)).then_inc(act_freed, 1)

        @block.vector
        def _(dve):
            vv = nc.vector
            step = [0]

            def then(ins):
                step[0] = step[0] + 1
                ins.then_inc(dve_step, 1)

            def settle():
                dve.wait_ge(dve_step, step[0])

            def bank_of(j, before):
                dve.wait_ge(pe_to_dve, before + j + 1)
                return dve_ps[j % RING]

            def stats(source):
                for t in range(NT):
                    for half in range(2):
                        then(vv.bn_stats(bns[:, t, half, :], source[:, t, half * HALF:(half + 1) * HALF]))
                settle()
                vv.memset(root[:, 0, :], 0.0)
                for t in range(NT):
                    then(vv.bn_aggr(mv[:, t, :], bns[:, t, :, :]))
                settle()
                v_eps, y, y2 = root[:, 0, :], rstd[:, :], root[:, 1, :]
                then(vv.tensor_scalar(v_eps, mv[:, :, 1], EPS, None, ALU.add))
                settle()
                then(vv.tensor_scalar(y2.bitcast(I32), v_eps.bitcast(I32), 1, None, ALU.logical_shift_right))
                settle()
                then(vv.tensor_scalar(y.bitcast(I32), y2.bitcast(I32), -1.0, float(0x5F3759DF), ALU.mult, ALU.add))
                settle()
                for _ in range(NEWTON):
                    then(vv.tensor_tensor(y2, y, y, ALU.mult))
                    settle()
                    then(vv.scalar_tensor_tensor(y2, y2, -0.5, v_eps, ALU.mult, ALU.mult))
                    settle()
                    then(vv.scalar_tensor_tensor(y, y2, 1.5, y, ALU.add, ALU.mult))
                    settle()

            def layer_norm(source, to):
                stats(source)
                for t in range(NT):
                    vv.tensor_scalar(to[:, t, :], source[:, t, :], mv[:, t, 0:1], rstd[:, t:t + 1],
                                     ALU.subtract, ALU.mult).then_inc(normed, 1)

            vv.memset(ones[:, :], 1.0).then_inc(const_set, 1)
            dve.wait_ge(in_x, 16)
            layer_norm(xres, xn)
            for c in range(1, DC, 2):
                bank = bank_of(c // 2, DVE0["xt0"])
                vv.tensor_copy(xn_t[:, c, :], bank[:, :]).then_inc(dve_freed, 1)
            dve.wait_ge(in_par, 32)
            for c in range(1, DC, 2):
                bank = bank_of(c // 2, DVE0["wn"])
                vv.tensor_scalar(nodes_t[:, c, :], bank[:, :], col("bn", c), None, ALU.add).then_inc(dve_freed, 1)
            for t in range(NT):
                bank = bank_of(t, DVE0["tok0"])
                vv.tensor_copy(nodes[:, t, HALF:D], bank[:, 0:HALF]).then_inc(dve_freed, 1)

            dve.wait_ge(in_ends, 48)
            then(vv.tensor_copy(ends[:, :, :], ends_i[:, :, :]))
            settle()
            vv.tensor_scalar(zero[:, :], iota[:, :], 0.0, None, ALU.mult).then_inc(const_set, 1)
            with dve.Fori(0, GROUPS // 2) as i:
                for b in range(2):
                    for c in range(GROUP):
                        if c == 0:
                            dve.wait_ge(ea_high, 2 * i + b + 1)
                            vv.tensor_tensor(ea_lo[:, b, :, :], ea_raw[:, b, :, :], ea_hi[:, b, :, :].bitcast(F32),
                                             ALU.subtract).then_inc(ea_split, 1)
                        k = (2 * i + b) * GROUP + c
                        if b == 0 and c < 2:
                            dve.wait_ge(chunk_done, 2 * GROUP * i)
                        else:
                            dve.wait_ge(chunk_done, k - 1)
                        vv.tensor_scalar(hot_d[:, c % 2, :], iota[:, :], ends[:, 1, bass.ds(k, 1)], None, ALU.is_equal)
                        vv.tensor_scalar(hot_s[:, c % 2, :], iota[:, :], ends[:, 0, bass.ds(k, 1)], None, ALU.is_equal
                                         ).then_inc(hots, 1)
            for m in range(2):
                bank = bank_of(m, DVE0["edges"])
                vv.tensor_copy(sea_t[:, m, :], bank[:, :]).then_inc(dve_freed, 1)
            bank = bank_of(0, DVE0["deg"])
            vv.tensor_copy(deg[:, :], bank[:, :]).then_inc(dve_freed, 1)
            dve.wait_ge(dve_freed, DVE0["base"])
            then(vv.tensor_copy(cpt[:, :, :], ct[:, :, :]))
            settle()
            for t in range(NT):
                own = cpt[:, t, t * P:(t + 1) * P]
                then(vv.tensor_tensor(iota[:, t * P:(t + 1) * P], ident[:, :], deg[:, t * P:(t + 1) * P], ALU.mult))
            settle()
            for t in range(NT):
                own = cpt[:, t, t * P:(t + 1) * P]
                last = vv.tensor_tensor(own, own, iota[:, t * P:(t + 1) * P], ALU.add)
                if t < NT - 1:
                    then(last)
                else:
                    last.then_inc(cpt_set, 1)
            settle()
            for c in range(DC):
                bank = bank_of(c, DVE0["base"])
                vv.scalar_tensor_tensor(base_t[:, c, :], deg[:, :], col("be", c), bank[:, :], ALU.mult, ALU.add).then_inc(dve_freed, 1)
            dve.wait_ge(dve_freed, DVE0["rounds"])

            before = step[0]
            with dve.Fori(0, L) as l:
                v0 = DVE0["rounds"] + 24 * l
                step[0] = before + STATS_STEPS * l
                for c in range(DC):
                    bank = bank_of(c, v0)
                    vv.tensor_tensor(agg_t[:, c, :], bank[:, :], base_t[:, c, :], ALU.add).then_inc(dve_freed, 1)
                dve.wait_ge(in_row[0], 16 * (l + 1))
                for u in range(8):
                    t, half = u // 2, u % 2
                    bank = bank_of(u, v0 + 6)
                    vv.tensor_tensor(h[:, t, half * HALF:(half + 1) * HALF], bank[:, 0:HALF],
                                     brow[:, 0, half * HALF:(half + 1) * HALF], ALU.add).then_inc(dve_freed, 1)
                dve.wait_ge(dve_freed, v0 + 14)
                stats(h)
                for t in range(NT):
                    vv.tensor_scalar(h[:, t, :], h[:, t, :], mv[:, t, 0:1], rstd[:, t:t + 1],
                                     ALU.subtract, ALU.mult).then_inc(normed, 1)
                for c in range(DC):
                    bank = bank_of(c, v0 + 14)
                    vv.scalar_tensor_tensor(nodes_t[:, c, :], bank[:, :], par[:, bass.ds(COLS["b2"] + DC * l + c, 1)],
                                            nodes_t[:, c, :], ALU.add, ALU.add).then_inc(dve_freed, 1)
                for t in range(NT):
                    bank = bank_of(t, v0 + 20)
                    vv.tensor_copy(nodes[:, t, HALF:D], bank[:, 0:HALF]).then_inc(dve_freed, 1)
            step[0] = before + STATS_STEPS * L

            dve.wait_ge(in_row[1], 16)
            for u in range(8):
                t, half = u // 2, u % 2
                bank = bank_of(u, DVE0["v"])
                vv.tensor_tensor(v[:, t, half * HALF:(half + 1) * HALF], bank[:, 0:HALF],
                                 brow[:, 1, half * HALF:(half + 1) * HALF], ALU.add).then_inc(dve_freed, 1)
            dve.wait_ge(act_freed, ACT0["heads"])
            dve.wait_ge(in_row[0], 16 * (L + 1))
            dve.wait_ge(dve_freed, DVE0["v"])
            then(vv.tensor_tensor(xres[:, :, :], xres[:, :, :], nodes[:, :, :], ALU.add))
            settle()
            for t in range(NT):
                then(vv.tensor_tensor(xres[:, t, :], xres[:, t, :], brow[:, 0, :], ALU.add))

            a0, v0 = ACT0["heads"], DVE0["heads"]

            def query(hd):
                bank = bank_of(q_unit(hd), v0)
                vv.tensor_scalar(q_t[:, hd % 2, :], bank[0:DH, :], par[0:DH, COLS["bq"] + hd:COLS["bq"] + hd + 1],
                                 float(DH) ** -0.5, ALU.add, ALU.mult).then_inc(dve_freed, 1)

            def maxima(hd):
                for t in range(NT):
                    dve.wait_ge(pe_to_act, a0 + score_unit(hd) + t + 1)
                    vv.tensor_reduce(nbias[:, hd % 2, t:t + 1], act_ps[(score_unit(hd) + t) % RING][:, :], AX_X, ALU.max,
                                     negate=True).then_inc(row_max, 1)

            def normalise(hd):
                dve.wait_ge(act_freed, a0 + score_unit(hd) + NT)
                then(vv.reciprocal(rinv[:, hd % 2, :], rsum[:, hd % 2, :]))
                settle()
                for t in range(NT):
                    vv.tensor_scalar(prb[:, hd % 2, t, :], prb[:, hd % 2, t, :], rinv[:, hd % 2, t:t + 1], None,
                                     ALU.mult).then_inc(prob_set, 1)

            query(0)
            maxima(0)
            for hd in range(NH):
                normalise(hd)
                if hd + 1 < NH:
                    query(hd + 1)
                for j in range(2):
                    bank = bank_of(turn_unit_v(hd) + j, v0)
                    wait(dve, pe_to_dve, v0 + pv_unit(hd - 1) + 1 if hd else 0)
                    vv.tensor_copy(prb_t[:, 2 * j + 1, :], bank[:, :]).then_inc(dve_freed, 1)
                if hd + 1 < NH:
                    maxima(hd + 1)
                bank = bank_of(pv_unit(hd), v0)
                vv.tensor_copy(attn_t[:, hd, :], bank[0:DH, :]).then_inc(dve_freed, 1)

            def add_to_x(stage):
                settle()
                for u in range(8):
                    t, half = u // 2, u % 2
                    bank = bank_of(u, DVE0[stage])
                    part = xres[:, t, half * HALF:(half + 1) * HALF]
                    vv.tensor_tensor(part, bank[:, 0:HALF], part, ALU.add).then_inc(dve_freed, 1)
                dve.wait_ge(dve_freed, DVE0[stage] + 8)

            add_to_x("wo")
            layer_norm(xres, xn1)

            def pick_top(values, ne, to, tmp):
                shape = [P, NT, ne]
                then(vv.tensor_reduce(top4[:, :], values, AX_X, ALU.max))
                settle()
                then(vv.tensor_tensor(tmp, values, top4[:, :].unsqueeze(2).to_broadcast(shape), ALU.is_equal))
                settle()
                then(vv.tensor_tensor(tmp, tmp, prio(ne), ALU.mult))
                settle()
                then(vv.tensor_reduce(top4[:, :], tmp, AX_X, ALU.max))
                settle()
                then(vv.tensor_tensor(to, tmp, top4[:, :].unsqueeze(2).to_broadcast(shape), ALU.is_equal))
                settle()

            def prio(ne):
                return col("prio", 0, NT * 8).rearrange("p (t e) -> p t e", t=NT)[:, :, 0:ne]

            def logits(stage, ne, b0):
                bank = bank_of(0, DVE0[stage])
                vv.tensor_tensor(logit[:, :, 0:ne], bank[:, 0:NT * ne].rearrange("p (t e) -> p t e", t=NT),
                                 bg[:, b0:b0 + ne].unsqueeze(1).to_broadcast([P, NT, ne]), ALU.add).then_inc(dve_freed, 1)
                dve.wait_ge(dve_freed, DVE0[stage] + 1)

            def gates_turned(stage, ne):
                bank = bank_of(1, DVE0[stage])
                vv.tensor_copy(gate_t[0:ne, :], bank[0:ne, :]).then_inc(dve_freed, 1)

            for c in range(1, DC, 2):
                bank = bank_of(c // 2, DVE0["xt1"])
                vv.tensor_copy(xn1_t[:, c, :], bank[:, :]).then_inc(dve_freed, 1)
            dve.wait_ge(in_gate, 48)
            logits("gate0", NE0, 0)
            then(vv.tensor_reduce(top4[:, :], logit[:, :, :], AX_X, ALU.max))
            settle()
            vv.tensor_tensor(logit[:, :, :], logit[:, :, :], top4[:, :].unsqueeze(2).to_broadcast([P, NT, NE0]),
                             ALU.subtract).then_inc(logit_set, 1)
            dve.wait_ge(prob_exp, 1)
            pick_top(prob[:, :, :], NE0, pick[0][:, :, :], pick[3][:, :, :])
            then(vv.scalar_tensor_tensor(pick[1][:, :, :], pick[0][:, :, :], -2.0, prob[:, :, :], ALU.mult, ALU.add))
            settle()
            pick_top(pick[1][:, :, :], NE0, pick[2][:, :, :], pick[3][:, :, :])
            then(vv.tensor_tensor(pick[2][:, :, :], pick[2][:, :, :], pick[0][:, :, :], ALU.add))
            settle()
            then(vv.tensor_tensor(pick[2][:, :, :], pick[2][:, :, :], prob[:, :, :], ALU.mult))
            settle()
            then(vv.tensor_reduce(top4[:, :], pick[2][:, :, :], AX_X, ALU.add))
            settle()
            then(vv.reciprocal(top4[:, :], top4[:, :]))
            settle()
            vv.tensor_tensor(gate[:, :, :], pick[2][:, :, :], top4[:, :].unsqueeze(2).to_broadcast([P, NT, NE0]),
                             ALU.mult).then_inc(gate_set, 1)
            dve.wait_ge(gate_set, 1)
            gates_turned("gate0", NE0)
            add_to_x("bias0")

            def add_expert(v0, scalar):
                for u in range(8):
                    t, half = u // 2, u % 2
                    bank = bank_of(u, v0)
                    part = xres[:, t, half * HALF:(half + 1) * HALF]
                    vv.scalar_tensor_tensor(part, bank[:, 0:HALF], scalar(t), part, ALU.mult, ALU.add).then_inc(dve_freed, 1)

            with dve.Fori(0, NE0) as e:
                v0 = DVE0["experts0"] + 8 * e
                dve.wait_ge(dve_freed, v0)
                add_expert(v0, lambda t: gate[:, t, bass.ds(e, 1)])
            dve.wait_ge(dve_freed, DVE0["xt2"])
            layer_norm(xres, xn2)
            for c in range(1, DC, 2):
                bank = bank_of(c // 2, DVE0["xt2"])
                vv.tensor_copy(xn2_t[:, c, :], bank[:, :]).then_inc(dve_freed, 1)
            then(vv.memset(h1x[:, :, :, GC:GC + 2], 1.0))
            for t in range(NT):
                bank = bank_of(t, DVE0["h1"])
                vv.tensor_copy(h1x[:, t, 4:8, 0:GC], bank[:, :].rearrange("p (h c) -> p h c", h=4)).then_inc(dve_freed, 1)
            for t in range(NT):
                bank = bank_of(t, DVE0["mask"])
                vv.tensor_scalar(mask[:, t, :], bank[:, :], 0.0, NONE, ALU.is_equal, ALU.mult).then_inc(dve_freed, 1)
            dve.wait_ge(act_freed, ACT0["mask"])
            dve.wait_ge(dve_freed, DVE0["mask"])
            dve.wait_ge(in_att1, 16)
            for which in range(2):
                for t in range(NT):
                    settle()
                    then(vv.tensor_tensor(scr[:, :].rearrange("p (h c) -> p h c", h=GH), h1x[:, t, :, 0:GC],
                                          att1[:, which, :].rearrange("p (h c) -> p h c", h=GH), ALU.mult))
                    settle()
                    last = vv.tensor_reduce(att[:, which, t, :], scr[:, :].rearrange("p (h c) -> p h c", h=GH), AX_X, ALU.add)
                    if which == 1 and t == NT - 1:
                        last.then_inc(att_set, 1)
                    else:
                        then(last)
            settle()
            dve.wait_ge(att_set, 1)

            def graph_front(g, unit, v0, a_dst):
                b = g % 2
                bank = bank_of(unit, v0)
                wait(dve, g_exp, g - 1)
                for t in range(NT):
                    last = vv.tensor_tensor_reduce(out=arg[:, b, t, :], in0=bank[:, :], in1=mask[:, t, :], scale=1.0, scalar=NONE,
                                                   op0=ALU.add, op1=ALU.max, accum_out=gmax[:, b, t:t + 1])
                    if t < NT - 1:
                        then(last)
                last.then_inc(dve_freed, 1)
                dve.wait_ge(dve_freed, v0 + unit + 1)
                settle()
                then(vv.scalar_tensor_tensor(gdec[:, b, 0, :], gmax[:, b, :], FLOOR, a_dst, ALU.max, ALU.add))
                settle()
                then(vv.scalar_tensor_tensor(gdec[:, b, 1, :], gdec[:, b, 0, :], 0.2, gdec[:, b, 0, :], ALU.mult, ALU.max))
                settle()
                then(vv.tensor_tensor(gdec[:, b, 2, :], a_dst, gdec[:, b, 1, :], ALU.subtract))
                vv.scalar_tensor_tensor(gdec[:, b, 3, :], a_dst, 0.2, gdec[:, b, 1, :], ALU.mult, ALU.subtract).then_inc(g_max, 1)

            def graph_arg(g):
                b = g % 2
                dve.wait_ge(g_low, g + 1)
                settle()
                for t in range(NT):
                    last = vv.scalar_tensor_tensor(arg[:, b, t, :], arg[:, b, t, :], gdec[:, b, 2, t:t + 1], arg2[:, t, :],
                                                   ALU.add, ALU.max)
                    if t < NT - 1:
                        then(last)
                last.then_inc(g_arg, 1)

            def graph_turned(unit, v0, used):
                for m in range(NT):
                    bank = bank_of(unit + m, v0)
                    wait(dve, pe_to_dve, used)
                    vv.tensor_tensor(gp_t[:, m, :], bank[:, :], ct[:, m, :], ALU.mult).then_inc(dve_freed, 1)

            v0 = DVE0["gat1"]
            dve.wait_ge(in_gb, 32)
            graph_front(0, 0, v0, att[:, 1, :, 0])
            graph_arg(0)
            unit = 1
            for hd in range(GH):
                if hd + 1 < GH:
                    graph_front(hd + 1, unit, v0, att[:, 1, :, hd + 1])
                    unit += 1
                graph_turned(unit, v0, v0 + unit - (1 if hd + 1 < GH else 0) if hd else 0)
                unit += NT
                if hd + 1 < GH:
                    graph_arg(hd + 1)
                for pair in range(2):
                    bank = bank_of(unit, v0)
                    w = GC + 2
                    den = bank[:, 0:2 * w].rearrange("p (t c) -> p t c", t=2)[:, :, GC]
                    then(vv.tensor_scalar(rinv[:, 0, 2 * pair:2 * pair + 2], den, DEN_EPS, None, ALU.add))
                    settle()
                    then(vv.reciprocal(rinv[:, 1, 2 * pair:2 * pair + 2], rinv[:, 0, 2 * pair:2 * pair + 2]))
                    settle()
                    for j in range(2):
                        t = 2 * pair + j
                        last = vv.scalar_tensor_tensor(out1[:, t, hd * GC:(hd + 1) * GC], bank[:, j * w:j * w + GC],
                                                       rinv[:, 1, t:t + 1], g_b1[:, hd * GC:(hd + 1) * GC], ALU.mult, ALU.add)
                        if j == 0:
                            then(last)
                    last.then_inc(dve_freed, 1)
                    unit += 1
            for t in range(NT):
                then(vv.tensor_tensor(xres[:, t, :], xres[:, t, :], g_b2[:, :], ALU.add))
            for c in range(1, GD // P, 2):
                bank = bank_of(c // 2, DVE0["o1t"])
                vv.tensor_scalar(out1_t[:, c, :], bank[:, :], 0.0, None, ALU.max).then_inc(dve_freed, 1)
            dve.wait_ge(pe_to_dve, DVE0["h2"])
            then(vv.memset(h2x[:, :, D:D + 2], 1.0))
            for t in range(NT):
                bank = bank_of(t, DVE0["h2"])
                vv.tensor_copy(h2x[:, t, HALF:D], bank[:, 0:HALF]).then_inc(dve_freed, 1)
            dve.wait_ge(in_row[0], 16 * (L + 2))
            dve.wait_ge(act_freed, ACT0["xt3"])
            dve.wait_ge(dve_freed, DVE0["gat2"])
            for which in range(2):
                for t in range(NT):
                    settle()
                    last = vv.tensor_tensor_reduce(out=gp_t[:, 0:2, :].rearrange("p a n -> p (a n)")[:, 0:D], in0=h2x[:, t, 0:D],
                                                   in1=brow[:, which, :], scale=1.0, scalar=0.0, op0=ALU.mult, op1=ALU.add,
                                                   accum_out=att[:, which, t, 0:1])
                    if which == 1 and t == NT - 1:
                        last.then_inc(att_set, 1)
                    else:
                        then(last)
            settle()
            dve.wait_ge(att_set, 2)
            v0 = DVE0["gat2"]
            graph_front(GH, 0, v0, att[:, 1, :, 0])
            graph_arg(GH)
            graph_turned(1, v0, 0)
            for u in range(8):
                t, half = u // 2, 1 - u % 2
                bank = bank_of(5 + u, v0)
                if half == 1:
                    then(vv.tensor_scalar(rinv[:, 0, t:t + 1], bank[:, HALF:HALF + 1], DEN_EPS, None, ALU.add))
                    settle()
                    then(vv.reciprocal(rinv[:, 1, t:t + 1], rinv[:, 0, t:t + 1]))
                    settle()
                part = xres[:, t, half * HALF:(half + 1) * HALF]
                vv.scalar_tensor_tensor(part, bank[:, 0:HALF], rinv[:, 1, t:t + 1], part, ALU.mult, ALU.add).then_inc(dve_freed, 1)
            dve.wait_ge(dve_freed, DVE0["xt3"])
            layer_norm(xres, xn3)
            for c in range(1, DC, 2):
                bank = bank_of(c // 2, DVE0["xt3"])
                vv.tensor_copy(xn3_t[:, c, :], bank[:, :]).then_inc(dve_freed, 1)
            logits("gate1", NE1, 8)
            pick_top(logit[:, :, 0:NE1], NE1, pick[0][:, :, 0:NE1], pick[3][:, :, 0:NE1])
            vv.tensor_copy(gate[:, :, 0:NE1], pick[0][:, :, 0:NE1]).then_inc(gate_set, 1)
            dve.wait_ge(gate_set, 2)
            gates_turned("gate1", NE1)
            add_to_x("bias1")
            for n in range(NE1):
                v0 = DVE0["experts1"] + 8 * n
                dve.wait_ge(dve_freed, v0)
                add_expert(v0, lambda t: gate[:, t, n:n + 1])


_OUT = ((N, D), "float32")


def kernel(**inputs):
    import numpy as np
    import concourse.bacc as bacc
    from concourse.bass_utils import run_bass_kernel_spmd

    a = {k: np.asarray(w) for k, w in inputs.items()}
    g0, e0, g1, e1 = "L0_gnn_", "L0_ffn_", "L1_gnn_", "L1_ffn_"

    def blocks(vec):
        return vec.reshape(-1, P).T

    def heads(vec):
        m = np.zeros((P, NH), np.float32)
        m[0:DH] = vec.reshape(NH, DH).T
        return m

    bqkv = a[g0 + "bqkv"]
    prio = np.tile(np.arange(8, 0, -1, dtype=np.float32), (P, NT))
    cols = np.concatenate([
        blocks(a[g0 + "bn"]), blocks(a[g0 + "be"]), blocks(a[g0 + "ln_g"]), blocks(a[g0 + "ln_b"]),
        blocks(a[g0 + "b2"]), heads(bqkv[0:D]), heads(bqkv[D:2 * D]), blocks(a[e0 + "b1"]), blocks(a[e1 + "b1"]), prio], axis=1)
    rows = np.concatenate([w.reshape(-1) for w in (
        a[g0 + "b1"], bqkv[2 * D:], a[g0 + "bo"], a[g1 + "b1"], a[g1 + "att_src1"], a[g1 + "att_dst1"],
        a[g1 + "b2"], a[g1 + "att_src2"], a[g1 + "att_dst2"], a[e0 + "bg"], a[e1 + "bg"])])
    arrays = {
        "x": a["x"], "src": a["src"].reshape(E // P, P).T, "dst": a["dst"].reshape(E // P, P).T,
        "edge": a["edge_attr_256"], "cols": cols, "rows": rows,
        "ident_d": np.eye(P, dtype=np.float32), "iota_d": np.arange(N, dtype=np.float32),
        "wn": a[g0 + "Wn"].T, "we": a[g0 + "We"].T, "w1": a[g0 + "W1"].transpose(0, 2, 1),
        "w2": a[g0 + "W2"].transpose(0, 2, 1), "wqkv": a[g0 + "Wqkv"].T, "wo": a[g0 + "Wo"].T,
        "wg0": a[e0 + "Wg"], "e0w1": a[e0 + "W1"], "e0w2": a[e0 + "W2"], "e0b2": a[e0 + "b2"],
        "gw1": a[g1 + "W1"].T, "gw2": a[g1 + "W2"].T,
        "wg1": a[e1 + "Wg"], "e1w1": a[e1 + "W1"], "e1w2": a[e1 + "W2"], "e1b2": a[e1 + "b2"],
    }
    nc = bacc.Bacc("TRN2", target_bir_lowering=False, num_devices=1)
    args, feed = [], {}
    for name, w in arrays.items():
        w = np.ascontiguousarray(w)
        feed[f"in_{name}"] = w
        args.append(nc.dram_tensor(f"in_{name}", w.shape, mybir.dt.from_np(w.dtype), kind="ExternalInput").ap())
    args.append(nc.dram_tensor("out_0", _OUT[0], F32, kind="ExternalOutput").ap())
    build(nc, *args)
    r = run_bass_kernel_spmd(nc, [feed], core_ids=[0])
    return r.results[0]["out_0"]
```

```python
from contextlib import ExitStack

import concourse.bass as bass
from concourse import mybir

P = 128
F32 = mybir.dt.float32
F32R = mybir.dt.float32r
I32 = mybir.dt.int32
ALU = mybir.AluOpType
ACT = mybir.ActivationFunctionType
AX_X = mybir.AxisListType.X

N = 512
NT = N // P
D = 768
DC = D // P
HALF = D // 2
DE = 256
E = 8192
L = 3
NH, DH = 8, 96
NE0, H0 = 8, 1536
NE1, H1 = 4, 384
GH, GC = 8, 128
GD = GH * GC
EPS = 1e-5
DEN_EPS = 1e-16
NONE = -1e30
FLOOR = -1e25

NEWTON = 4

RING = 4
STATS_STEPS = 3 * NT + 3 + 3 * NEWTON
GROUP = 8
GROUPS = E // P // GROUP

STAGES = [
    ("xt0", 3, 3), ("wn", 3, 3), ("tok0", 4, 4), ("edges", 4, 2), ("deg", 0, 1), ("base", 0, DC),
    ("rounds", L * 10, L * 24), ("v", 0, 8), ("heads", NH * 7, NH * 4), ("wo", 0, 8),
    ("xt1", 3, 3), ("gate0", 0, 3), ("bias0", 0, 8),
    ("xt2", 3, 3), ("h1", 4, 4), ("mask", 0, 4), ("gat1", 0, GH * 7), ("o1t", 4, 4), ("h2", 4, 4),
    ("gat2", 0, 13), ("xt3", 3, 3), ("gate1", 0, 3), ("bias1", 0, 8),
]
ACT0, DVE0 = {}, {}
_a = _v = 0
for _name, _da, _dv in STAGES:
    if _name == "xt2":
        _a = _v = 0
    ACT0[_name], DVE0[_name] = _a, _v
    _a, _v = _a + _da, _v + _dv

COLS = {}
_c = 0
for _name, _w in [("bn", DC), ("be", DC), ("ln_g", L * DC), ("ln_b", L * DC), ("b2", L * DC),
                  ("bq", NH), ("bk", NH), ("e0b1", NE0 * H0 // P), ("e1b1", NE1 * H1 // P),
                  ("prio", NT * 8), ("tri8", 64), ("iota16", 16)]:
    COLS[_name] = _c
    _c += _w
NCOLS = _c
ROWS = {}
_c = 0
for _name, _w in [("b1", L * D), ("bv", D), ("bo", D), ("g_b1", GD), ("g_src1", GD), ("g_dst1", GD),
                  ("g_b2", D), ("g_src2", D), ("g_dst2", D), ("bg0", NE0), ("bg1", NE1)]:
    ROWS[_name] = _c
    _c += _w
NROWS = _c


def wait(eng, sem, value):
    if not isinstance(value, int) or value > 0:
        eng.wait_ge(sem, value)


def build(nc, x, src, dst, edge, cols, rows, ident_d, iota_d, tri_d, wn, we, w1, w2, wqkv, wo, wg0, e0w1,
          e0w2, e0b2, gw1, gw2, wg1, e1w1, e1w2, e1b2, xs0, ys0, xs1, ys1, out):
    ctx = ExitStack()
    with ctx:
        start = (nc.sbuf_base + 63) // 64 * 64
        top = [0]

        def place(name, shape, dt, at=None):
            size = 1
            for s in shape[1:]:
                size *= s
            if at is None:
                at = top[0]
                top[0] += (size + 7) // 8 * 8
            return nc.alloc_sbuf_tensor_at(name, shape, dt, offset=start + 4 * at)

        def sem(name):
            return ctx.enter_context(nc.semaphore(name))

        slot = [place(f"slot{s}", [P, 4608], F32) for s in range(4)]
        ident = place("ident", [P, P], F32)
        ones = place("ones", [P, P], F32)
        tri = place("tri", [P, P], F32)
        par = place("par", [P, NCOLS], F32)
        xres = place("xres", [P, NT, D], F32)
        ct = place("ct", [P, NT, N], F32)
        cpt_at = top[0]
        cpt = place("cpt", [P, NT, N], F32)
        mask = place("mask", [P, NT, N], F32, cpt_at)
        bc_at = top[0]
        brow = place("brow", [P, 2, D], F32)
        bns = place("bns", [P, NT, 2, 6], F32)
        mv = place("mv", [P, NT, 2], F32)
        rstd = place("rstd", [P, NT], F32)
        root = place("root", [P, 2, NT], F32)
        nbias = place("nbias", [P, 2, NT], F32)
        rsum = place("rsum", [P, 2, NT], F32)
        rinv = place("rinv", [P, 2, NT], F32)
        logit = place("logit", [P, NT, 8], F32)
        prob = place("prob", [P, NT, 8], F32)
        pick = [place(f"pick{i}", [P, NT, 8], F32) for i in range(4)]
        top4 = place("top4", [P, NT], F32)
        gate = place("gate", [P, NT, 8], F32)
        gate_t = place("gate_t", [8, N], F32)
        wg = place("wg", [P, DC, 8], F32)
        bg = place("bg", [P, 12], F32)
        att = place("att", [P, 2, NT, GH], F32)
        gmax = place("gmax", [P, 2, NT], F32)
        gdec = place("gdec", [P, 2, 4, NT], F32)
        sel = place("sel", [P, NT, 8], F32)
        count = place("count", [P, NT + 1, 8], F32)
        chunks = place("chunks", [P, 3, 8], F32)
        low8 = place("low8", [P, 8, 8], F32)
        low16 = place("low16", [P, 16, 8], F32)
        slot_of = place("slot_of", [P, NT, 8], F32)
        pos = place("pos", [P, 2, NT], F32)
        pos_i = place("pos_i", [P, 2, NT], I32)
        share = place("share", [P, 2, NT], F32)
        plan = place("plan", [P, 17], F32)
        plan_i = place("plan_i", [P, 17], I32)
        zrow = place("zrow", [P, D], F32)
        area = top[0]

        def over(name, shape, at, dt=F32):
            return place(name, shape, dt, area + at)

        nodes = over("nodes", [P, NT, D], 0)
        nodes_t = over("nodes_t", [P, DC, N], 3072)
        xn = over("xn", [P, NT, D], 0)
        xn_t = over("xn_t", [P, DC, N], 6144)
        ea_raw = over("ea_raw", [P, 2, GROUP, DE], 6144)
        ea_hi = over("ea_hi", [P, 2, GROUP, DE], 10240, F32R)
        ea_lo = over("ea_lo", [P, 2, GROUP, DE], 14336, F32R)
        hot_d = over("hot_d", [P, 2, N], 18432, F32R)
        hot_s = over("hot_s", [P, 2, N], 19456, F32R)
        iota = over("iota", [P, N], 20480)
        ends_i = over("ends_i", [P, 2, E // P], 20992, I32)
        ends = over("ends", [P, 2, E // P], 21120)
        sea_t = over("sea_t", [P, DE // P, N], 21248)
        zero = over("zero", [P, N], 22272, F32R)
        deg = over("deg", [P, N], 18432)
        agg_t = over("agg_t", [P, DC, N], 6144)
        base_t = over("base_t", [P, DC, N], 9216)
        h = over("h", [P, NT, D], 12288)
        h_t = over("h_t", [P, DC, N], 15360)
        v = over("v", [P, NT, D], 12288)
        attn_t = over("attn_t", [DH, NH, N], 6144)
        q_t = over("q_t", [DH, 2, N], 10240)
        k_t = over("k_t", [DH, 2, N], 11264)
        prb = over("prb", [P, 2, NT, N], 15360)
        prb_t = over("prb_t", [P, NT, N], 19456)
        xn1 = over("xn1", [P, NT, D], 0)
        xn1_t = over("xn1_t", [P, DC, N], 3072)
        e0b2_s = place("e0b2_s", [NE0, D], F32, cpt_at)
        item_x = over("item_x", [P, D], 6144)
        item_xt = over("item_xt", [P, DC, P], 6912)
        hid = over("hid", [P, H0], 7680)
        hid_t = over("hid_t", [P, H0 // P, P], 9216)
        item_y = over("item_y", [P, D], 10752)
        got = over("got", [P, NT, 2, D], 12288)
        xn2 = over("xn2", [P, NT, D], 0)
        xn2_t = over("xn2_t", [P, DC, N], 3072)
        h1x = over("h1x", [P, NT, GH, GC + 2], 6144)
        out1 = over("out1", [P, NT, GD], 0)
        g_b1 = over("g_b1", [P, GD], 4096)
        g_b2 = over("g_b2", [P, D], 5120)
        h2x = over("h2x", [P, NT, D + 2], 6144)
        att1 = over("att1", [P, 2, GD], 10304)
        scr = over("scr", [P, GD], 12352)
        arg = over("arg", [P, 2, NT, N], 10304)
        arg2 = over("arg2", [P, NT, N], 14400)
        gp = over("gp", [P, NT, N], 16448)
        gp_t = over("gp_t", [P, NT, N], 18496)
        out1_t = over("out1_t", [P, GD // P, N], 10304)
        xn3 = over("xn3", [P, NT, D], 0)
        xn3_t = over("xn3_t", [P, DC, N], 3072)
        e1b2_s = place("e1b2_s", [NE1, D], F32, cpt_at)

        act_ps = [ctx.enter_context(nc.psum_tensor(f"act_ps{i}", [P, N], F32)) for i in range(RING)]
        dve_ps = [ctx.enter_context(nc.psum_tensor(f"dve_ps{i}", [P, N], F32)) for i in range(RING)]

        class Signals:
            def __init__(self, part):
                self.to_act = sem(f"to_act_{part}")
                self.to_dve = sem(f"to_dve_{part}")
                self.act_freed = sem(f"act_freed_{part}")
                self.dve_freed = sem(f"dve_freed_{part}")

        class Run(Signals):

            def __init__(self, layer, ne, hidden, picks, up, down, scattered, results, b1, up_slots, down_slots, down_banks):
                super().__init__(f"run{layer}")
                self.layer, self.ne, self.picks, self.up, self.down = layer, ne, picks, up, down
                self.scattered, self.results, self.b1 = scattered, results, b1
                self.up_slots, self.down_slots, self.down_banks = up_slots, down_slots, down_banks
                self.blocks = hidden // P
                self.n_up = hidden // HALF
                self.n_turn = -(-self.blocks // 4)
                self.items_min = picks * N // P
                self.items_max = self.items_min + ne - 1
                self.w_in = {s: sem(f"w_in{layer}_{s}") for s in up_slots + down_slots}
                self.x_in = sem(f"x_in{layer}")
                self.y_out = sem(f"y_out{layer}")
                self.filled = sem(f"filled{layer}")
                self.scattered_in = sem(f"scattered{layer}")
                self.gathered = [sem(f"gathered{layer}_{t}") for t in range(NT)]
                self.sel_set = sem(f"sel_set{layer}")
                self.plan_set = sem(f"plan_set{layer}")
                self.gate_set = sem(f"gate_set{layer}")

            def act_after(self, k):
                return k * (1 + self.n_turn) + 1

            def dve_after(self, k):
                return k * (1 + self.n_up + 2) + (1 + self.n_up)

        sig0, sig1 = Signals("a"), Signals("b")
        run0 = Run(0, NE0, H0, 2, e0w1, e0w2, xs0, ys0, "e0b1", (2, 3), (0, 1), (3, 0))
        run1 = Run(1, NE1, H1, 1, e1w1, e1w2, xs1, ys1, "e1b1", (2,), (0,), (0, 1))
        slot_in = [sem(f"slot_in{s}") for s in range(4)]
        in_x = sem("in_x")
        in_par = sem("in_par")
        in_ends = sem("in_ends")
        in_edge = [sem("in_edge0"), sem("in_edge1")]
        in_row = [sem("in_row0"), sem("in_row1")]
        in_gate = sem("in_gate")
        in_eb2 = sem("in_eb2")
        in_tri = sem("in_tri")
        stood = sem("stood")
        in_att1 = sem("in_att1")
        in_gb = sem("in_gb")
        in_gate1 = sem("in_gate1")
        out_done = sem("out_done")
        final = sem("final")
        dve_step = sem("dve_step")
        act_step = sem("act_step")
        normed = sem("normed")
        const_set = sem("const_set")
        zrow_set = sem("zrow_set")
        ea_split = sem("ea_split")
        ea_high = sem("ea_high")
        hots = sem("hots")
        chunk_done = sem("chunk_done")
        cpt_set = sem("cpt_set")
        row_max = sem("row_max")
        exp_done = sem("exp_done")
        prob_set = sem("prob_set")
        logit_set = sem("logit_set")
        prob_exp = sem("prob_exp")
        att_set = sem("att_set")
        g_max = sem("g_max")
        g_low = sem("g_low")
        g_arg = sem("g_arg")
        g_exp = sem("g_exp")

        block = ctx.enter_context(nc.Block())

        def bview(name, width):
            return rows[ROWS[name]:ROWS[name] + width].partition_broadcast(P)

        def col(name, i, n=1):
            return par[:, COLS[name] + i:COLS[name] + i + n]

        def k_unit(hd):
            return 0 if hd == 0 else 1 + 7 * (hd - 1) + 4

        def score_unit(hd):
            return 1 + 7 * hd

        def turn_unit_a(hd):
            return 1 + 7 * hd + 4 + (1 if hd < NH - 1 else 0)

        def q_unit(hd):
            return 0 if hd == 0 else 1 + 4 * (hd - 1)

        def turn_unit_v(hd):
            return 1 + 4 * hd + (1 if hd < NH - 1 else 0)

        def pv_unit(hd):
            return turn_unit_v(hd) + 2

        @block.sync
        def _(sp):
            sig = sig0
            def load(s, dst, source):
                sp.dma_start(dst, source).then_inc(slot_in[s], 16)

            def kview(ap):
                return ap.rearrange("(k p) n -> p k n", p=P)

            def sview(s, k, n):
                return slot[s][:, 0:k * n].rearrange("p (k n) -> p k n", k=k)

            sp.dma_start(xres[:, :, :], x.rearrange("(t p) d -> p t d", p=P)).then_inc(in_x, 16)
            sp.dma_start(ident[:, :], ident_d).then_inc(in_par, 16)
            sp.dma_start(par[:, :], cols).then_inc(in_par, 16)
            sp.dma_start(tri[:, :], tri_d).then_inc(in_tri, 16)
            load(0, sview(0, DC, D), kview(wn))
            sp.dma_start(iota[:, :], iota_d.partition_broadcast(P)).then_inc(in_ends, 16)
            sp.dma_start(ends_i[:, 0, :], src).then_inc(in_ends, 16)
            sp.dma_start(ends_i[:, 1, :], dst).then_inc(in_ends, 16)
            wait(sp, sig.to_act, ACT0["tok0"])
            wait(sp, sig.to_dve, DVE0["tok0"])

            def load_edges(g, b):
                sp.dma_start(ea_raw[:, b, :, :],
                             edge[bass.ds(g * GROUP * P, GROUP * P), :].rearrange("(c p) d -> p c d", p=P)
                             ).then_inc(in_edge[b], 16)

            for b in range(2):
                load_edges(b, b)
            load(1, sview(1, DE // P, D), kview(we))
            load(2, sview(2, DC, D), kview(w1[0, 0:D, :]))
            load(3, sview(3, DC, D), kview(w1[0, D:2 * D, :]))
            load(0, sview(0, DC, D), kview(w2[0]))
            sp.dma_start(brow[:, 0, :], bview("b1", D)).then_inc(in_row[0], 16)
            sp.dma_start(brow[:, 1, :], bview("bv", D)).then_inc(in_row[1], 16)
            with sp.Fori(1, GROUPS // 2) as i:
                for b in range(2):
                    sp.wait_ge(ea_split, 2 * i - 1 + b)
                    load_edges(2 * i + b, b)
            with sp.Fori(1, L) as l:
                sp.wait_ge(sig.to_dve, DVE0["rounds"] + 24 * (l - 1) + 14)
                load(2, sview(2, DC, D), kview(w1[bass.ds(l, 1), 0:D, :].rearrange("a k n -> (a k) n")))
                load(3, sview(3, DC, D), kview(w1[bass.ds(l, 1), D:2 * D, :].rearrange("a k n -> (a k) n")))
                sp.wait_ge(sig.dve_freed, DVE0["rounds"] + 24 * (l - 1) + 14)
                sp.dma_start(brow[:, 0, :], rows[bass.ds(ROWS["b1"] + l * D, D)].partition_broadcast(P)
                             ).then_inc(in_row[0], 16)
                sp.wait_ge(sig.to_dve, DVE0["rounds"] + 24 * (l - 1) + 20)
                load(0, sview(0, DC, D), kview(w2[bass.ds(l, 1), :, :].rearrange("a k n -> (a k) n")))
            last = DVE0["rounds"] + 24 * (L - 1)
            load(1, sview(1, DC, D), kview(wqkv[:, 0:D]))
            sp.wait_ge(sig.to_dve, last + 14)
            load(2, sview(2, DC, D), kview(wqkv[:, D:2 * D]))
            load(3, sview(3, DC, D), kview(wqkv[:, 2 * D:3 * D]))
            sp.wait_ge(sig.dve_freed, last + 14)
            sp.dma_start(brow[:, 0, :], bview("bo", D)).then_inc(in_row[0], 16)
            sp.wait_ge(sig.to_dve, last + 20)
            load(0, slot[0][0:DH, 0:4 * D].rearrange("p (k n) -> p k n", k=4),
                 wo[0:4 * DH, :].rearrange("(k p) n -> p k n", p=DH))
            sp.dma_start(wg[:, :, :], wg0.rearrange("(k p) n -> p k n", p=P)).then_inc(in_gate, 16)
            sp.dma_start(bg[:, 0:NE0], bview("bg0", NE0)).then_inc(in_gate, 16)
            sp.dma_start(bg[:, 8:8 + NE1], bview("bg1", NE1)).then_inc(in_gate, 16)
            sp.wait_ge(sig.to_act, ACT0["heads"] + k_unit(NH - 1) + 1)
            sp.wait_ge(sig.to_dve, DVE0["heads"] + q_unit(NH - 1) + 1)
            load(1, slot[1][0:DH, 0:4 * D].rearrange("p (k n) -> p k n", k=4),
                 wo[4 * DH:8 * DH, :].rearrange("(k p) n -> p k n", p=DH))

            sp.dma_start(e0b2_s[:, :], e0b2).then_inc(in_eb2, 16)

            def run_items(run):
                sp.wait_ge(run.plan_set, 1)
                last = sp.value_load(plan_i[0:1, 16:17], min_val=run.items_min - 1, max_val=run.items_max - 1)

                def expert(i):
                    return sp.value_load(plan_i[0:1, bass.ds(i, 1)], min_val=0, max_val=run.ne - 1)

                def load_x(i):
                    sp.dma_start(item_x[:, :], run.scattered[bass.ds(i * P, P), :]).then_inc(run.x_in, 16)

                def load_up(i, free):
                    w = run.up[bass.ds(expert(i), 1), :, :].rearrange("a k n -> (a k) n")
                    width = run.blocks * P // len(run.up_slots)
                    for j, s in enumerate(run.up_slots):
                        wait(sp, run.to_dve, free[j])
                        sp.dma_start(sview(s, DC, width), kview(w[:, j * width:(j + 1) * width])).then_inc(run.w_in[s], 16)

                def load_down(i):
                    w = run.down[bass.ds(expert(i), 1), :, :].rearrange("a k n -> (a k) n")
                    rows_in = run.blocks * P // len(run.down_slots)
                    for j, s in enumerate(run.down_slots):
                        sp.dma_start(sview(s, rows_in // P, D), kview(w[j * rows_in:(j + 1) * rows_in, :])).then_inc(run.w_in[s], 16)

                n = len(run.up_slots)
                load_up(0, [0] * n)
                sp.wait_ge(run.scattered_in, 16 * NT * run.picks)
                load_x(0)
                sp.wait_ge(run.to_act, 1)
                sp.wait_ge(run.to_dve, 1)
                load_x(1)
                load_up(1, [1 + run.n_up * (j + 1) // n for j in range(n)])
                load_down(0)
                with sp.Fori(1, last) as k:
                    a, v = run.act_after(k - 1), run.dve_after(k - 1)
                    sp.wait_ge(run.to_act, a + 1)
                    sp.wait_ge(run.to_dve, v + 1)
                    load_x(k + 1)
                    load_up(k + 1, [v + 1 + run.n_up * (j + 1) // n for j in range(n)])
                    sp.wait_ge(run.to_dve, run.dve_after(k))
                    sp.sem_inc(stood, 1)
                    load_down(k)
                sp.wait_ge(run.to_dve, run.dve_after(last))
                sp.sem_inc(stood, 1)
                load_down(last)
                return last

            last = run_items(run0)
            sig = sig1
            load(2, sview(2, DC, N), kview(gw1[:, 0:N]))
            load(3, sview(3, DC, N), kview(gw1[:, N:2 * N]))
            sp.wait_ge(run0.to_dve, run0.dve_after(last) + 2)
            load(0, sview(0, 4, D), kview(gw2[0:N, :]))
            load(1, sview(1, 4, D), kview(gw2[N:2 * N, :]))
            sp.wait_ge(normed, NT * (L + 3))
            sp.dma_start(att1[:, :, :], rows[ROWS["g_src1"]:ROWS["g_src1"] + 2 * GD]
                         .rearrange("(a n) -> a n", a=2).partition_broadcast(P)).then_inc(in_att1, 16)
            sp.dma_start(brow[:, :, :], rows[ROWS["g_src2"]:ROWS["g_src2"] + 2 * D]
                         .rearrange("(a n) -> a n", a=2).partition_broadcast(P)).then_inc(in_row[0], 16)
            sp.wait_ge(sig.to_act, ACT0["mask"])
            sp.wait_ge(sig.to_dve, DVE0["mask"])
            sp.dma_start(g_b1[:, :], bview("g_b1", GD)).then_inc(in_gb, 16)
            sp.dma_start(g_b2[:, :], bview("g_b2", D)).then_inc(in_gb, 16)

            sp.dma_start(wg[:, :, 0:NE1], wg1.rearrange("(k p) n -> p k n", p=P)).then_inc(in_gate1, 16)
            sp.wait_ge(sig.to_dve, DVE0["xt3"])
            sp.dma_start(e1b2_s[:, :], e1b2).then_inc(in_eb2, 16)
            run_items(run1)
            for t in range(NT):
                sp.wait_ge(final, t + 1)
                sp.dma_start(out[t * P:(t + 1) * P, :], xres[:, t, :]).then_inc(out_done, 16)
            sp.wait_ge(out_done, 16 * NT)

        @block.tensor
        def _(pe):
            sig = sig0
            mm = nc.tensor.matmul

            def act_bank(j, before):
                wait(pe, sig.act_freed, before + max(0, j - RING + 1))
                return act_ps[j % RING]

            def dve_bank(j, before):
                wait(pe, sig.dve_freed, before + max(0, j - RING + 1))
                return dve_ps[j % RING]

            def turn_features(source, a0, v0, normed_by=None):
                for c in range(DC):
                    bank = act_bank(c // 2, a0) if c % 2 == 0 else dve_bank(c // 2, v0)
                    for t in range(NT):
                        last = nc.tensor.transpose(bank[:, t * P:(t + 1) * P], source[:, t, c * P:(c + 1) * P], ident[:, :])
                    last.then_inc(sig.to_act if c % 2 == 0 else sig.to_dve, 1)

            def turn_tokens(source, a0, v0):
                for t in range(NT):
                    for half in range(2):
                        bank = act_bank(t, a0) if half == 0 else dve_bank(t, v0)
                        for j in range(3):
                            last = nc.tensor.transpose(bank[:, j * P:(j + 1) * P],
                                                       source[:, half * 3 + j, t * P:(t + 1) * P], ident[:, :])
                        last.then_inc(sig.to_act if half == 0 else sig.to_dve, 1)

            def kslot(s, n):
                return slot[s][:, 0:4608 // n * n].rearrange("p (k n) -> p k n", n=n)

            pe.wait_ge(in_par, 32)
            pe.wait_ge(normed, NT)
            turn_features(xn, ACT0["xt0"], DVE0["xt0"])
            pe.wait_ge(slot_in[0], 16)
            pe.wait_ge(sig.act_freed, ACT0["wn"])
            pe.wait_ge(sig.dve_freed, DVE0["wn"])
            wn_s = kslot(0, D)
            for c in range(DC):
                bank = act_bank(c // 2, ACT0["wn"]) if c % 2 == 0 else dve_bank(c // 2, DVE0["wn"])
                for k in range(DC):
                    last = mm(bank[:, :], wn_s[:, k, c * P:(c + 1) * P], xn_t[:, k, :], start=(k == 0), stop=(k == DC - 1))
                last.then_inc(sig.to_act if c % 2 == 0 else sig.to_dve, 1)
            pe.wait_ge(sig.act_freed, ACT0["tok0"])
            pe.wait_ge(sig.dve_freed, DVE0["tok0"])
            turn_tokens(nodes_t, ACT0["tok0"], DVE0["tok0"])

            pe.wait_ge(sig.act_freed, ACT0["edges"])
            pe.wait_ge(sig.dve_freed, DVE0["edges"])
            pe.wait_ge(const_set, 2)
            sums = act_ps + dve_ps[0:2]
            for bank in sums:
                last = mm(bank[:, :], zero[:, 0:P], zero[:, :], start=True, stop=False)
            last.then_inc(chunk_done, 1)
            with pe.Fori(0, GROUPS // 2) as i:
                for b in range(2):
                    pe.wait_ge(ea_split, 2 * i + b + 1)
                    pe.wait_ge(ea_high, 2 * i + b + 1)
                    for c in range(GROUP):
                        pe.wait_ge(hots, (2 * i + b) * GROUP + c + 1)
                        hd, hs = hot_d[:, c % 2, :], hot_s[:, c % 2, :]
                        for m in range(NT):
                            mm(act_ps[m][:, :], hs[:, m * P:(m + 1) * P], hd, start=False, stop=False)
                        for m in range(DE // P):
                            for part in (ea_hi, ea_lo):
                                last = mm(dve_ps[m][:, :], part[:, b, c, m * P:(m + 1) * P], hd, start=False, stop=False)
                        last.then_inc(chunk_done, 1)
            for n, bank in enumerate(sums):
                mm(bank[:, :], zero[:, 0:P], zero[:, :], start=False, stop=True).then_inc(
                    sig.to_act if n < NT else sig.to_dve, 1)

            pe.wait_ge(sig.act_freed, ACT0["deg"])
            bank = dve_bank(0, DVE0["deg"])
            for m in range(NT):
                last = mm(bank[:, :], ones[:, :], ct[:, m, :], start=(m == 0), stop=(m == NT - 1))
            last.then_inc(sig.to_dve, 1)
            pe.wait_ge(slot_in[1], 16)
            pe.wait_ge(sig.dve_freed, DVE0["base"])
            for c in range(DC):
                bank = dve_bank(c, DVE0["base"])
                for k in range(DE // P):
                    last = mm(bank[:, :], kslot(1, D)[:, k, c * P:(c + 1) * P], sea_t[:, k, :],
                              start=(k == 0), stop=(k == DE // P - 1))
                last.then_inc(sig.to_dve, 1)

            pe.wait_ge(cpt_set, 1)
            with pe.Fori(0, L) as l:
                a0, v0 = ACT0["rounds"] + 10 * l, DVE0["rounds"] + 24 * l
                pe.wait_ge(sig.act_freed, a0)
                for c in range(DC):
                    bank = dve_bank(c, v0)
                    for k in range(NT):
                        last = mm(bank[:, :], nodes[:, k, c * P:(c + 1) * P], cpt[:, k, :], start=(k == 0), stop=(k == NT - 1))
                    last.then_inc(sig.to_dve, 1)
                pe.wait_ge(slot_in[2], 16 * (l + 1))
                pe.wait_ge(slot_in[3], 16 * (l + 1))
                pe.wait_ge(sig.dve_freed, v0 + DC)
                for u in range(8):
                    t, half = u // 2, u % 2
                    bank = dve_bank(u, v0 + 6)
                    for k in range(2 * DC):
                        act_t = nodes_t[:, k, :] if k < DC else agg_t[:, k - DC, :]
                        w = kslot(2 if k < DC else 3, D)[:, k % DC, half * HALF:(half + 1) * HALF]
                        last = mm(bank[:, 0:HALF], act_t[:, t * P:(t + 1) * P], w, start=(k == 0), stop=(k == 2 * DC - 1))
                    last.then_inc(sig.to_dve, 1)
                pe.wait_ge(normed, NT * (l + 2))
                for c in range(DC):
                    bank = act_bank(c, a0)
                    for t in range(NT):
                        last = nc.tensor.transpose(bank[:, t * P:(t + 1) * P], h[:, t, c * P:(c + 1) * P], ident[:, :])
                    last.then_inc(sig.to_act, 1)
                pe.wait_ge(slot_in[0], 16 * (l + 2))
                pe.wait_ge(sig.act_freed, a0 + DC)
                for c in range(DC):
                    bank = dve_bank(c, v0 + 14)
                    for k in range(DC):
                        last = mm(bank[:, :], kslot(0, D)[:, k, c * P:(c + 1) * P], h_t[:, k, :], start=(k == 0), stop=(k == DC - 1))
                    last.then_inc(sig.to_dve, 1)
                pe.wait_ge(sig.dve_freed, v0 + 20)
                turn_tokens(nodes_t, a0 + 6, v0 + 20)

            pe.wait_ge(slot_in[3], 16 * (L + 1))
            for u in range(8):
                t, half = u // 2, u % 2
                bank = dve_bank(u, DVE0["v"])
                for k in range(DC):
                    last = mm(bank[:, 0:HALF], nodes_t[:, k, t * P:(t + 1) * P],
                              kslot(3, D)[:, k, half * HALF:(half + 1) * HALF], start=(k == 0), stop=(k == DC - 1))
                last.then_inc(sig.to_dve, 1)

            a0, v0 = ACT0["heads"], DVE0["heads"]

            def project(hd):
                for bank, s, signal in ((dve_bank(q_unit(hd), v0), 1, sig.to_dve), (act_bank(k_unit(hd), a0), 2, sig.to_act)):
                    for k in range(DC):
                        last = mm(bank[0:DH, :], kslot(s, D)[:, k, hd * DH:(hd + 1) * DH], nodes_t[:, k, :],
                                  start=(k == 0), stop=(k == DC - 1))
                    last.then_inc(signal, 1)

            def scores(hd):
                pe.wait_ge(sig.dve_freed, v0 + q_unit(hd) + 1)
                pe.wait_ge(sig.act_freed, a0 + k_unit(hd) + 1)
                for t in range(NT):
                    bank = act_bank(score_unit(hd) + t, a0)
                    mm(bank[:, :], q_t[:, hd % 2, t * P:(t + 1) * P], k_t[:, hd % 2, :], start=True, stop=True
                       ).then_inc(sig.to_act, 1)

            def turn_probs(hd):
                pe.wait_ge(prob_set, NT * (hd + 1))
                for m in range(NT):
                    bank = act_bank(turn_unit_a(hd) + m // 2, a0) if m % 2 == 0 else dve_bank(turn_unit_v(hd) + m // 2, v0)
                    for t in range(NT):
                        last = nc.tensor.transpose(bank[:, t * P:(t + 1) * P], prb[:, hd % 2, t, m * P:(m + 1) * P], ident[:, :])
                    last.then_inc(sig.to_act if m % 2 == 0 else sig.to_dve, 1)

            def weigh(hd):
                pe.wait_ge(sig.act_freed, a0 + turn_unit_a(hd) + 2)
                pe.wait_ge(sig.dve_freed, v0 + turn_unit_v(hd) + 2)
                bank = dve_bank(pv_unit(hd), v0)
                for m in range(NT):
                    last = mm(bank[0:DH, :], v[:, m, hd * DH:(hd + 1) * DH], prb_t[:, m, :], start=(m == 0), stop=(m == NT - 1))
                last.then_inc(sig.to_dve, 1)

            pe.wait_ge(slot_in[1], 32)
            pe.wait_ge(slot_in[2], 16 * (L + 1))
            project(0)
            scores(0)
            for hd in range(NH):
                if hd + 1 < NH:
                    project(hd + 1)
                turn_probs(hd)
                if hd + 1 < NH:
                    scores(hd + 1)
                weigh(hd)
            pe.wait_ge(slot_in[0], 16 * (L + 2))
            pe.wait_ge(slot_in[1], 48)
            pe.wait_ge(sig.dve_freed, DVE0["wo"])
            for u in range(8):
                t, half = u // 2, u % 2
                bank = dve_bank(u, DVE0["wo"])
                for hd in range(NH):
                    w = slot[hd // 4][0:DH, 0:4 * D].rearrange("p (k n) -> p k n", k=4)[:, hd % 4, half * HALF:(half + 1) * HALF]
                    last = mm(bank[:, 0:HALF], attn_t[:, hd, t * P:(t + 1) * P], w, start=(hd == 0), stop=(hd == NH - 1))
                last.then_inc(sig.to_dve, 1)

            def gates(run, xt, ne, stage, bias_stage, b2, k_in):
                pe.wait_ge(*k_in)
                bank = dve_bank(0, DVE0[stage])
                for t in range(NT):
                    for k in range(DC):
                        last = mm(bank[:, t * ne:(t + 1) * ne], xt[:, k, t * P:(t + 1) * P], wg[:, k, 0:ne],
                                  start=(k == 0), stop=(k == DC - 1))
                last.then_inc(sig.to_dve, 1)
                pe.wait_ge(run.sel_set, 1)
                bank = dve_bank(1, DVE0[stage])
                for t in range(NT + 1):
                    for m in range(min(t + 1, NT)):
                        last = mm(bank[:, t * ne:(t + 1) * ne], tri[:, :] if m == t else ones[:, :], sel[:, m, 0:ne],
                                  start=(m == 0), stop=(m == min(t, NT - 1)))
                last.then_inc(sig.to_dve, 1)
                pe.wait_ge(run.gate_set, 1)
                bank = dve_bank(2, DVE0[stage])
                for t in range(NT):
                    last = nc.tensor.transpose(bank[0:ne, t * P:(t + 1) * P], gate[:, t, 0:ne], ident[:, :])
                last.then_inc(sig.to_dve, 1)
                pe.wait_ge(in_eb2, 16 if ne == NE0 else 32)
                pe.wait_ge(sig.dve_freed, DVE0[bias_stage])
                for u in range(8):
                    t, half = u // 2, u % 2
                    bank = dve_bank(u, DVE0[bias_stage])
                    mm(bank[:, 0:HALF], gate_t[0:ne, t * P:(t + 1) * P], b2[:, half * HALF:(half + 1) * HALF],
                       start=True, stop=True).then_inc(sig.to_dve, 1)

            pe.wait_ge(normed, NT * (L + 2))
            turn_features(xn1, ACT0["xt1"], DVE0["xt1"])
            pe.wait_ge(sig.act_freed, ACT0["gate0"])
            pe.wait_ge(sig.dve_freed, DVE0["gate0"])
            pe.wait_ge(in_tri, 16)
            gates(run0, xn1_t, NE0, "gate0", "bias0", e0b2_s, (in_gate, 48))

            def run_items(run):
                pe.wait_ge(run.plan_set, 1)
                last = pe.value_load(plan_i[0:1, 16:17], min_val=run.items_min - 1, max_val=run.items_max - 1)

                def turn_x(i, a, v):
                    pe.wait_ge(run.x_in, 16 * (i + 1))
                    wait(pe, run.act_freed, a)
                    wait(pe, run.dve_freed, v if isinstance(v, int) else v - 2)
                    for half, (bank, signal) in enumerate(((act_ps[3], run.to_act), (dve_ps[2], run.to_dve))):
                        for j in range(3):
                            c = 3 * half + j
                            last = nc.tensor.transpose(bank[:, j * P:(j + 1) * P], item_x[:, c * P:(c + 1) * P], ident[:, :])
                        last.then_inc(signal, 1)

                def turn_hidden(v_up):
                    pe.wait_ge(run.dve_freed, v_up)
                    for u in range(run.n_turn):
                        for j in range(min(4, run.blocks - 4 * u)):
                            last = nc.tensor.transpose(act_ps[u][:, j * P:(j + 1) * P],
                                                       hid[:, (4 * u + j) * P:(4 * u + j + 1) * P], ident[:, :])
                        last.then_inc(run.to_act, 1)

                def times_up(i, a, v):
                    pe.wait_ge(run.act_freed, a + 1)
                    pe.wait_ge(run.dve_freed, v + 1)
                    per = run.n_up // len(run.up_slots)
                    for u in range(run.n_up):
                        s = run.up_slots[u // per]
                        if u % per == 0:
                            pe.wait_ge(run.w_in[s], 16 * (i + 1))
                        for k in range(DC):
                            last = mm(dve_ps[(3 + u) % 4][:, 0:HALF], item_xt[:, k, :],
                                      kslot(s, per * HALF)[:, k, u % per * HALF:(u % per + 1) * HALF],
                                      start=(k == 0), stop=(k == DC - 1))
                        last.then_inc(run.to_dve, 1)

                def times_down(i, a_turned, v_banks):
                    pe.wait_ge(run.act_freed, a_turned)
                    for s in run.down_slots:
                        pe.wait_ge(run.w_in[s], 16 * (i + 1))
                    for half in range(2):
                        pe.wait_ge(run.dve_freed, v_banks[half])
                        for k in range(run.blocks):
                            s = run.down_slots[k // DC]
                            last = mm(dve_ps[run.down_banks[half]][:, 0:HALF], hid_t[:, k, :],
                                      kslot(s, D)[:, k % DC, half * HALF:(half + 1) * HALF],
                                      start=(k == 0), stop=(k == run.blocks - 1))
                        last.then_inc(run.to_dve, 1)

                pe.wait_ge(sig.act_freed, ACT0[f"bias{run.layer}"])
                pe.wait_ge(sig.dve_freed, DVE0[f"bias{run.layer}"] + 8)
                turn_x(0, 0, 0)
                times_up(0, 0, 0)

                def iteration(k):
                    a, v = run.act_after(k), run.dve_after(k)
                    turn_x(k + 1, a, v)
                    turn_hidden(v if isinstance(k, int) else v - 2)
                    times_up(k + 1, a, v)
                    times_down(k, a + 1 + run.n_turn, (v + 2, v + 3) if run.n_up > 1 else (v, v))

                iteration(0)
                with pe.Fori(1, last) as k:
                    iteration(k)
                a, v = run.act_after(last), run.dve_after(last)
                turn_hidden(v - 2)
                times_down(last, a + run.n_turn, (v, v))

            run_items(run0)
            sig = sig1

            pe.wait_ge(normed, NT * (L + 3))
            turn_features(xn2, ACT0["xt2"], DVE0["xt2"])
            pe.wait_ge(sig.act_freed, ACT0["h1"])
            pe.wait_ge(sig.dve_freed, DVE0["h1"])
            for s in (2, 3):
                pe.wait_ge(slot_in[s], 16 * (L + 2))
            for u in range(8):
                t, half = u // 2, u % 2
                bank = act_bank(t, ACT0["h1"]) if half == 0 else dve_bank(t, DVE0["h1"])
                for k in range(DC):
                    last = mm(bank[:, :], xn2_t[:, k, t * P:(t + 1) * P], kslot(2 + half, N)[:, k, :], start=(k == 0), stop=(k == DC - 1))
                last.then_inc(sig.to_act if half == 0 else sig.to_dve, 1)
            for t in range(NT):
                bank = dve_bank(t, DVE0["mask"])
                for m in range(NT):
                    last = nc.tensor.transpose(bank[:, m * P:(m + 1) * P], ct[:, m, t * P:(t + 1) * P], ident[:, :])
                last.then_inc(sig.to_dve, 1)

            def spread(a_src, unit, v0):
                bank = dve_bank(unit, v0)
                for t in range(NT):
                    last = mm(bank[:, t * P:(t + 1) * P], a_src(t).to_broadcast([P, P]), ident[:, :], start=True, stop=True)
                last.then_inc(sig.to_dve, 1)

            def turn_graph(unit, v0, g):
                pe.wait_ge(g_exp, g + 1)
                for m in range(NT):
                    bank = dve_bank(unit + m, v0)
                    for t in range(NT):
                        last = nc.tensor.transpose(bank[:, t * P:(t + 1) * P], gp[:, t, m * P:(m + 1) * P], ident[:, :])
                    last.then_inc(sig.to_dve, 1)
                pe.wait_ge(sig.dve_freed, v0 + unit + 4)

            pe.wait_ge(att_set, 1)
            v0 = DVE0["gat1"]
            spread(lambda t: att[:, 0, t, 0:1], 0, v0)
            unit = 1
            for hd in range(GH):
                if hd + 1 < GH:
                    spread(lambda t: att[:, 0, t, hd + 1:hd + 2], unit, v0)
                    unit += 1
                turn_graph(unit, v0, hd)
                unit += NT
                for pair in range(2):
                    bank = dve_bank(unit, v0)
                    for t in (2 * pair, 2 * pair + 1):
                        w = GC + 2
                        for m in range(NT):
                            last = mm(bank[:, (t % 2) * w:(t % 2 + 1) * w], gp_t[:, m, t * P:(t + 1) * P], h1x[:, m, hd, :],
                                      start=(m == 0), stop=(m == NT - 1))
                    last.then_inc(sig.to_dve, 1)
                    unit += 1
            pe.wait_ge(sig.dve_freed, DVE0["o1t"])
            for c in range(GD // P):
                bank = act_bank(c // 2, ACT0["o1t"]) if c % 2 == 0 else dve_bank(c // 2, DVE0["o1t"])
                for t in range(NT):
                    last = nc.tensor.transpose(bank[:, t * P:(t + 1) * P], out1[:, t, c * P:(c + 1) * P], ident[:, :])
                last.then_inc(sig.to_act if c % 2 == 0 else sig.to_dve, 1)
            pe.wait_ge(sig.act_freed, ACT0["h2"])
            pe.wait_ge(sig.dve_freed, DVE0["h2"])
            pe.wait_ge(slot_in[0], 16 * (L + 3))
            pe.wait_ge(slot_in[1], 64)
            for u in range(8):
                t, half = u // 2, u % 2
                bank = act_bank(t, ACT0["h2"]) if half == 0 else dve_bank(t, DVE0["h2"])
                for k in range(GD // P):
                    last = mm(bank[:, 0:HALF], out1_t[:, k, t * P:(t + 1) * P],
                              kslot(k // 4, D)[:, k % 4, half * HALF:(half + 1) * HALF], start=(k == 0), stop=(k == GD // P - 1))
                last.then_inc(sig.to_act if half == 0 else sig.to_dve, 1)
            pe.wait_ge(att_set, 2)
            v0 = DVE0["gat2"]
            spread(lambda t: att[:, 0, t, 0:1], 0, v0)
            turn_graph(1, v0, GH)
            for u in range(8):
                t, half = u // 2, 1 - u % 2
                bank = dve_bank(5 + u, v0)
                lo, hi = (0, HALF) if half == 0 else (HALF, D + 2)
                for m in range(NT):
                    last = mm(bank[:, 0:hi - lo], gp_t[:, m, t * P:(t + 1) * P], h2x[:, m, lo:hi], start=(m == 0), stop=(m == NT - 1))
                last.then_inc(sig.to_dve, 1)

            pe.wait_ge(normed, NT * (L + 4))
            turn_features(xn3, ACT0["xt3"], DVE0["xt3"])
            pe.wait_ge(sig.act_freed, ACT0["gate1"])
            pe.wait_ge(sig.dve_freed, DVE0["gate1"])
            gates(run1, xn3_t, NE1, "gate1", "bias1", e1b2_s, (in_gate1, 16))
            run_items(run1)

        @block.scalar
        def _(act):
            sig = sig0
            go = nc.scalar.activation

            def bank_of(j, before):
                act.wait_ge(sig.to_act, before + j + 1)
                return act_ps[j % RING]

            for c in range(0, DC, 2):
                bank = bank_of(c // 2, ACT0["xt0"])
                go(xn_t[:, c, :], bank[:, :], ACT.Copy).then_inc(sig.act_freed, 1)
            act.wait_ge(in_par, 32)
            for c in range(0, DC, 2):
                bank = bank_of(c // 2, ACT0["wn"])
                go(nodes_t[:, c, :], bank[:, :], ACT.Identity, bias=col("bn", c)).then_inc(sig.act_freed, 1)
            for t in range(NT):
                bank = bank_of(t, ACT0["tok0"])
                go(nodes[:, t, 0:HALF], bank[:, 0:HALF], ACT.Copy).then_inc(sig.act_freed, 1)
            with act.Fori(0, GROUPS // 2) as i:
                for b in range(2):
                    act.wait_ge(in_edge[b], 16 * (i + 1))
                    act.wait_ge(chunk_done, 1 + 2 * GROUP * i)
                    go(ea_hi[:, b, :, :], ea_raw[:, b, :, :], ACT.Copy).then_inc(ea_high, 1)
            for m in range(NT):
                bank = bank_of(m, ACT0["edges"])
                go(ct[:, m, :], bank[:, :], ACT.Copy).then_inc(sig.act_freed, 1)
            with act.Fori(0, L) as l:
                a0 = ACT0["rounds"] + 10 * l
                for c in range(DC):
                    bank = bank_of(c, a0)
                    go(h_t[:, c, :], bank[:, :], ACT.Relu, bias=par[:, bass.ds(COLS["ln_b"] + DC * l + c, 1)],
                       scale=par[:, bass.ds(COLS["ln_g"] + DC * l + c, 1)]).then_inc(sig.act_freed, 1)
                for t in range(NT):
                    bank = bank_of(t, a0 + 6)
                    go(nodes[:, t, 0:HALF], bank[:, 0:HALF], ACT.Copy).then_inc(sig.act_freed, 1)
            a0 = ACT0["heads"]

            def key(hd):
                bank = bank_of(k_unit(hd), a0)
                go(k_t[:, hd % 2, :], bank[0:DH, :], ACT.Identity, bias=par[0:DH, COLS["bk"] + hd:COLS["bk"] + hd + 1]).then_inc(sig.act_freed, 1)

            key(0)
            for hd in range(NH):
                wait(act, sig.to_dve, DVE0["heads"] + turn_unit_v(hd - 2) + 2 if hd >= 2 else 0)
                for t in range(NT):
                    act.wait_ge(row_max, NT * hd + t + 1)
                    go(prb[:, hd % 2, t, :], act_ps[(score_unit(hd) + t) % RING][:, :], ACT.Exp, bias=nbias[:, hd % 2, t:t + 1],
                       accum_out=rsum[:, hd % 2, t:t + 1]).then_inc(sig.act_freed, 1)
                if hd + 1 < NH:
                    key(hd + 1)
                for j in range(2):
                    bank = bank_of(turn_unit_a(hd) + j, a0)
                    wait(act, sig.to_dve, DVE0["heads"] + pv_unit(hd - 1) + 1 if hd else 0)
                    go(prb_t[:, 2 * j, :], bank[:, :], ACT.Copy).then_inc(sig.act_freed, 1)
            for c in range(0, DC, 2):
                bank = bank_of(c // 2, ACT0["xt1"])
                go(xn1_t[:, c, :], bank[:, :], ACT.Copy).then_inc(sig.act_freed, 1)
            act.wait_ge(logit_set, 1)
            go(prob[:, :, :], logit[:, :, :], ACT.Exp).then_inc(prob_exp, 1)

            def run_items(run):
                act.wait_ge(run.plan_set, 1)
                last = act.value_load(plan_i[0:1, 16:17], min_val=run.items_min - 1, max_val=run.items_max - 1)

                def x_in(a):
                    act.wait_ge(run.to_act, a + 1)
                    go(item_xt[:, 0:3, :].rearrange("p c n -> p (c n)"), act_ps[3][:, 0:HALF], ACT.Copy).then_inc(run.act_freed, 1)

                def gelus(i, a):
                    e = act.value_load(plan_i[0:1, bass.ds(i, 1)], min_val=0, max_val=run.ne - 1)
                    for u in range(run.n_turn):
                        act.wait_ge(run.to_act, a + u + 1)
                        for j in range(min(4, run.blocks - 4 * u)):
                            c = 4 * u + j
                            done = go(hid_t[:, c, :], act_ps[u][:, j * P:(j + 1) * P], ACT.Gelu,
                                      bias=par[:, bass.ds(e * run.blocks + (COLS[run.b1] + c), 1)])
                        done.then_inc(run.act_freed, 1)

                x_in(0)

                def iteration(k):
                    a = run.act_after(k)
                    x_in(a)
                    gelus(k, a + 1)

                iteration(0)
                with act.Fori(1, last) as k:
                    iteration(k)
                gelus(last, run.act_after(last))

            run_items(run0)
            sig = sig1
            for c in range(0, DC, 2):
                bank = bank_of(c // 2, ACT0["xt2"])
                go(xn2_t[:, c, :], bank[:, :], ACT.Copy).then_inc(sig.act_freed, 1)
            for t in range(NT):
                bank = bank_of(t, ACT0["h1"])
                go(h1x[:, t, 0:4, 0:GC], bank[:, :].rearrange("p (h c) -> p h c", h=4), ACT.Copy).then_inc(sig.act_freed, 1)

            def graph(g):
                b = g % 2
                act.wait_ge(g_max, g + 1)
                wait(act, g_arg, g)
                for t in range(NT):
                    last = go(arg2[:, t, :], arg[:, b, t, :], ACT.Identity, bias=gdec[:, b, 3, t:t + 1], scale=0.2)
                last.then_inc(g_low, 1)

            def graph_exp(g):
                act.wait_ge(g_arg, g + 1)
                if g:
                    act.wait_ge(sig.to_dve, gp_free(g))
                go(gp[:, :, :], arg[:, g % 2, :, :], ACT.Exp).then_inc(g_exp, 1)

            def gp_free(g):
                return DVE0["gat1"] + 1 + 7 * (g - 1) + (1 if g < GH else 0) + NT

            graph(0)
            for g in range(GH):
                graph_exp(g)
                if g + 1 < GH:
                    graph(g + 1)
            for c in range(0, GD // P, 2):
                bank = bank_of(c // 2, ACT0["o1t"])
                go(out1_t[:, c, :], bank[:, :], ACT.Relu).then_inc(sig.act_freed, 1)
            for t in range(NT):
                bank = bank_of(t, ACT0["h2"])
                go(h2x[:, t, 0:HALF], bank[:, 0:HALF], ACT.Copy).then_inc(sig.act_freed, 1)
            graph(GH)
            graph_exp(GH)
            for c in range(0, DC, 2):
                bank = bank_of(c // 2, ACT0["xt3"])
                go(xn3_t[:, c, :], bank[:, :], ACT.Copy).then_inc(sig.act_freed, 1)
            run_items(run1)

        @block.vector
        def _(dve):
            sig = sig0
            vv = nc.vector
            step = [0]

            def then(ins):
                step[0] = step[0] + 1
                ins.then_inc(dve_step, 1)

            def settle():
                dve.wait_ge(dve_step, step[0])

            def bank_of(j, before):
                dve.wait_ge(sig.to_dve, before + j + 1)
                return dve_ps[j % RING]

            def stats(source):
                for t in range(NT):
                    for half in range(2):
                        then(vv.bn_stats(bns[:, t, half, :], source[:, t, half * HALF:(half + 1) * HALF]))
                settle()
                vv.memset(root[:, 0, :], 0.0)
                for t in range(NT):
                    then(vv.bn_aggr(mv[:, t, :], bns[:, t, :, :]))
                settle()
                v_eps, y, y2 = root[:, 0, :], rstd[:, :], root[:, 1, :]
                then(vv.tensor_scalar(v_eps, mv[:, :, 1], EPS, None, ALU.add))
                settle()
                then(vv.tensor_scalar(y2.bitcast(I32), v_eps.bitcast(I32), 1, None, ALU.logical_shift_right))
                settle()
                then(vv.tensor_scalar(y.bitcast(I32), y2.bitcast(I32), -1.0, float(0x5F3759DF), ALU.mult, ALU.add))
                settle()
                for _ in range(NEWTON):
                    then(vv.tensor_tensor(y2, y, y, ALU.mult))
                    settle()
                    then(vv.scalar_tensor_tensor(y2, y2, -0.5, v_eps, ALU.mult, ALU.mult))
                    settle()
                    then(vv.scalar_tensor_tensor(y, y2, 1.5, y, ALU.add, ALU.mult))
                    settle()

            def layer_norm(source, to):
                stats(source)
                for t in range(NT):
                    vv.tensor_scalar(to[:, t, :], source[:, t, :], mv[:, t, 0:1], rstd[:, t:t + 1],
                                     ALU.subtract, ALU.mult).then_inc(normed, 1)

            vv.memset(zrow[:, :], 0.0).then_inc(zrow_set, 1)
            vv.memset(ones[:, :], 1.0).then_inc(const_set, 1)
            dve.wait_ge(in_x, 16)
            layer_norm(xres, xn)
            for c in range(1, DC, 2):
                bank = bank_of(c // 2, DVE0["xt0"])
                vv.tensor_copy(xn_t[:, c, :], bank[:, :]).then_inc(sig.dve_freed, 1)
            dve.wait_ge(in_par, 32)
            for c in range(1, DC, 2):
                bank = bank_of(c // 2, DVE0["wn"])
                vv.tensor_scalar(nodes_t[:, c, :], bank[:, :], col("bn", c), None, ALU.add).then_inc(sig.dve_freed, 1)
            for t in range(NT):
                bank = bank_of(t, DVE0["tok0"])
                vv.tensor_copy(nodes[:, t, HALF:D], bank[:, 0:HALF]).then_inc(sig.dve_freed, 1)

            dve.wait_ge(in_ends, 48)
            then(vv.tensor_copy(ends[:, :, :], ends_i[:, :, :]))
            settle()
            vv.tensor_scalar(zero[:, :], iota[:, :], 0.0, None, ALU.mult).then_inc(const_set, 1)
            with dve.Fori(0, GROUPS // 2) as i:
                for b in range(2):
                    for c in range(GROUP):
                        if c == 0:
                            dve.wait_ge(ea_high, 2 * i + b + 1)
                            vv.tensor_tensor(ea_lo[:, b, :, :], ea_raw[:, b, :, :], ea_hi[:, b, :, :].bitcast(F32),
                                             ALU.subtract).then_inc(ea_split, 1)
                        k = (2 * i + b) * GROUP + c
                        if b == 0 and c < 2:
                            dve.wait_ge(chunk_done, 1 + 2 * GROUP * i)
                        else:
                            dve.wait_ge(chunk_done, k)
                        vv.tensor_scalar(hot_d[:, c % 2, :], iota[:, :], ends[:, 1, bass.ds(k, 1)], None, ALU.is_equal)
                        vv.tensor_scalar(hot_s[:, c % 2, :], iota[:, :], ends[:, 0, bass.ds(k, 1)], None, ALU.is_equal
                                         ).then_inc(hots, 1)
            for m in range(2):
                bank = bank_of(m, DVE0["edges"])
                vv.tensor_copy(sea_t[:, m, :], bank[:, :]).then_inc(sig.dve_freed, 1)
            bank = bank_of(0, DVE0["deg"])
            vv.tensor_copy(deg[:, :], bank[:, :]).then_inc(sig.dve_freed, 1)
            dve.wait_ge(sig.dve_freed, DVE0["base"])
            then(vv.tensor_copy(cpt[:, :, :], ct[:, :, :]))
            settle()
            for t in range(NT):
                own = cpt[:, t, t * P:(t + 1) * P]
                then(vv.tensor_tensor(iota[:, t * P:(t + 1) * P], ident[:, :], deg[:, t * P:(t + 1) * P], ALU.mult))
            settle()
            for t in range(NT):
                own = cpt[:, t, t * P:(t + 1) * P]
                last = vv.tensor_tensor(own, own, iota[:, t * P:(t + 1) * P], ALU.add)
                if t < NT - 1:
                    then(last)
                else:
                    last.then_inc(cpt_set, 1)
            settle()
            for c in range(DC):
                bank = bank_of(c, DVE0["base"])
                vv.scalar_tensor_tensor(base_t[:, c, :], deg[:, :], col("be", c), bank[:, :], ALU.mult, ALU.add).then_inc(sig.dve_freed, 1)
            dve.wait_ge(sig.dve_freed, DVE0["rounds"])

            before = step[0]
            with dve.Fori(0, L) as l:
                v0 = DVE0["rounds"] + 24 * l
                step[0] = before + STATS_STEPS * l
                for c in range(DC):
                    bank = bank_of(c, v0)
                    vv.tensor_tensor(agg_t[:, c, :], bank[:, :], base_t[:, c, :], ALU.add).then_inc(sig.dve_freed, 1)
                dve.wait_ge(in_row[0], 16 * (l + 1))
                for u in range(8):
                    t, half = u // 2, u % 2
                    bank = bank_of(u, v0 + 6)
                    vv.tensor_tensor(h[:, t, half * HALF:(half + 1) * HALF], bank[:, 0:HALF],
                                     brow[:, 0, half * HALF:(half + 1) * HALF], ALU.add).then_inc(sig.dve_freed, 1)
                dve.wait_ge(sig.dve_freed, v0 + 14)
                stats(h)
                for t in range(NT):
                    vv.tensor_scalar(h[:, t, :], h[:, t, :], mv[:, t, 0:1], rstd[:, t:t + 1],
                                     ALU.subtract, ALU.mult).then_inc(normed, 1)
                for c in range(DC):
                    bank = bank_of(c, v0 + 14)
                    vv.scalar_tensor_tensor(nodes_t[:, c, :], bank[:, :], par[:, bass.ds(COLS["b2"] + DC * l + c, 1)],
                                            nodes_t[:, c, :], ALU.add, ALU.add).then_inc(sig.dve_freed, 1)
                for t in range(NT):
                    bank = bank_of(t, v0 + 20)
                    vv.tensor_copy(nodes[:, t, HALF:D], bank[:, 0:HALF]).then_inc(sig.dve_freed, 1)
            step[0] = before + STATS_STEPS * L

            dve.wait_ge(in_row[1], 16)
            for u in range(8):
                t, half = u // 2, u % 2
                bank = bank_of(u, DVE0["v"])
                vv.tensor_tensor(v[:, t, half * HALF:(half + 1) * HALF], bank[:, 0:HALF],
                                 brow[:, 1, half * HALF:(half + 1) * HALF], ALU.add).then_inc(sig.dve_freed, 1)
            dve.wait_ge(sig.act_freed, ACT0["heads"])
            dve.wait_ge(in_row[0], 16 * (L + 1))
            dve.wait_ge(sig.dve_freed, DVE0["v"])
            then(vv.tensor_tensor(xres[:, :, :], xres[:, :, :], nodes[:, :, :], ALU.add))
            settle()
            for t in range(NT):
                then(vv.tensor_tensor(xres[:, t, :], xres[:, t, :], brow[:, 0, :], ALU.add))

            a0, v0 = ACT0["heads"], DVE0["heads"]

            def query(hd):
                bank = bank_of(q_unit(hd), v0)
                vv.tensor_scalar(q_t[:, hd % 2, :], bank[0:DH, :], par[0:DH, COLS["bq"] + hd:COLS["bq"] + hd + 1],
                                 float(DH) ** -0.5, ALU.add, ALU.mult).then_inc(sig.dve_freed, 1)

            def maxima(hd):
                for t in range(NT):
                    dve.wait_ge(sig.to_act, a0 + score_unit(hd) + t + 1)
                    vv.tensor_reduce(nbias[:, hd % 2, t:t + 1], act_ps[(score_unit(hd) + t) % RING][:, :], AX_X, ALU.max,
                                     negate=True).then_inc(row_max, 1)

            def normalise(hd):
                dve.wait_ge(sig.act_freed, a0 + score_unit(hd) + NT)
                then(vv.reciprocal(rinv[:, hd % 2, :], rsum[:, hd % 2, :]))
                settle()
                for t in range(NT):
                    vv.tensor_scalar(prb[:, hd % 2, t, :], prb[:, hd % 2, t, :], rinv[:, hd % 2, t:t + 1], None,
                                     ALU.mult).then_inc(prob_set, 1)

            query(0)
            maxima(0)
            for hd in range(NH):
                normalise(hd)
                if hd + 1 < NH:
                    query(hd + 1)
                for j in range(2):
                    bank = bank_of(turn_unit_v(hd) + j, v0)
                    wait(dve, sig.to_dve, v0 + pv_unit(hd - 1) + 1 if hd else 0)
                    vv.tensor_copy(prb_t[:, 2 * j + 1, :], bank[:, :]).then_inc(sig.dve_freed, 1)
                if hd + 1 < NH:
                    maxima(hd + 1)
                bank = bank_of(pv_unit(hd), v0)
                vv.tensor_copy(attn_t[:, hd, :], bank[0:DH, :]).then_inc(sig.dve_freed, 1)

            def add_to_x(stage):
                settle()
                for u in range(8):
                    t, half = u // 2, u % 2
                    bank = bank_of(u, DVE0[stage])
                    part = xres[:, t, half * HALF:(half + 1) * HALF]
                    vv.tensor_tensor(part, bank[:, 0:HALF], part, ALU.add).then_inc(sig.dve_freed, 1)
                dve.wait_ge(sig.dve_freed, DVE0[stage] + 8)

            add_to_x("wo")
            layer_norm(xres, xn1)

            def pick_top(values, ne, to, tmp):
                shape = [P, NT, ne]
                then(vv.tensor_reduce(top4[:, :], values, AX_X, ALU.max))
                settle()
                then(vv.tensor_tensor(tmp, values, top4[:, :].unsqueeze(2).to_broadcast(shape), ALU.is_equal))
                settle()
                then(vv.tensor_tensor(tmp, tmp, prio(ne), ALU.mult))
                settle()
                then(vv.tensor_reduce(top4[:, :], tmp, AX_X, ALU.max))
                settle()
                then(vv.tensor_tensor(to, tmp, top4[:, :].unsqueeze(2).to_broadcast(shape), ALU.is_equal))
                settle()

            def prio(ne):
                return col("prio", 0, NT * 8).rearrange("p (t e) -> p t e", t=NT)[:, :, 0:ne]

            def logits(stage, ne, b0):
                bank = bank_of(0, DVE0[stage])
                vv.tensor_tensor(logit[:, :, 0:ne], bank[:, 0:NT * ne].rearrange("p (t e) -> p t e", t=NT),
                                 bg[:, b0:b0 + ne].unsqueeze(1).to_broadcast([P, NT, ne]), ALU.add).then_inc(sig.dve_freed, 1)
                dve.wait_ge(sig.dve_freed, DVE0[stage] + 1)

            def gates_turned(stage, ne):
                bank = bank_of(2, DVE0[stage])
                vv.tensor_copy(gate_t[0:ne, :], bank[0:ne, :]).then_inc(sig.dve_freed, 1)

            for c in range(1, DC, 2):
                bank = bank_of(c // 2, DVE0["xt1"])
                vv.tensor_copy(xn1_t[:, c, :], bank[:, :]).then_inc(sig.dve_freed, 1)
            dve.wait_ge(in_gate, 48)
            logits("gate0", NE0, 0)
            then(vv.tensor_reduce(top4[:, :], logit[:, :, :], AX_X, ALU.max))
            settle()
            vv.tensor_tensor(logit[:, :, :], logit[:, :, :], top4[:, :].unsqueeze(2).to_broadcast([P, NT, NE0]),
                             ALU.subtract).then_inc(logit_set, 1)
            dve.wait_ge(prob_exp, 1)
            pick_top(prob[:, :, :], NE0, pick[0][:, :, :], pick[3][:, :, :])
            then(vv.scalar_tensor_tensor(pick[1][:, :, :], pick[0][:, :, :], -2.0, prob[:, :, :], ALU.mult, ALU.add))
            settle()
            pick_top(pick[1][:, :, :], NE0, pick[2][:, :, :], pick[3][:, :, :])
            vv.tensor_tensor(sel[:, :, :], pick[2][:, :, :], pick[0][:, :, :], ALU.add).then_inc(run0.sel_set, 1)
            dve.wait_ge(run0.sel_set, 1)
            then(vv.tensor_tensor(pick[1][:, :, :], sel[:, :, :], prob[:, :, :], ALU.mult))
            settle()
            then(vv.tensor_reduce(top4[:, :], pick[1][:, :, :], AX_X, ALU.add))
            settle()
            then(vv.reciprocal(top4[:, :], top4[:, :]))
            settle()
            vv.tensor_tensor(gate[:, :, :], pick[1][:, :, :], top4[:, :].unsqueeze(2).to_broadcast([P, NT, NE0]),
                             ALU.mult).then_inc(run0.gate_set, 1)
            dve.wait_ge(run0.gate_set, 1)

            def make_plan(run, stage, choices):
                ne = run.ne
                bank = bank_of(1, DVE0[stage])
                vv.tensor_copy(count[:, :, 0:ne], bank[:, 0:(NT + 1) * ne].rearrange("p (t e) -> p t e", e=ne)).then_inc(sig.dve_freed, 1)
                dve.wait_ge(sig.dve_freed, DVE0[stage] + 2)
                total, n, end, begin = count[:, NT, 0:ne], chunks[:, 0, 0:ne], chunks[:, 1, 0:ne], chunks[:, 2, 0:ne]
                then(vv.tensor_scalar(n, total, 0.0, None, ALU.is_gt))
                for k in range(1, NT):
                    settle()
                    then(vv.scalar_tensor_tensor(n, total, float(P * k), n, ALU.is_gt, ALU.add))
                settle()
                tri8 = col("tri8", 0, 64).rearrange("p (a b) -> p a b", a=8)[:, 0:ne, 0:ne]
                then(vv.tensor_tensor(low8[:, 0:ne, 0:ne], n.unsqueeze(1).to_broadcast([P, ne, ne]), tri8, ALU.mult))
                settle()
                then(vv.tensor_reduce(end, low8[:, 0:ne, 0:ne], AX_X, ALU.add))
                settle()
                then(vv.tensor_tensor(begin, end, n, ALU.subtract))
                iota16 = col("iota16", 0, 16)
                then(vv.tensor_tensor(low16[:, :, 0:ne], iota16.unsqueeze(2).to_broadcast([P, 16, ne]),
                                      end.unsqueeze(1).to_broadcast([P, 16, ne]), ALU.is_ge))
                settle()
                then(vv.tensor_reduce(plan[:, 0:16], low16[:, :, 0:ne], AX_X, ALU.add))
                then(vv.tensor_scalar(plan[:, 16:17], chunks[:, 1, ne - 1:ne], -1.0, None, ALU.add))
                then(vv.tensor_scalar(begin, begin, float(P), None, ALU.mult))
                settle()
                then(vv.tensor_tensor(slot_of[:, :, 0:ne], count[:, 0:NT, 0:ne], begin.unsqueeze(1).to_broadcast([P, NT, ne]), ALU.add))
                settle()
                for j, choice in enumerate(choices):
                    then(vv.tensor_tensor(pick[3][:, :, 0:ne], slot_of[:, :, 0:ne], choice[:, :, 0:ne], ALU.mult))
                    settle()
                    then(vv.tensor_reduce(pos[:, j, :], pick[3][:, :, 0:ne], AX_X, ALU.add))
                    settle()
                n = len(choices)
                then(vv.tensor_copy(pos_i[:, 0:n, :], pos[:, 0:n, :]))
                settle()
                vv.tensor_copy(plan_i[:, :], plan[:, :]).then_inc(run.plan_set, 1)
                dve.wait_ge(run.plan_set, 1)

            make_plan(run0, "gate0", (pick[0], pick[2]))
            for j, choice in enumerate((pick[0], pick[2])):
                then(vv.tensor_tensor(pick[3][:, :, :], gate[:, :, :], choice[:, :, :], ALU.mult))
                settle()
                then(vv.tensor_reduce(share[:, j, :], pick[3][:, :, :], AX_X, ALU.add))
                settle()
            gates_turned("gate0", NE0)
            add_to_x("bias0")

            def run_items(run):
                last = dve.value_load(plan_i[0:1, 16:17], min_val=run.items_min - 1, max_val=run.items_max - 1)

                def x_in(v):
                    dve.wait_ge(run.to_dve, v + 1)
                    vv.tensor_copy(item_xt[:, 3:6, :].rearrange("p c n -> p (c n)"), dve_ps[2][:, 0:HALF]).then_inc(run.dve_freed, 1)

                def hidden(v):
                    for u in range(run.n_up):
                        dve.wait_ge(run.to_dve, v + 2 + u)
                        vv.tensor_copy(hid[:, u * HALF:(u + 1) * HALF], dve_ps[(3 + u) % 4][:, 0:HALF]).then_inc(run.dve_freed, 1)

                def result(v, stored):
                    wait(dve, run.y_out, 16 * stored)
                    for half in range(2):
                        dve.wait_ge(run.to_dve, v + 1 + half)
                        vv.tensor_copy(item_y[:, half * HALF:(half + 1) * HALF],
                                       dve_ps[run.down_banks[half]][:, 0:HALF]).then_inc(run.dve_freed, 1)

                x_in(0)
                hidden(0)

                def iteration(k):
                    v = run.dve_after(k)
                    x_in(v)
                    hidden(v)
                    result(v + 1 + run.n_up, k)

                iteration(0)
                with dve.Fori(1, last) as k:
                    iteration(k)
                result(run.dve_after(last), last)

            run_items(run0)
            for t in range(NT):
                dve.wait_ge(run0.gathered[t], 32)
                for j in range(2):
                    then(vv.scalar_tensor_tensor(xres[:, t, :], got[:, t, j, :], share[:, j, t:t + 1], xres[:, t, :], ALU.mult, ALU.add))
                    settle()
            sig = sig1
            layer_norm(xres, xn2)
            for c in range(1, DC, 2):
                bank = bank_of(c // 2, DVE0["xt2"])
                vv.tensor_copy(xn2_t[:, c, :], bank[:, :]).then_inc(sig.dve_freed, 1)
            then(vv.memset(h1x[:, :, :, GC:GC + 2], 1.0))
            for t in range(NT):
                bank = bank_of(t, DVE0["h1"])
                vv.tensor_copy(h1x[:, t, 4:8, 0:GC], bank[:, :].rearrange("p (h c) -> p h c", h=4)).then_inc(sig.dve_freed, 1)
            for t in range(NT):
                bank = bank_of(t, DVE0["mask"])
                vv.tensor_scalar(mask[:, t, :], bank[:, :], 0.0, NONE, ALU.is_equal, ALU.mult).then_inc(sig.dve_freed, 1)
            dve.wait_ge(sig.act_freed, ACT0["mask"])
            dve.wait_ge(sig.dve_freed, DVE0["mask"])
            dve.wait_ge(in_att1, 16)
            for which in range(2):
                for t in range(NT):
                    settle()
                    then(vv.tensor_tensor(scr[:, :].rearrange("p (h c) -> p h c", h=GH), h1x[:, t, :, 0:GC],
                                          att1[:, which, :].rearrange("p (h c) -> p h c", h=GH), ALU.mult))
                    settle()
                    last = vv.tensor_reduce(att[:, which, t, :], scr[:, :].rearrange("p (h c) -> p h c", h=GH), AX_X, ALU.add)
                    if which == 1 and t == NT - 1:
                        last.then_inc(att_set, 1)
                    else:
                        then(last)
            settle()
            dve.wait_ge(att_set, 1)

            def graph_front(g, unit, v0, a_dst):
                b = g % 2
                bank = bank_of(unit, v0)
                wait(dve, g_exp, g - 1)
                for t in range(NT):
                    last = vv.tensor_tensor_reduce(out=arg[:, b, t, :], in0=bank[:, :], in1=mask[:, t, :], scale=1.0, scalar=NONE,
                                                   op0=ALU.add, op1=ALU.max, accum_out=gmax[:, b, t:t + 1])
                    if t < NT - 1:
                        then(last)
                last.then_inc(sig.dve_freed, 1)
                dve.wait_ge(sig.dve_freed, v0 + unit + 1)
                settle()
                then(vv.scalar_tensor_tensor(gdec[:, b, 0, :], gmax[:, b, :], FLOOR, a_dst, ALU.max, ALU.add))
                settle()
                then(vv.scalar_tensor_tensor(gdec[:, b, 1, :], gdec[:, b, 0, :], 0.2, gdec[:, b, 0, :], ALU.mult, ALU.max))
                settle()
                then(vv.tensor_tensor(gdec[:, b, 2, :], a_dst, gdec[:, b, 1, :], ALU.subtract))
                vv.scalar_tensor_tensor(gdec[:, b, 3, :], a_dst, 0.2, gdec[:, b, 1, :], ALU.mult, ALU.subtract).then_inc(g_max, 1)

            def graph_arg(g):
                b = g % 2
                dve.wait_ge(g_low, g + 1)
                settle()
                for t in range(NT):
                    last = vv.scalar_tensor_tensor(arg[:, b, t, :], arg[:, b, t, :], gdec[:, b, 2, t:t + 1], arg2[:, t, :],
                                                   ALU.add, ALU.max)
                    if t < NT - 1:
                        then(last)
                last.then_inc(g_arg, 1)

            def graph_turned(unit, v0, used):
                for m in range(NT):
                    bank = bank_of(unit + m, v0)
                    wait(dve, sig.to_dve, used)
                    vv.tensor_tensor(gp_t[:, m, :], bank[:, :], ct[:, m, :], ALU.mult).then_inc(sig.dve_freed, 1)

            v0 = DVE0["gat1"]
            dve.wait_ge(in_gb, 32)
            graph_front(0, 0, v0, att[:, 1, :, 0])
            graph_arg(0)
            unit = 1
            for hd in range(GH):
                if hd + 1 < GH:
                    graph_front(hd + 1, unit, v0, att[:, 1, :, hd + 1])
                    unit += 1
                graph_turned(unit, v0, v0 + unit - (1 if hd + 1 < GH else 0) if hd else 0)
                unit += NT
                if hd + 1 < GH:
                    graph_arg(hd + 1)
                for pair in range(2):
                    bank = bank_of(unit, v0)
                    w = GC + 2
                    den = bank[:, 0:2 * w].rearrange("p (t c) -> p t c", t=2)[:, :, GC]
                    then(vv.tensor_scalar(rinv[:, 0, 2 * pair:2 * pair + 2], den, DEN_EPS, None, ALU.add))
                    settle()
                    then(vv.reciprocal(rinv[:, 1, 2 * pair:2 * pair + 2], rinv[:, 0, 2 * pair:2 * pair + 2]))
                    settle()
                    for j in range(2):
                        t = 2 * pair + j
                        last = vv.scalar_tensor_tensor(out1[:, t, hd * GC:(hd + 1) * GC], bank[:, j * w:j * w + GC],
                                                       rinv[:, 1, t:t + 1], g_b1[:, hd * GC:(hd + 1) * GC], ALU.mult, ALU.add)
                        if j == 0:
                            then(last)
                    last.then_inc(sig.dve_freed, 1)
                    unit += 1
            for t in range(NT):
                then(vv.tensor_tensor(xres[:, t, :], xres[:, t, :], g_b2[:, :], ALU.add))
            for c in range(1, GD // P, 2):
                bank = bank_of(c // 2, DVE0["o1t"])
                vv.tensor_scalar(out1_t[:, c, :], bank[:, :], 0.0, None, ALU.max).then_inc(sig.dve_freed, 1)
            dve.wait_ge(sig.to_dve, DVE0["h2"])
            then(vv.memset(h2x[:, :, D:D + 2], 1.0))
            for t in range(NT):
                bank = bank_of(t, DVE0["h2"])
                vv.tensor_copy(h2x[:, t, HALF:D], bank[:, 0:HALF]).then_inc(sig.dve_freed, 1)
            dve.wait_ge(in_row[0], 16 * (L + 2))
            dve.wait_ge(sig.act_freed, ACT0["xt3"])
            dve.wait_ge(sig.dve_freed, DVE0["gat2"])
            for which in range(2):
                for t in range(NT):
                    settle()
                    last = vv.tensor_tensor_reduce(out=gp_t[:, 0:2, :].rearrange("p a n -> p (a n)")[:, 0:D], in0=h2x[:, t, 0:D],
                                                   in1=brow[:, which, :], scale=1.0, scalar=0.0, op0=ALU.mult, op1=ALU.add,
                                                   accum_out=att[:, which, t, 0:1])
                    if which == 1 and t == NT - 1:
                        last.then_inc(att_set, 1)
                    else:
                        then(last)
            settle()
            dve.wait_ge(att_set, 2)
            v0 = DVE0["gat2"]
            graph_front(GH, 0, v0, att[:, 1, :, 0])
            graph_arg(GH)
            graph_turned(1, v0, 0)
            for u in range(8):
                t, half = u // 2, 1 - u % 2
                bank = bank_of(5 + u, v0)
                if half == 1:
                    then(vv.tensor_scalar(rinv[:, 0, t:t + 1], bank[:, HALF:HALF + 1], DEN_EPS, None, ALU.add))
                    settle()
                    then(vv.reciprocal(rinv[:, 1, t:t + 1], rinv[:, 0, t:t + 1]))
                    settle()
                part = xres[:, t, half * HALF:(half + 1) * HALF]
                vv.scalar_tensor_tensor(part, bank[:, 0:HALF], rinv[:, 1, t:t + 1], part, ALU.mult, ALU.add).then_inc(sig.dve_freed, 1)
            dve.wait_ge(sig.dve_freed, DVE0["xt3"])
            layer_norm(xres, xn3)
            for c in range(1, DC, 2):
                bank = bank_of(c // 2, DVE0["xt3"])
                vv.tensor_copy(xn3_t[:, c, :], bank[:, :]).then_inc(sig.dve_freed, 1)
            logits("gate1", NE1, 8)
            pick_top(logit[:, :, 0:NE1], NE1, pick[0][:, :, 0:NE1], pick[3][:, :, 0:NE1])
            vv.tensor_copy(sel[:, :, 0:NE1], pick[0][:, :, 0:NE1]).then_inc(run1.sel_set, 1)
            vv.tensor_copy(gate[:, :, 0:NE1], pick[0][:, :, 0:NE1]).then_inc(run1.gate_set, 1)
            dve.wait_ge(run1.gate_set, 1)
            make_plan(run1, "gate1", (pick[0],))
            gates_turned("gate1", NE1)
            add_to_x("bias1")
            run_items(run1)
            for t in range(NT):
                dve.wait_ge(run1.gathered[t], 16)
                vv.tensor_tensor(xres[:, t, :], xres[:, t, :], got[:, t, 0, :], ALU.add).then_inc(final, 1)

        @block.gpsimd
        def _(pool):
            pool.wait_ge(zrow_set, 1)
            for run in (run0, run1):
                for table in (run.scattered, run.results):
                    pool.dma_start(table.rearrange("(i p) d -> p i d", p=P),
                                   zrow[:, :].unsqueeze(1).to_broadcast([P, run.items_max, D])).then_inc(run.filled, 16)

            def run_items(run, nodes_in, normed_by):
                pool.wait_ge(run.filled, 32)
                pool.wait_ge(normed, normed_by)
                pool.wait_ge(run.plan_set, 1)
                last = pool.value_load(plan_i[0:1, 16:17], min_val=run.items_min - 1, max_val=run.items_max - 1)
                for t in range(NT):
                    for j in range(run.picks):
                        pool.indirect_dma_start(out=run.scattered, out_offset=bass.IndirectOffsetOnAxis(pos_i[:, j, t:t + 1], 0),
                                                in_=nodes_in[:, t, :], in_offset=None).then_inc(run.scattered_in, 16)

                def store(i, v):
                    pool.wait_ge(run.dve_freed, v)
                    pool.dma_start(run.results[bass.ds(i * P, P), :], item_y[:, :]).then_inc(run.y_out, 16)

                store(0, run.dve_after(1))
                with pool.Fori(1, last) as k:
                    store(k, run.dve_after(k + 1))
                store(last, run.dve_after(last) + 2)
                pool.wait_ge(run.y_out, 16 * last + 16)
                pool.sem_inc(stood, 1)
                for t in range(NT):
                    for j in range(run.picks):
                        pool.indirect_dma_start(out=got[:, t, j, :], out_offset=None, in_=run.results,
                                                in_offset=bass.IndirectOffsetOnAxis(pos_i[:, j, t:t + 1], 0)
                                                ).then_inc(run.gathered[t], 16)

            run_items(run0, xn1, NT * (L + 2))
            run_items(run1, xn3, NT * (L + 4))


_OUT = ((N, D), "float32")


def kernel(**inputs):
    import numpy as np
    import concourse.bacc as bacc
    from concourse.bass_utils import run_bass_kernel_spmd

    a = {k: np.asarray(w) for k, w in inputs.items()}
    g0, e0, g1, e1 = "L0_gnn_", "L0_ffn_", "L1_gnn_", "L1_ffn_"

    def blocks(vec):
        return vec.reshape(-1, P).T

    def heads(vec):
        m = np.zeros((P, NH), np.float32)
        m[0:DH] = vec.reshape(NH, DH).T
        return m

    bqkv = a[g0 + "bqkv"]
    prio = np.tile(np.arange(8, 0, -1, dtype=np.float32), (P, NT))
    cols = np.concatenate([
        blocks(a[g0 + "bn"]), blocks(a[g0 + "be"]), blocks(a[g0 + "ln_g"]), blocks(a[g0 + "ln_b"]),
        blocks(a[g0 + "b2"]), heads(bqkv[0:D]), heads(bqkv[D:2 * D]), blocks(a[e0 + "b1"]), blocks(a[e1 + "b1"]), prio,
        np.tile(np.tril(np.ones((8, 8), np.float32)).reshape(-1), (P, 1)), np.tile(np.arange(16, dtype=np.float32), (P, 1))], axis=1)
    rows = np.concatenate([w.reshape(-1) for w in (
        a[g0 + "b1"], bqkv[2 * D:], a[g0 + "bo"], a[g1 + "b1"], a[g1 + "att_src1"], a[g1 + "att_dst1"],
        a[g1 + "b2"], a[g1 + "att_src2"], a[g1 + "att_dst2"], a[e0 + "bg"], a[e1 + "bg"])])
    arrays = {
        "x": a["x"], "src": a["src"].reshape(E // P, P).T, "dst": a["dst"].reshape(E // P, P).T,
        "edge": a["edge_attr_256"], "cols": cols, "rows": rows,
        "ident_d": np.eye(P, dtype=np.float32), "iota_d": np.arange(N, dtype=np.float32),
        "tri_d": np.triu(np.ones((P, P), np.float32), 1),
        "wn": a[g0 + "Wn"].T, "we": a[g0 + "We"].T, "w1": a[g0 + "W1"].transpose(0, 2, 1),
        "w2": a[g0 + "W2"].transpose(0, 2, 1), "wqkv": a[g0 + "Wqkv"].T, "wo": a[g0 + "Wo"].T,
        "wg0": a[e0 + "Wg"], "e0w1": a[e0 + "W1"], "e0w2": a[e0 + "W2"], "e0b2": a[e0 + "b2"],
        "gw1": a[g1 + "W1"].T, "gw2": a[g1 + "W2"].T,
        "wg1": a[e1 + "Wg"], "e1w1": a[e1 + "W1"], "e1w2": a[e1 + "W2"], "e1b2": a[e1 + "b2"],
    }
    nc = bacc.Bacc("TRN2", target_bir_lowering=False, num_devices=1)
    args, feed = [], {}
    for name, w in arrays.items():
        w = np.ascontiguousarray(w)
        feed[f"in_{name}"] = w
        args.append(nc.dram_tensor(f"in_{name}", w.shape, mybir.dt.from_np(w.dtype), kind="ExternalInput").ap())
    for name, slots in (("xs0", 15 * P), ("ys0", 15 * P), ("xs1", 7 * P), ("ys1", 7 * P)):
        args.append(nc.dram_tensor(name, (slots, D), F32, kind="Internal").ap())
    args.append(nc.dram_tensor("out_0", _OUT[0], F32, kind="ExternalOutput").ap())
    build(nc, *args)
    r = run_bass_kernel_spmd(nc, [feed], core_ids=[0])
    return r.results[0]["out_0"]
```

```python
from contextlib import ExitStack

import concourse.bass as bass
from concourse import mybir

P = 128
F32 = mybir.dt.float32
F32R = mybir.dt.float32r
I32 = mybir.dt.int32
ALU = mybir.AluOpType
ACT = mybir.ActivationFunctionType
AX_X = mybir.AxisListType.X

N = 512
NT = N // P
D = 768
DC = D // P
HALF = D // 2
DE = 256
E = 8192
L = 3
NH, DH = 8, 96
NE0, H0 = 8, 1536
NE1, H1 = 4, 384
GH, GC = 8, 128
GD = GH * GC
EPS = 1e-5
DEN_EPS = 1e-16
NONE = -1e30
FLOOR = -1e25

NEWTON = 3

RING = 4
NORM_STEPS = 3 * NT + 2 * (3 + 3 * NEWTON)
GROUP = 8
GROUPS = E // P // GROUP
OPENED = 9

STAGES = [
    ("xt0", 3, 3), ("wn", 3, 3), ("tok0", 4, 4), ("edges", 4, 2), ("deg", 0, 1), ("base", 0, DC),
    ("rounds", L * 10, L * 24), ("v", 0, 8), ("heads", NH * 7, NH * 4), ("wo", 0, 8),
    ("xt1", 3, 3), ("gate0", 0, 3), ("bias0", 0, 8),
    ("xt2", 3, 3), ("h1", 4, 4), ("mask", 0, 4), ("gat1", 0, GH * 3), ("o1t", 4, 4), ("h2", 4, 4),
    ("gat2", 0, 9), ("xt3", 3, 3), ("gate1", 0, 3), ("bias1", 0, 8),
]
ACT0, DVE0 = {}, {}
_a = _v = 0
for _name, _da, _dv in STAGES:
    if _name == "xt2":
        _a = _v = 0
    ACT0[_name], DVE0[_name] = _a, _v
    _a, _v = _a + _da, _v + _dv

COLS = {}
_c = 0
for _name, _w in [("bn", DC), ("be", DC), ("ln_g", L * DC), ("ln_b", L * DC), ("b2", L * DC),
                  ("bq", NH), ("bk", NH), ("e0b1", NE0 * H0 // P), ("e1b1", NE1 * H1 // P),
                  ("prio", NT * 8), ("tri8", 64), ("iota16", 16)]:
    COLS[_name] = _c
    _c += _w
NCOLS = _c
ROWS = {}
_c = 0
for _name, _w in [("b1", L * D), ("bv", D), ("bo", D), ("g_b1", GD), ("g_src1", GD), ("g_dst1", GD),
                  ("g_b2", D), ("g_src2", D), ("g_dst2", D), ("bg0", NE0), ("bg1", NE1)]:
    ROWS[_name] = _c
    _c += _w
NROWS = _c


def wait(eng, sem, value):
    if not isinstance(value, int) or value > 0:
        eng.wait_ge(sem, value)


def build(nc, x, src, dst, edge, cols, rows, ident_d, iota_d, tri_d, wn, we, w1, w2, wqkv, wo, wg0, e0w1,
          e0w2, e0b2, gw1, gw2, wg1, e1w1, e1w2, e1b2, xs0, ys0, xs1, ys1, out):
    ctx = ExitStack()
    with ctx:
        start = (nc.sbuf_base + 63) // 64 * 64
        top = [0]

        def place(name, shape, dt, at=None):
            size = 1
            for s in shape[1:]:
                size *= s
            if at is None:
                at = top[0]
                top[0] += (size + 7) // 8 * 8
            return nc.alloc_sbuf_tensor_at(name, shape, dt, offset=start + 4 * at)

        def sem(name):
            return ctx.enter_context(nc.semaphore(name))

        slot = [place(f"slot{s}", [P, 4608], F32) for s in range(4)]
        part_slot = [place(f"part_slot{s}", [P, 4608], F32R, 4608 * s) for s in range(4)]
        ident = place("ident", [P, P], F32)
        ones = place("ones", [P, P], F32)
        tri = place("tri", [P, P], F32)
        par = place("par", [P, NCOLS], F32)
        xres_at = top[0]
        xres = place("xres", [P, NT, D], F32)
        ct = place("ct", [P, NT, N], F32)
        cpt_at = top[0]
        cpt = place("cpt", [P, NT, N], F32)
        mask = place("mask", [P, NT, N], F32, cpt_at)
        bc_at = top[0]
        brow = place("brow", [P, 2, D], F32)
        bns = place("bns", [P, NT, 2, 6], F32)
        mv = place("mv", [P, NT, 2], F32)
        rstd = place("rstd", [P, NT], F32)
        root = place("root", [P, 2, NT], F32)
        nbias = place("nbias", [P, 2, NT], F32)
        rsum = place("rsum", [P, 2, NT], F32)
        rinv = place("rinv", [P, 2, NT], F32)
        logit = place("logit", [P, NT, 8], F32)
        prob = place("prob", [P, NT, 8], F32)
        pick = [place(f"pick{i}", [P, NT, 8], F32) for i in range(4)]
        top4 = place("top4", [P, NT], F32)
        gate = place("gate", [P, NT, 8], F32)
        gate_t = place("gate_t", [8, N], F32)
        wg = place("wg", [P, DC, 8], F32)
        bg = place("bg", [P, 12], F32)
        att = place("att", [P, 2, NT, GH], F32)
        gmax = place("gmax", [P, 2, NT], F32)
        gdec = place("gdec", [P, 2, 4, NT], F32)
        sel = place("sel", [P, NT, 8], F32)
        count = place("count", [P, NT + 1, 8], F32)
        chunks = place("chunks", [P, 3, 8], F32)
        low8 = place("low8", [P, 8, 8], F32)
        low16 = place("low16", [P, 16, 8], F32)
        slot_of = place("slot_of", [P, NT, 8], F32)
        pos = place("pos", [P, 2, NT], F32)
        pos_i = place("pos_i", [P, 2, NT], I32)
        share = place("share", [P, 2, NT], F32)
        plan = place("plan", [P, 17], F32)
        plan_i = place("plan_i", [P, 17], I32)
        zrow = place("zrow", [P, HALF], F32)
        slot_iota = place("slot_iota", [P, P], F32)
        pos_last = place("pos_last", [P, 2, NT], F32)
        area = top[0]

        def over(name, shape, at, dt=F32):
            return place(name, shape, dt, area + at)

        nodes = over("nodes", [P, NT, D], 0)
        nodes_t = over("nodes_t", [P, DC, N], 3072)
        xn = over("xn", [P, NT, D], 0)
        xn_t = over("xn_t", [P, DC, N], 6144)
        ea_raw = over("ea_raw", [P, 2, GROUP, DE], 14336)
        ea_hi = over("ea_hi", [P, 2, GROUP, DE], 10240, F32R)
        ea_lo = over("ea_lo", [P, 2, GROUP, DE], 6144, F32R)
        hot_d = over("hot_d", [P, 2, N], 18432, F32R)
        hot_s = over("hot_s", [P, 2, N], 19456, F32R)
        iota = over("iota", [P, N], 20480)
        ends_i = over("ends_i", [P, 2, E // P], 20992, I32)
        ends = over("ends", [P, 2, E // P], 21120)
        sea_t = over("sea_t", [P, DE // P, N], 21248)
        zero = over("zero", [P, N], 22272, F32R)
        deg = over("deg", [P, N], 18432)
        agg_t = over("agg_t", [P, DC, N], 6144)
        base_t = over("base_t", [P, DC, N], 9216)
        h = over("h", [P, NT, D], 12288)
        h_t = over("h_t", [P, DC, N], 18432)
        h_hi = over("h_hi", [P, DC, N], 15360, F32R)
        nt_hi = over("nt_hi", [P, DC, N], 15360, F32R)
        nt_lo = over("nt_lo", [P, DC, N], 18432, F32R)
        w1_hi = [place(f"w1_hi{k}", [P, D], F32R, at) for k, at in
                 enumerate([xres_at + D * t for t in range(NT)] + [area + 21504, bc_at + D])]
        agg_hi = over("agg_hi", [P, DC, N], 0, F32R)
        agg_lo = over("agg_lo", [P, DC, N], 6144, F32R)
        h_lo = over("h_lo", [P, DC, N], 18432, F32R)
        v = over("v", [P, NT, D], 12288)
        attn_t = over("attn_t", [DH, NH, N], 6144)
        q_t = over("q_t", [DH, 2, N], 0)
        k_t = over("k_t", [DH, 2, N], 1024)
        na_hi = [place(f"na_hi{c}", [P, N], F32R, at) for c, at in
                 enumerate([area + 10240 + N * c for c in range(4)] + [cpt_at, cpt_at + N])]
        na_lo = over("na_lo", [P, DC, N], 3072, F32R)
        wv_hi = over("wv_hi", [P, DC * D], 15360, F32R)
        wq_hi = [place(f"wq_hi{k}", [P, D], F32R, at) for k, at in
                 enumerate([3072, 3072 + D, cpt_at + 2 * N, area + 21504, area + 2048, bc_at])]
        prb = over("prb", [P, 2, NT, N], 15360)
        prb_t = over("prb_t", [P, NT, N], 19456)
        xn1 = over("xn1", [P, NT, D], 0)
        xn1_t = over("xn1_t", [P, DC, N], 3072)
        e0b2_s = place("e0b2_s", [NE0, D], F32, cpt_at)
        item_x = over("item_x", [P, D], 6144)
        item_xt = over("item_xt", [P, DC, P], 6912)
        hid = over("hid", [P, H0], 7680)
        hid_t = over("hid_t", [P, H0 // P, P], 9216)
        item_y = over("item_y", [P, D], 10752)
        got = over("got", [P, NT, 2, D], 12288)
        first_sel = over("first_sel", [P, NT, P], 18432)
        last_sel = over("last_sel", [P, NT, P], 18944)
        last_tmp = over("last_tmp", [P, NT, P], 19456)
        last_t = over("last_t", [P, N], 19968)
        x_hi = over("x_hi", [P, DC * P], 6912, F32R)
        x_lo = over("x_lo", [P, DC * P], 11520, F32R)
        up_hi = [[place(f"up_hi{j}_{k}", [P, D], F32R, at) for k, at in enumerate(places)] for j, places in enumerate(
            ([area + 12288 + D * k for k in range(6)],
             [area + 16896, area + 16896 + D] + [area + 20480 + D * k for k in range(3)] + [cpt_at + 1024]))]
        xn2 = over("xn2", [P, NT, D], 0)
        xn2_hi = over("xn2_hi", [P, DC, N], 3072, F32R)
        xn2_lo = over("xn2_lo", [P, DC, N], 14400, F32R)
        gw1_hi = [place(f"gw1_hi{i}", [P, N], F32R, at) for i, at in enumerate(
            [4608 * s + 3072 + N * j for s in range(2) for j in range(3)] + [cpt_at + N * j for j in range(4)]
            + [area + 20480, area + 20480 + N])]
        h1x = over("h1x", [P, NT, GH, GC + 2], 6144)
        out1 = over("out1", [P, NT, GD], 0)
        g_b1 = over("g_b1", [P, GD], 4096)
        g_b2 = over("g_b2", [P, D], 5120)
        h2x = over("h2x", [P, NT, D + 2], 6144)
        att1 = over("att1", [P, 2, GD], 10304)
        scr = over("scr", [P, 2, GD], 12352)
        branch = over("branch", [P, 2, 2, NT, N], 10304)
        gp_t = over("gp_t", [P, 2, NT, N], 18496)
        unread = [place(f"unread{t}", [P, N], F32, at) for t, at in
                  enumerate([3072, 3072 + N, 3072 + 2 * N, 4608 + 3072])]
        unread_sum = [place(f"unread_sum{j}", [P, D], F32, 3072 + D * j) for j in range(2)]
        neg_src = over("neg_src", [P, 2, NT, GH], 22592)
        out1_hi = over("out1_hi", [P, GD // P, N], 10304, F32R)
        out1_lo = over("out1_lo", [P, GD // P, N], 14400, F32R)
        xn3 = over("xn3", [P, NT, D], 0)
        xn3_t = over("xn3_t", [P, DC, N], 3072)
        e1b2_s = place("e1b2_s", [NE1, D], F32, cpt_at)

        act_ps = [ctx.enter_context(nc.psum_tensor(f"act_ps{i}", [P, N], F32)) for i in range(RING)]
        dve_ps = [ctx.enter_context(nc.psum_tensor(f"dve_ps{i}", [P, N], F32)) for i in range(RING)]

        class Signals:
            def __init__(self, part):
                self.to_act = sem(f"to_act_{part}")
                self.to_dve = sem(f"to_dve_{part}")
                self.act_freed = sem(f"act_freed_{part}")
                self.dve_freed = sem(f"dve_freed_{part}")

        class Run(Signals):

            def __init__(self, layer, ne, hidden, picks, up, down, scattered, results, b1, up_slots, down_slots, down_banks):
                super().__init__(f"run{layer}")
                self.layer, self.ne, self.picks, self.up, self.down = layer, ne, picks, up, down
                self.scattered, self.results, self.b1 = scattered, results, b1
                self.up_slots, self.down_slots, self.down_banks = up_slots, down_slots, down_banks
                self.blocks = hidden // P
                self.n_up = hidden // HALF
                self.n_turn = -(-self.blocks // 4)
                self.items_min = picks * N // P
                self.items_max = self.items_min + ne - 1
                self.w_in = {s: sem(f"w_in{layer}_{s}") for s in up_slots + down_slots}
                self.x_in = sem(f"x_in{layer}")
                self.y_out = sem(f"y_out{layer}")
                self.filled = sem(f"filled{layer}")
                self.scattered_in = sem(f"scattered{layer}")
                self.gathered = [sem(f"gathered{layer}_{t}") for t in range(NT)]
                self.sel_set = sem(f"sel_set{layer}")
                self.plan_set = sem(f"plan_set{layer}")
                self.gate_set = sem(f"gate_set{layer}")
                self.first_set = sem(f"first_set{layer}")
                self.last_set = sem(f"last_set{layer}")

            def act_after(self, k):
                return k * (1 + self.n_turn) + 1

            def dve_after(self, k):
                return k * (1 + self.n_up + 2) + (1 + self.n_up)

        sig0, sig1 = Signals("a"), Signals("b")
        run0 = Run(0, NE0, H0, 2, e0w1, e0w2, xs0, ys0, "e0b1", (2, 3), (0, 1), (3, 0))
        run1 = Run(1, NE1, H1, 1, e1w1, e1w2, xs1, ys1, "e1b1", (2,), (0,), (0, 1))
        slot_in = [sem(f"slot_in{s}") for s in range(4)]
        in_x = [sem(f"in_x{t}") for t in range(NT)]
        in_par = sem("in_par")
        in_ends = sem("in_ends")
        in_edge = [sem("in_edge0"), sem("in_edge1")]
        in_row = [sem("in_row0"), sem("in_row1")]
        in_gate = sem("in_gate")
        in_eb2 = sem("in_eb2")
        in_tri = sem("in_tri")
        stood = sem("stood")
        in_att1 = sem("in_att1")
        in_gb = sem("in_gb")
        in_gate1 = sem("in_gate1")
        out_done = sem("out_done")
        final = sem("final")
        dve_step = sem("dve_step")
        normed = sem("normed")
        const_set = sem("const_set")
        zrow_set = sem("zrow_set")
        ea_split = sem("ea_split")
        ea_high = sem("ea_high")
        hots = sem("hots")
        chunk_done = sem("chunk_done")
        cpt_set = sem("cpt_set")
        w_high = sem("w_high")
        w_low = sem("w_low")
        nt_high = sem("nt_high")
        nt_low = sem("nt_low")
        turned_high = sem("turned_high")
        x_high = sem("x_high")
        x_low = sem("x_low")
        up_high = [sem("up_high0"), sem("up_high1")]
        up_low = [sem("up_low0"), sem("up_low1")]
        agg_high = sem("agg_high")
        agg_low = sem("agg_low")
        x_added = sem("x_added")
        in_x_again = sem("in_x_again")
        h_low = sem("h_low")
        row_max = sem("row_max")
        prob_set = sem("prob_set")
        logit_set = sem("logit_set")
        prob_exp = sem("prob_exp")
        att_set = sem("att_set")
        g_dec = sem("g_dec")
        g_rows = sem("g_rows")
        g_low = sem("g_low")
        g_arg = sem("g_arg")
        g_exp = sem("g_exp")
        g_weight = sem("g_weight")

        block = ctx.enter_context(nc.Block())

        def bview(name, width):
            return rows[ROWS[name]:ROWS[name] + width].partition_broadcast(P)

        def col(name, i, n=1):
            return par[:, COLS[name] + i:COLS[name] + i + n]

        def k_unit(hd):
            return 0 if hd == 0 else 1 + 7 * (hd - 1) + 4

        def score_unit(hd):
            return 1 + 7 * hd

        def turn_unit_a(hd):
            return 1 + 7 * hd + 4 + (1 if hd < NH - 1 else 0)

        def q_unit(hd):
            return 0 if hd == 0 else 1 + 4 * (hd - 1)

        def turn_unit_v(hd):
            return 1 + 4 * hd + (1 if hd < NH - 1 else 0)

        def pv_unit(hd):
            return turn_unit_v(hd) + 2

        def row_unit(hd):
            return hd if hd < 3 else 3 + 3 * (hd - 3)

        def out_unit(hd):
            return 4 + 3 * hd if hd + 3 < GH else 3 + 3 * (GH - 3) + 2 * (hd - (GH - 3))

        @block.sync
        def _(sp):
            sig = sig0
            def load(s, dst, source):
                sp.dma_start(dst, source).then_inc(slot_in[s], 16)

            def kview(ap):
                return ap.rearrange("(k p) n -> p k n", p=P)

            def sview(s, k, n):
                return slot[s][:, 0:k * n].rearrange("p (k n) -> p k n", k=k)

            def load_up(run, expert, free):
                w = run.up[bass.ds(expert, 1), :, :].rearrange("a k n -> (a k) n")
                width = run.blocks * P // len(run.up_slots)
                for j, s in enumerate(run.up_slots):
                    wait(sp, run.to_dve, free[j])
                    sp.dma_start(sview(s, DC, width), kview(w[:, j * width:(j + 1) * width])).then_inc(run.w_in[s], 16)

            def load_down(run, expert, slots, free=None):
                w = run.down[bass.ds(expert, 1), :, :].rearrange("a k n -> (a k) n")
                rows_in = run.blocks * P // len(slots)
                for j, s in enumerate(slots):
                    if free is not None:
                        sp.wait_ge(run.to_dve, free[j])
                    sp.dma_start(sview(s, rows_in // P, D), kview(w[j * rows_in:(j + 1) * rows_in, :])).then_inc(run.w_in[s], 16)

            for t in range(NT):
                sp.dma_start(xres[:, t, :], x[t * P:(t + 1) * P, :]).then_inc(in_x[t], 16)
            sp.dma_start(ident[:, :], ident_d).then_inc(in_par, 16)
            sp.dma_start(par[:, :], cols).then_inc(in_par, 16)
            sp.dma_start(tri[:, :], tri_d).then_inc(in_tri, 16)
            sp.dma_start(slot_iota[:, :], iota_d[0:P].partition_broadcast(P)).then_inc(in_tri, 16)
            load(0, sview(0, DC, D), kview(wn))
            sp.dma_start(iota[:, :], iota_d.partition_broadcast(P)).then_inc(in_ends, 16)
            sp.dma_start(ends_i[:, 0, :], src).then_inc(in_ends, 16)
            sp.dma_start(ends_i[:, 1, :], dst).then_inc(in_ends, 16)

            def load_edges(g, b):
                sp.dma_start(ea_raw[:, b, :, :],
                             edge[bass.ds(g * GROUP * P, GROUP * P), :].rearrange("(c p) d -> p c d", p=P)
                             ).then_inc(in_edge[b], 16)

            for b in range(2):
                load_edges(b, b)
            load(1, sview(1, DE // P, D), kview(we))
            load(2, sview(2, DC, D), kview(w1[0, 0:D, :]))
            load(3, sview(3, DC, D), kview(w1[0, D:2 * D, :]))
            wait(sp, sig.to_act, ACT0["tok0"])
            wait(sp, sig.to_dve, DVE0["tok0"])
            load(0, sview(0, DC, D), kview(w2[0]))
            sp.dma_start(brow[:, 0, :], bview("b1", D)).then_inc(in_row[0], 16)
            with sp.Fori(1, GROUPS // 2) as i:
                for b in range(2):
                    sp.wait_ge(ea_split, 2 * (2 * i - 1 + b))
                    load_edges(2 * i + b, b)
            with sp.Fori(1, L) as l:
                sp.wait_ge(sig.to_dve, DVE0["rounds"] + 24 * (l - 1) + 14)
                load(2, sview(2, DC, D), kview(w1[bass.ds(l, 1), 0:D, :].rearrange("a k n -> (a k) n")))
                load(3, sview(3, DC, D), kview(w1[bass.ds(l, 1), D:2 * D, :].rearrange("a k n -> (a k) n")))
                sp.wait_ge(sig.dve_freed, DVE0["rounds"] + 24 * (l - 1) + 14)
                sp.dma_start(brow[:, 0, :], rows[bass.ds(ROWS["b1"] + l * D, D)].partition_broadcast(P)
                             ).then_inc(in_row[0], 16)
                sp.wait_ge(sig.to_dve, DVE0["rounds"] + 24 * (l - 1) + 20)
                load(0, sview(0, DC, D), kview(w2[bass.ds(l, 1), :, :].rearrange("a k n -> (a k) n")))
            last = DVE0["rounds"] + 24 * (L - 1)
            sp.wait_ge(sig.to_dve, last + 14)
            sp.dma_start(brow[:, 1, :], bview("bv", D)).then_inc(in_row[1], 16)
            sp.dma_start(xres[:, :, :], x.rearrange("(t p) d -> p t d", p=P)).then_inc(in_x_again, 16)
            load(2, sview(2, DC, D), kview(wqkv[:, D:2 * D]))
            load(3, sview(3, DC, D), kview(wqkv[:, 2 * D:3 * D]))
            sp.wait_ge(sig.dve_freed, last + 14)
            sp.dma_start(brow[:, 0, :], bview("bo", D)).then_inc(in_row[0], 16)
            sp.wait_ge(sig.to_dve, last + 20)
            load(1, sview(1, DC, D), kview(wqkv[:, 0:D]))
            load(0, slot[0][0:DH, 0:4 * D].rearrange("p (k n) -> p k n", k=4),
                 wo[0:4 * DH, :].rearrange("(k p) n -> p k n", p=DH))
            sp.dma_start(wg[:, :, :], wg0.rearrange("(k p) n -> p k n", p=P)).then_inc(in_gate, 16)
            sp.dma_start(bg[:, 0:NE0], bview("bg0", NE0)).then_inc(in_gate, 16)
            sp.dma_start(bg[:, 8:8 + NE1], bview("bg1", NE1)).then_inc(in_gate, 16)
            sp.wait_ge(sig.to_act, ACT0["heads"] + k_unit(NH - 1) + 1)
            sp.wait_ge(sig.to_dve, DVE0["heads"] + q_unit(NH - 1) + 1)
            load(1, slot[1][0:DH, 0:4 * D].rearrange("p (k n) -> p k n", k=4),
                 wo[4 * DH:8 * DH, :].rearrange("(k p) n -> p k n", p=DH))

            sp.dma_start(e0b2_s[:, :], e0b2).then_inc(in_eb2, 16)
            load_up(run0, 0, [0, 0])
            sp.wait_ge(sig.to_dve, DVE0["xt1"])
            load_down(run0, 0, run0.down_slots)

            def run_items(run):
                sp.wait_ge(run.plan_set, 1)
                last = sp.value_load(plan_i[0:1, 16:17], min_val=run.items_min - 1, max_val=run.items_max - 1)

                def expert(i):
                    return sp.value_load(plan_i[0:1, bass.ds(i, 1)], min_val=0, max_val=run.ne - 1)

                def load_x(i):
                    sp.dma_start(item_x[:, :], run.scattered[bass.ds(i * P, P), :]).then_inc(run.x_in, 16)

                n = len(run.up_slots)
                sp.wait_ge(run.scattered_in, 16 * NT * run.picks)
                load_x(1)
                load_up(run, expert(1), [1 + run.n_up * (j + 1) // n for j in range(n)])
                with sp.Fori(1, last) as k:
                    a, v = run.act_after(k - 1), run.dve_after(k - 1)
                    sp.wait_ge(run.to_act, a + 1)
                    sp.wait_ge(run.to_dve, v + 1)
                    load_x(k + 1)
                    load_up(run, expert(k + 1), [v + 1 + run.n_up * (j + 1) // n for j in range(n)])
                    sp.wait_ge(run.to_dve, run.dve_after(k))
                    sp.sem_inc(stood, 1)
                    load_down(run, expert(k), run.down_slots)
                before = run.dve_after(last) - 2 - run.n_up
                load_down(run, expert(last), run.up_slots, [before + run.n_up * (j + 1) // n for j in range(n)])
                return last

            last = run_items(run0)
            sig = sig1
            sp.wait_ge(run0.to_dve, run0.dve_after(last))
            load(0, sview(0, DC, N), kview(gw1[:, 0:N]))
            load(1, sview(1, DC, N), kview(gw1[:, N:2 * N]))
            sp.wait_ge(run0.to_dve, run0.dve_after(last) + 2)
            load(2, sview(2, 4, D), kview(gw2[0:N, :]))
            load(3, sview(3, 4, D), kview(gw2[N:2 * N, :]))
            sp.wait_ge(normed, NT * (L + 3))
            sp.dma_start(att1[:, :, :], rows[ROWS["g_src1"]:ROWS["g_src1"] + 2 * GD]
                         .rearrange("(a n) -> a n", a=2).partition_broadcast(P)).then_inc(in_att1, 16)
            sp.dma_start(brow[:, :, :], rows[ROWS["g_src2"]:ROWS["g_src2"] + 2 * D]
                         .rearrange("(a n) -> a n", a=2).partition_broadcast(P)).then_inc(in_row[0], 16)
            sp.wait_ge(sig.to_act, ACT0["mask"])
            sp.wait_ge(sig.to_dve, DVE0["mask"])
            sp.dma_start(g_b1[:, :], bview("g_b1", GD)).then_inc(in_gb, 16)
            sp.dma_start(g_b2[:, :], bview("g_b2", D)).then_inc(in_gb, 16)

            sp.dma_start(wg[:, :, 0:NE1], wg1.rearrange("(k p) n -> p k n", p=P)).then_inc(in_gate1, 16)
            sp.wait_ge(sig.to_dve, DVE0["gat2"])
            sp.wait_ge(sig.to_act, ACT0["gat2"])
            load_up(run1, 0, [0])
            load_down(run1, 0, run1.down_slots)
            sp.wait_ge(sig.to_dve, DVE0["xt3"])
            sp.dma_start(e1b2_s[:, :], e1b2).then_inc(in_eb2, 16)
            run_items(run1)
            for t in range(NT):
                sp.wait_ge(final, t + 1)
                sp.dma_start(out[t * P:(t + 1) * P, :], xres[:, t, :]).then_inc(out_done, 16)
            sp.wait_ge(out_done, 16 * NT)

        @block.tensor
        def _(pe):
            sig = sig0
            mm = nc.tensor.matmul

            def act_bank(j, before):
                wait(pe, sig.act_freed, before + max(0, j - RING + 1))
                return act_ps[j % RING]

            def dve_bank(j, before):
                wait(pe, sig.dve_freed, before + max(0, j - RING + 1))
                return dve_ps[j % RING]

            def turn_features(source, a0, v0, before):
                pe.wait_ge(normed, before + NT - 1)
                for t in range(NT):
                    if t == NT - 1:
                        pe.wait_ge(normed, before + NT)
                    for c in range(DC):
                        if t == 0:
                            bank = act_bank(c // 2, a0) if c % 2 == 0 else dve_bank(c // 2, v0)
                        else:
                            bank = (act_ps if c % 2 == 0 else dve_ps)[c // 2]
                        last = nc.tensor.transpose(bank[:, t * P:(t + 1) * P], source[:, t, c * P:(c + 1) * P], ident[:, :])
                        if t == NT - 1:
                            last.then_inc(sig.to_act if c % 2 == 0 else sig.to_dve, 1)

            def turn_tokens(source, a0, v0):
                for t in range(NT):
                    for half in range(2):
                        bank = act_bank(t, a0) if half == 0 else dve_bank(t, v0)
                        for j in range(3):
                            last = nc.tensor.transpose(bank[:, j * P:(j + 1) * P],
                                                       source[:, half * 3 + j, t * P:(t + 1) * P], ident[:, :])
                        last.then_inc(sig.to_act if half == 0 else sig.to_dve, 1)

            def kslot(s, n, parts=False):
                return (part_slot if parts else slot)[s][:, 0:4608 // n * n].rearrange("p (k n) -> p k n", n=n)

            def mm_parts(to, kept, moved, start, stop):
                mm(to, kept[0], moved[0], start=start, stop=False)
                mm(to, kept[0], moved[1], start=False, stop=False)
                return mm(to, kept[1], moved[0], start=False, stop=stop)

            pe.wait_ge(in_par, 32)
            turn_features(xn, ACT0["xt0"], DVE0["xt0"], 0)
            pe.wait_ge(slot_in[0], 16)
            pe.wait_ge(sig.act_freed, ACT0["wn"])
            pe.wait_ge(sig.dve_freed, DVE0["wn"])
            wn_s = kslot(0, D)
            for c in range(DC):
                bank = act_bank(c // 2, ACT0["wn"]) if c % 2 == 0 else dve_bank(c // 2, DVE0["wn"])
                for k in range(DC):
                    last = mm(bank[:, :], wn_s[:, k, c * P:(c + 1) * P], xn_t[:, k, :], start=(k == 0), stop=(k == DC - 1))
                last.then_inc(sig.to_act if c % 2 == 0 else sig.to_dve, 1)
            pe.wait_ge(sig.act_freed, ACT0["tok0"])
            pe.wait_ge(sig.dve_freed, DVE0["tok0"])
            turn_tokens(nodes_t, ACT0["tok0"], DVE0["tok0"])

            pe.wait_ge(sig.act_freed, ACT0["edges"])
            pe.wait_ge(sig.dve_freed, DVE0["edges"])
            pe.wait_ge(const_set, 2)
            sums = act_ps + dve_ps[0:2]
            for n in range(OPENED):
                mm(sums[n % 6][:, :], zero[:, 0:P], zero[:, :], start=(n < 6), stop=False).then_inc(chunk_done, 1)
            with pe.Fori(0, GROUPS // 2) as i:
                for b in range(2):
                    pe.wait_ge(ea_split, 2 * (2 * i + b + 1))
                    pe.wait_ge(ea_high, 2 * i + b + 1)
                    for c in range(GROUP):
                        pe.wait_ge(hots, (2 * i + b) * GROUP + c + 1)
                        hd, hs = hot_d[:, c % 2, :], hot_s[:, c % 2, :]
                        for m in range(NT):
                            mm(act_ps[m][:, :], hs[:, m * P:(m + 1) * P], hd, start=False, stop=False)
                        for m in range(DE // P):
                            for part in (ea_hi, ea_lo):
                                last = mm(dve_ps[m][:, :], part[:, b, c, m * P:(m + 1) * P], hd, start=False, stop=False)
                        last.then_inc(chunk_done, 1)
            for n, bank in enumerate(sums):
                mm(bank[:, :], zero[:, 0:P], zero[:, :], start=False, stop=True).then_inc(
                    sig.to_act if n < NT else sig.to_dve, 1)

            pe.wait_ge(sig.act_freed, ACT0["deg"])
            bank = dve_bank(0, DVE0["deg"])
            for m in range(NT):
                last = mm(bank[:, :], ones[:, :], ct[:, m, :], start=(m == 0), stop=(m == NT - 1))
            last.then_inc(sig.to_dve, 1)
            pe.wait_ge(slot_in[1], 16)
            pe.wait_ge(sig.dve_freed, DVE0["base"])
            for c in range(DC):
                bank = dve_bank(c, DVE0["base"])
                for k in range(DE // P):
                    last = mm(bank[:, :], kslot(1, D)[:, k, c * P:(c + 1) * P], sea_t[:, k, :],
                              start=(k == 0), stop=(k == DE // P - 1))
                last.then_inc(sig.to_dve, 1)

            pe.wait_ge(cpt_set, 1)
            with pe.Fori(0, L) as l:
                a0, v0 = ACT0["rounds"] + 10 * l, DVE0["rounds"] + 24 * l
                pe.wait_ge(sig.act_freed, a0)
                for c in range(DC):
                    bank = dve_bank(c, v0)
                    for k in range(NT):
                        last = mm(bank[:, :], nodes[:, k, c * P:(c + 1) * P], cpt[:, k, :], start=(k == 0), stop=(k == NT - 1))
                    last.then_inc(sig.to_dve, 1)
                pe.wait_ge(nt_low, DC * (l + 1))
                pe.wait_ge(w_low, 3 * DC * l + DC)
                pe.wait_ge(sig.dve_freed, v0 + DC)
                for u in range(8):
                    t, half = u // 2, u % 2
                    bank = dve_bank(u, v0 + 6)
                    ts, hs = slice(t * P, (t + 1) * P), slice(half * HALF, (half + 1) * HALF)
                    for k in range(DC):
                        mm_parts(bank[:, 0:HALF], (nt_hi[:, k, ts], nt_lo[:, k, ts]), (w1_hi[k][:, hs], kslot(2, D, True)[:, k, hs]),
                                 start=(k == 0), stop=False)
                    for k in range(DC):
                        if u == 0:
                            pe.wait_ge(w_low, 3 * DC * l + DC + k + 1)
                            pe.wait_ge(agg_low, DC * l + k + 1)
                        last = mm_parts(bank[:, 0:HALF], (agg_hi[:, k, ts], agg_lo[:, k, ts]),
                                        (kslot(1, D, True)[:, k, hs], kslot(3, D, True)[:, k, hs]), start=False, stop=(k == DC - 1))
                    last.then_inc(sig.to_dve, 1)

                def turn_h(c, ts):
                    for t in ts:
                        last = nc.tensor.transpose(act_ps[c % RING][:, t * P:(t + 1) * P], h[:, t, c * P:(c + 1) * P], ident[:, :])
                    if t == NT - 1:
                        last.then_inc(sig.to_act, 1)

                pe.wait_ge(normed, NT * (l + 2) - 1)
                for c in range(RING):
                    turn_h(c, range(NT - 1))
                pe.wait_ge(normed, NT * (l + 2))
                for c in range(DC):
                    if c >= RING:
                        act_bank(c, a0)
                    turn_h(c, range(NT - 1, NT) if c < RING else range(NT))
                for c in range(DC):
                    bank = dve_bank(c, v0 + 14)
                    cs = slice(c * P, (c + 1) * P)
                    for k in range(DC):
                        if c == 0:
                            pe.wait_ge(w_low, 3 * DC * l + 2 * DC + k + 1)
                            pe.wait_ge(h_low, DC * l + k + 1)
                        last = mm_parts(bank[:, :], (kslot(1, D, True)[:, k, cs], kslot(0, D, True)[:, k, cs]),
                                        (h_hi[:, k, :], h_lo[:, k, :]), start=(k == 0), stop=(k == DC - 1))
                    last.then_inc(sig.to_dve, 1)
                pe.wait_ge(sig.dve_freed, v0 + 20)
                turn_tokens(nodes_t, a0 + 6, v0 + 20)

            split = 3 * DC * L
            pe.wait_ge(nt_low, DC * (L + 1))
            for u in range(8):
                t, half = u // 2, u % 2
                bank = dve_bank(u, DVE0["v"])
                ts, hs = slice(t * P, (t + 1) * P), slice(half * HALF, (half + 1) * HALF)
                for k in range(DC):
                    if u == 0:
                        pe.wait_ge(w_low, split + k + 1)
                    last = mm_parts(bank[:, 0:HALF], (na_hi[k][:, ts], na_lo[:, k, ts]),
                                    (wv_hi[:, k * D:(k + 1) * D][:, hs], kslot(3, D, True)[:, k, hs]), start=(k == 0), stop=(k == DC - 1))
                last.then_inc(sig.to_dve, 1)

            a0, v0 = ACT0["heads"], DVE0["heads"]

            def project(hd):
                fs = slice(hd * DH, (hd + 1) * DH)
                for which, (bank, s, signal) in enumerate(((dve_bank(q_unit(hd), v0), 1, sig.to_dve),
                                                           (act_bank(k_unit(hd), a0), 2, sig.to_act))):
                    for k in range(DC):
                        if hd == 0:
                            pe.wait_ge(w_low, split + DC * (1 + which) + k + 1)
                        high = wq_hi[k] if which == 0 else kslot(3, D, True)[:, k, :]
                        last = mm_parts(bank[0:DH, :], (high[:, fs], kslot(s, D, True)[:, k, fs]), (na_hi[k][:, :], na_lo[:, k, :]),
                                        start=(k == 0), stop=(k == DC - 1))
                    last.then_inc(signal, 1)

            def scores(hd):
                pe.wait_ge(sig.dve_freed, v0 + q_unit(hd) + 1)
                pe.wait_ge(sig.act_freed, a0 + k_unit(hd) + 1)
                for t in range(NT):
                    bank = act_bank(score_unit(hd) + t, a0)
                    mm(bank[:, :], q_t[:, hd % 2, t * P:(t + 1) * P], k_t[:, hd % 2, :], start=True, stop=True
                       ).then_inc(sig.to_act, 1)

            def turn_probs(hd):
                pe.wait_ge(prob_set, NT * (hd + 1))
                for m in range(NT):
                    bank = act_bank(turn_unit_a(hd) + m // 2, a0) if m % 2 == 0 else dve_bank(turn_unit_v(hd) + m // 2, v0)
                    for t in range(NT):
                        last = nc.tensor.transpose(bank[:, t * P:(t + 1) * P], prb[:, hd % 2, t, m * P:(m + 1) * P], ident[:, :])
                    last.then_inc(sig.to_act if m % 2 == 0 else sig.to_dve, 1)

            def weigh(hd):
                pe.wait_ge(sig.act_freed, a0 + turn_unit_a(hd) + 2)
                pe.wait_ge(sig.dve_freed, v0 + turn_unit_v(hd) + 2)
                bank = dve_bank(pv_unit(hd), v0)
                for m in range(NT):
                    last = mm(bank[0:DH, :], v[:, m, hd * DH:(hd + 1) * DH], prb_t[:, m, :], start=(m == 0), stop=(m == NT - 1))
                last.then_inc(sig.to_dve, 1)

            project(0)
            scores(0)
            for hd in range(NH):
                if hd + 1 < NH:
                    project(hd + 1)
                turn_probs(hd)
                if hd + 1 < NH:
                    scores(hd + 1)
                weigh(hd)
            pe.wait_ge(slot_in[0], 16 * (L + 2))
            pe.wait_ge(slot_in[1], 48)
            pe.wait_ge(sig.dve_freed, DVE0["wo"])
            for u in range(8):
                t, half = u // 2, u % 2
                bank = dve_bank(u, DVE0["wo"])
                for hd in range(NH):
                    w = slot[hd // 4][0:DH, 0:4 * D].rearrange("p (k n) -> p k n", k=4)[:, hd % 4, half * HALF:(half + 1) * HALF]
                    last = mm(bank[:, 0:HALF], attn_t[:, hd, t * P:(t + 1) * P], w, start=(hd == 0), stop=(hd == NH - 1))
                last.then_inc(sig.to_dve, 1)

            def gates(run, xt, ne, stage, bias_stage, b2, k_in):
                pe.wait_ge(*k_in)
                bank = dve_bank(0, DVE0[stage])
                for t in range(NT):
                    for k in range(DC):
                        last = mm(bank[:, t * ne:(t + 1) * ne], xt[:, k, t * P:(t + 1) * P], wg[:, k, 0:ne],
                                  start=(k == 0), stop=(k == DC - 1))
                last.then_inc(sig.to_dve, 1)
                pe.wait_ge(run.sel_set, 1)
                bank = dve_bank(1, DVE0[stage])
                for t in range(NT + 1):
                    for m in range(min(t + 1, NT)):
                        last = mm(bank[:, t * ne:(t + 1) * ne], tri[:, :] if m == t else ones[:, :], sel[:, m, 0:ne],
                                  start=(m == 0), stop=(m == min(t, NT - 1)))
                last.then_inc(sig.to_dve, 1)
                pe.wait_ge(run.gate_set, 1)
                bank = dve_bank(2, DVE0[stage])
                for t in range(NT):
                    last = nc.tensor.transpose(bank[0:ne, t * P:(t + 1) * P], gate[:, t, 0:ne], ident[:, :])
                last.then_inc(sig.to_dve, 1)
                pe.wait_ge(in_eb2, 16 if ne == NE0 else 32)
                pe.wait_ge(sig.dve_freed, DVE0[bias_stage])
                for u in range(8):
                    t, half = u // 2, u % 2
                    bank = dve_bank(u, DVE0[bias_stage])
                    mm(bank[:, 0:HALF], gate_t[0:ne, t * P:(t + 1) * P], b2[:, half * HALF:(half + 1) * HALF],
                       start=True, stop=True).then_inc(sig.to_dve, 1)

            turn_features(xn1, ACT0["xt1"], DVE0["xt1"], NT * (L + 1))
            pe.wait_ge(sig.act_freed, ACT0["gate0"])
            pe.wait_ge(sig.dve_freed, DVE0["gate0"])
            pe.wait_ge(in_tri, 32)
            gates(run0, xn1_t, NE0, "gate0", "bias0", e0b2_s, (in_gate, 48))

            def run_items(run, nodes_in):
                pe.wait_ge(run.plan_set, 1)
                last = pe.value_load(plan_i[0:1, 16:17], min_val=run.items_min - 1, max_val=run.items_max - 1)

                def pick_x():
                    pe.wait_ge(run.first_set, 1)
                    for half, (bank, signal) in enumerate(((act_ps[3], run.to_act), (dve_ps[2], run.to_dve))):
                        for j in range(3):
                            c = 3 * half + j
                            for m in range(NT):
                                last = mm(bank[:, j * P:(j + 1) * P], nodes_in[:, m, c * P:(c + 1) * P], first_sel[:, m, :],
                                          start=(m == 0), stop=(m == NT - 1))
                        last.then_inc(signal, 1)

                def turn_x(i, a, v):
                    pe.wait_ge(run.x_in, 16 * i)
                    pe.wait_ge(run.act_freed, a)
                    pe.wait_ge(run.dve_freed, v if isinstance(v, int) else v - 2)
                    for half, (bank, signal) in enumerate(((act_ps[3], run.to_act), (dve_ps[2], run.to_dve))):
                        for j in range(3):
                            c = 3 * half + j
                            last = nc.tensor.transpose(bank[:, j * P:(j + 1) * P], item_x[:, c * P:(c + 1) * P], ident[:, :])
                        last.then_inc(signal, 1)

                def turn_hidden(v_up):
                    pe.wait_ge(run.dve_freed, v_up)
                    for u in range(run.n_turn):
                        for j in range(min(4, run.blocks - 4 * u)):
                            last = nc.tensor.transpose(act_ps[u][:, j * P:(j + 1) * P],
                                                       hid[:, (4 * u + j) * P:(4 * u + j + 1) * P], ident[:, :])
                        last.then_inc(run.to_act, 1)

                def times_up(i, a, v):
                    if run.layer == 0:
                        pe.wait_ge(x_low, i + 1)
                    else:
                        pe.wait_ge(run.act_freed, a + 1)
                    pe.wait_ge(run.dve_freed, v + 1)
                    per = run.n_up // len(run.up_slots)
                    for u in range(run.n_up):
                        j = u // per
                        s = run.up_slots[j]
                        to, cols_in = dve_ps[(3 + u) % 4][:, 0:HALF], slice(u % per * HALF, (u % per + 1) * HALF)
                        if u % per == 0:
                            if run.layer == 0:
                                pe.wait_ge(up_low[j], DC * (i + 1))
                            else:
                                pe.wait_ge(run.w_in[s], 16 * (i + 1))
                        for k in range(DC):
                            if run.layer == 0:
                                ks = slice(k * P, (k + 1) * P)
                                last = mm_parts(to, (x_hi[:, ks], x_lo[:, ks]), (up_hi[j][k][:, cols_in], kslot(s, D, True)[:, k, cols_in]),
                                                start=(k == 0), stop=(k == DC - 1))
                            else:
                                last = mm(to, item_xt[:, k, :], kslot(s, per * HALF)[:, k, cols_in], start=(k == 0), stop=(k == DC - 1))
                        last.then_inc(run.to_dve, 1)

                def times_down(i, a_turned, v_banks, slots=run.down_slots, ahead=1):
                    pe.wait_ge(run.act_freed, a_turned)
                    for s in slots:
                        pe.wait_ge(run.w_in[s], 16 * (i + ahead))
                    for half in range(2):
                        pe.wait_ge(run.dve_freed, v_banks[half])
                        for k in range(run.blocks):
                            last = mm(dve_ps[run.down_banks[half]][:, 0:HALF], hid_t[:, k, :],
                                      kslot(slots[k // DC], D)[:, k % DC, half * HALF:(half + 1) * HALF],
                                      start=(k == 0), stop=(k == run.blocks - 1))
                        last.then_inc(run.to_dve, 1)

                pe.wait_ge(sig.act_freed, ACT0[f"bias{run.layer}"])
                pe.wait_ge(sig.dve_freed, DVE0[f"bias{run.layer}"] + 8)
                pick_x()
                times_up(0, 0, 0)

                def iteration(k):
                    a, v = run.act_after(k), run.dve_after(k)
                    turn_x(k + 1, a, v)
                    turn_hidden(v if isinstance(k, int) else v - 2)
                    times_up(k + 1, a, v)
                    times_down(k, a + 1 + run.n_turn, (v + 2, v + 3) if run.n_up > 1 else (v, v))

                iteration(0)
                with pe.Fori(1, last) as k:
                    iteration(k)
                a, v = run.act_after(last), run.dve_after(last)
                turn_hidden(v - 2)
                pe.wait_ge(run.last_set, 1)
                pe.wait_ge(run.act_freed, a)
                for t in range(NT):
                    turned = nc.tensor.transpose(act_ps[3][:, t * P:(t + 1) * P], last_sel[:, t, :], ident[:, :])
                turned.then_inc(run.to_act, 1)
                times_down(last, a + run.n_turn, (v, v), run.up_slots, 2)
                pe.wait_ge(run.act_freed, a + run.n_turn + 1)
                for u in range(8):
                    t, half = u // 2, u % 2
                    pe.wait_ge(run.dve_freed, v + 2 + max(0, u - RING + 1))
                    mm(dve_ps[u % RING][:, 0:HALF], last_t[:, t * P:(t + 1) * P], item_y[:, half * HALF:(half + 1) * HALF],
                       start=True, stop=True).then_inc(run.to_dve, 1)
                return last

            last = run_items(run0, xn1)
            sig = sig1

            pe.wait_ge(run0.dve_freed, run0.dve_after(last) + 10)
            turn_features(xn2, ACT0["xt2"], DVE0["xt2"], NT * (L + 2))
            pe.wait_ge(sig.act_freed, ACT0["h1"])
            pe.wait_ge(sig.dve_freed, DVE0["h1"])
            pe.wait_ge(w_low, split + 3 * DC + 2 * DC)
            for u in range(8):
                t, half = u // 2, u % 2
                bank = act_bank(t, ACT0["h1"]) if half == 0 else dve_bank(t, DVE0["h1"])
                for k in range(DC):
                    ts = slice(t * P, (t + 1) * P)
                    last = mm_parts(bank[:, :], (xn2_hi[:, k, ts], xn2_lo[:, k, ts]),
                                    (gw1_hi[half * DC + k][:, :], kslot(half, N, True)[:, k, :]), start=(k == 0), stop=(k == DC - 1))
                last.then_inc(sig.to_act if half == 0 else sig.to_dve, 1)
            for t in range(NT):
                bank = dve_bank(t, DVE0["mask"])
                for m in range(NT):
                    last = nc.tensor.transpose(bank[:, m * P:(m + 1) * P], ct[:, m, t * P:(t + 1) * P], ident[:, :])
                last.then_inc(sig.to_dve, 1)

            pe.wait_ge(sig.act_freed, ACT0["gat1"])

            def spread(a_src, unit, v0):
                bank = dve_bank(unit, v0)
                for t in range(NT):
                    last = mm(bank[:, t * P:(t + 1) * P], a_src(t).to_broadcast([P, P]), ident[:, :], start=True, stop=True)
                last.then_inc(sig.to_dve, 1)

            def spread_shifts(g):
                if g >= 2:
                    pe.wait_ge(g_low, NT * (g - 1))
                pe.wait_ge(g_dec, g + 1)
                for j in range(2):
                    bank = act_ps[2 * (g % 2) + j]
                    for t in range(NT):
                        last = mm(bank[:, t * P:(t + 1) * P], gdec[:, g % 2, 2 + j, t:t + 1].to_broadcast([P, P]), ident[:, :],
                                  start=True, stop=True)
                last.then_inc(g_rows, 1)

            pe.wait_ge(att_set, 1)
            v0 = DVE0["gat1"]
            spread(lambda t: att[:, 0, t, 0:1], row_unit(0), v0)
            spread(lambda t: att[:, 0, t, 1:2], row_unit(1), v0)
            spread(lambda t: att[:, 0, t, 2:3], row_unit(2), v0)
            spread_shifts(0)
            spread_shifts(1)
            for hd in range(GH):
                if hd + 2 < GH:
                    spread_shifts(hd + 2)
                if hd + 3 < GH:
                    spread(lambda t: att[:, 0, t, hd + 3:hd + 4], row_unit(hd + 3), v0)
                pe.wait_ge(g_weight, NT * (hd + 1))
                for pair in range(2):
                    bank = dve_bank(out_unit(hd) + pair, v0)
                    for t in (2 * pair, 2 * pair + 1):
                        w = GC + 2
                        for m in range(NT):
                            last = mm(bank[:, (t % 2) * w:(t % 2 + 1) * w], gp_t[:, hd % 2, m, t * P:(t + 1) * P], h1x[:, m, hd, :],
                                      start=(m == 0), stop=(m == NT - 1))
                    last.then_inc(sig.to_dve, 1)
            pe.wait_ge(sig.dve_freed, DVE0["o1t"])
            for c in range(GD // P):
                bank = act_bank(c // 2, ACT0["o1t"]) if c % 2 == 0 else dve_bank(c // 2, DVE0["o1t"])
                for t in range(NT):
                    last = nc.tensor.transpose(bank[:, t * P:(t + 1) * P], out1[:, t, c * P:(c + 1) * P], ident[:, :])
                last.then_inc(sig.to_act if c % 2 == 0 else sig.to_dve, 1)
            pe.wait_ge(sig.act_freed, ACT0["h2"])
            pe.wait_ge(sig.dve_freed, DVE0["h2"])
            pe.wait_ge(w_low, split + 3 * DC + 2 * DC + GD // P)
            for u in range(8):
                t, half = u // 2, u % 2
                bank = act_bank(t, ACT0["h2"]) if half == 0 else dve_bank(t, DVE0["h2"])
                for k in range(GD // P):
                    ts, hs = slice(t * P, (t + 1) * P), slice(half * HALF, (half + 1) * HALF)
                    last = mm_parts(bank[:, 0:HALF], (out1_hi[:, k, ts], out1_lo[:, k, ts]),
                                    (kslot(k // 4, D, True)[:, k % 4, hs], kslot(2 + k // 4, D, True)[:, k % 4, hs]),
                                    start=(k == 0), stop=(k == GD // P - 1))
                last.then_inc(sig.to_act if half == 0 else sig.to_dve, 1)
            pe.wait_ge(att_set, 2)
            v0 = DVE0["gat2"]
            spread(lambda t: att[:, 0, t, 0:1], 0, v0)
            pe.wait_ge(sig.act_freed, ACT0["gat2"])
            spread_shifts(GH)
            pe.wait_ge(g_weight, NT * (GH + 1))
            for u in range(8):
                t, half = u // 2, 1 - u % 2
                bank = dve_bank(1 + u, v0)
                lo, hi = (0, HALF) if half == 0 else (HALF, D + 2)
                for m in range(NT):
                    last = mm(bank[:, 0:hi - lo], gp_t[:, GH % 2, m, t * P:(t + 1) * P], h2x[:, m, lo:hi], start=(m == 0), stop=(m == NT - 1))
                last.then_inc(sig.to_dve, 1)

            turn_features(xn3, ACT0["xt3"], DVE0["xt3"], NT * (L + 3))
            pe.wait_ge(sig.act_freed, ACT0["gate1"])
            pe.wait_ge(sig.dve_freed, DVE0["gate1"])
            gates(run1, xn3_t, NE1, "gate1", "bias1", e1b2_s, (in_gate1, 16))
            run_items(run1, xn3)

        @block.scalar
        def _(act):
            sig = sig0
            go = nc.scalar.activation

            def bank_of(j, before):
                act.wait_ge(sig.to_act, before + j + 1)
                return act_ps[j % RING]

            for c in range(0, DC, 2):
                bank = bank_of(c // 2, ACT0["xt0"])
                go(xn_t[:, c, :], bank[:, :], ACT.Copy).then_inc(sig.act_freed, 1)
            for b in range(2):
                act.wait_ge(in_edge[b], 16)
                go(ea_hi[:, b, :, :], ea_raw[:, b, :, :], ACT.Copy).then_inc(ea_high, 1)
            act.wait_ge(in_par, 32)
            for c in range(0, DC, 2):
                bank = bank_of(c // 2, ACT0["wn"])
                go(nodes_t[:, c, :], bank[:, :], ACT.Identity, bias=col("bn", c)).then_inc(sig.act_freed, 1)
            for t in range(NT):
                bank = bank_of(t, ACT0["tok0"])
                go(nodes[:, t, 0:HALF], bank[:, 0:HALF], ACT.Copy).then_inc(sig.act_freed, 1)
            with act.Fori(1, GROUPS // 2) as i:
                for b in range(2):
                    act.wait_ge(in_edge[b], 16 * (i + 1))
                    act.wait_ge(chunk_done, OPENED + 2 * GROUP * i - (GROUP if b == 0 else 0))
                    go(ea_hi[:, b, :, :], ea_raw[:, b, :, :], ACT.Copy).then_inc(ea_high, 1)
            for m in range(NT):
                bank = bank_of(m, ACT0["edges"])
                go(ct[:, m, :], bank[:, :], ACT.Copy).then_inc(sig.act_freed, 1)
            with act.Fori(0, L) as l:
                a0 = ACT0["rounds"] + 10 * l
                act.wait_ge(sig.dve_freed, DVE0["rounds"] + 24 * l)
                act.wait_ge(sig.act_freed, a0)
                for c in range(DC):
                    go(nt_hi[:, c, :], nodes_t[:, c, :], ACT.Copy).then_inc(nt_high, 1)
                act.wait_ge(slot_in[2], 16 * (l + 1))
                act.wait_ge(sig.to_dve, DVE0["rounds"])
                for k in range(DC):
                    go(w1_hi[k][:, :], slot[2][:, k * D:(k + 1) * D], ACT.Copy).then_inc(w_high, 1)
                act.wait_ge(slot_in[3], 16 * (l + 1))
                for k in range(DC):
                    go(part_slot[1][:, k * D:(k + 1) * D], slot[3][:, k * D:(k + 1) * D], ACT.Copy).then_inc(w_high, 1)
                act.wait_ge(sig.to_dve, DVE0["rounds"] + 24 * l + DC)
                for c in range(DC):
                    act.wait_ge(sig.dve_freed, DVE0["rounds"] + 24 * l + c + 1)
                    go(agg_hi[:, c, :], agg_t[:, c, :], ACT.Copy).then_inc(agg_high, 1)
                act.wait_ge(sig.to_dve, DVE0["rounds"] + 24 * l + 14)
                act.wait_ge(slot_in[0], 16 * (l + 2))
                for k in range(DC):
                    go(part_slot[1][:, k * D:(k + 1) * D], slot[0][:, k * D:(k + 1) * D], ACT.Copy).then_inc(w_high, 1)
                for c in range(DC):
                    bank = bank_of(c, a0)
                    for to in (h_t, h_hi):
                        last = go(to[:, c, :], bank[:, :], ACT.Relu, bias=par[:, bass.ds(COLS["ln_b"] + DC * l + c, 1)],
                                  scale=par[:, bass.ds(COLS["ln_g"] + DC * l + c, 1)])
                    last.then_inc(sig.act_freed, 1)
                for t in range(NT):
                    bank = bank_of(t, a0 + 6)
                    go(nodes[:, t, 0:HALF], bank[:, 0:HALF], ACT.Copy).then_inc(sig.act_freed, 1)
            a0 = ACT0["heads"]
            act.wait_ge(sig.dve_freed, DVE0["v"])
            act.wait_ge(sig.act_freed, a0)
            for c in range(DC):
                go(na_hi[c][:, :], nodes_t[:, c, :], ACT.Copy).then_inc(nt_high, 1)
            act.wait_ge(slot_in[3], 16 * (L + 1))
            for k in range(DC):
                go(wv_hi[:, k * D:(k + 1) * D], slot[3][:, k * D:(k + 1) * D], ACT.Copy).then_inc(w_high, 1)
            act.wait_ge(slot_in[1], 32)
            for k in range(DC):
                if k == 4:
                    act.wait_ge(x_added, 1)
                go(wq_hi[k][:, :], slot[1][:, k * D:(k + 1) * D], ACT.Copy).then_inc(w_high, 1)
            act.wait_ge(slot_in[2], 16 * (L + 1))
            act.wait_ge(sig.to_dve, DVE0["heads"])
            for k in range(DC):
                go(part_slot[3][:, k * D:(k + 1) * D], slot[2][:, k * D:(k + 1) * D], ACT.Copy).then_inc(w_high, 1)

            def key(hd):
                bank = bank_of(k_unit(hd), a0)
                go(k_t[:, hd % 2, :], bank[0:DH, :], ACT.Identity, bias=par[0:DH, COLS["bk"] + hd:COLS["bk"] + hd + 1]).then_inc(sig.act_freed, 1)

            key(0)
            for hd in range(NH):
                wait(act, sig.to_dve, DVE0["heads"] + turn_unit_v(hd - 2) + 2 if hd >= 2 else 0)
                for t in range(NT):
                    act.wait_ge(row_max, NT * hd + t + 1)
                    go(prb[:, hd % 2, t, :], act_ps[(score_unit(hd) + t) % RING][:, :], ACT.Exp, bias=nbias[:, hd % 2, t:t + 1],
                       accum_out=rsum[:, hd % 2, t:t + 1]).then_inc(sig.act_freed, 1)
                if hd + 1 < NH:
                    key(hd + 1)
                for j in range(2):
                    bank = bank_of(turn_unit_a(hd) + j, a0)
                    wait(act, sig.to_dve, DVE0["heads"] + pv_unit(hd - 1) + 1 if hd else 0)
                    go(prb_t[:, 2 * j, :], bank[:, :], ACT.Copy).then_inc(sig.act_freed, 1)
            def high_up(j, i):
                s = run0.up_slots[j]
                act.wait_ge(run0.w_in[s], 16 * (i + 1))
                for k in range(DC):
                    go(up_hi[j][k][:, :], slot[s][:, k * D:(k + 1) * D], ACT.Copy).then_inc(up_high[j], 1)

            act.wait_ge(sig.to_dve, DVE0["wo"])
            for j in range(2):
                high_up(j, 0)
            for c in range(0, DC, 2):
                bank = bank_of(c // 2, ACT0["xt1"])
                go(xn1_t[:, c, :], bank[:, :], ACT.Copy).then_inc(sig.act_freed, 1)

            act.wait_ge(logit_set, 1)
            go(prob[:, :, :], logit[:, :, :], ACT.Exp).then_inc(prob_exp, 1)

            def run_items(run):
                act.wait_ge(run.plan_set, 1)
                last = act.value_load(plan_i[0:1, 16:17], min_val=run.items_min - 1, max_val=run.items_max - 1)

                def x_in(a):
                    act.wait_ge(run.to_act, a + 1)
                    if run.layer == 0:
                        go(x_hi[:, 0:HALF], act_ps[3][:, 0:HALF], ACT.Copy).then_inc(run.act_freed, 1)
                        return
                    go(item_xt[:, 0:3, :].rearrange("p c n -> p (c n)"), act_ps[3][:, 0:HALF], ACT.Copy).then_inc(run.act_freed, 1)

                def gelus(i, a):
                    e = act.value_load(plan_i[0:1, bass.ds(i, 1)], min_val=0, max_val=run.ne - 1)
                    for u in range(run.n_turn):
                        act.wait_ge(run.to_act, a + u + 1)
                        for j in range(min(4, run.blocks - 4 * u)):
                            c = 4 * u + j
                            done = go(hid_t[:, c, :], act_ps[u][:, j * P:(j + 1) * P], ACT.Gelu,
                                      bias=par[:, bass.ds(e * run.blocks + (COLS[run.b1] + c), 1)])
                        done.then_inc(run.act_freed, 1)

                x_in(0)

                def iteration(k):
                    a = run.act_after(k)
                    if run.layer == 0:
                        act.wait_ge(run.to_dve, run.dve_after(k) - (2 if not isinstance(k, int) else 0) - 2)
                        high_up(0, k + 1)
                    x_in(a)
                    if run.layer == 0:
                        act.wait_ge(run.to_dve, run.dve_after(k) - (2 if not isinstance(k, int) else 0))
                        high_up(1, k + 1)
                    gelus(k, a + 1)

                iteration(0)
                with act.Fori(1, last) as k:
                    iteration(k)
                gelus(last, run.act_after(last))
                act.wait_ge(run.to_act, run.act_after(last) + run.n_turn + 1)
                go(last_t[:, :], act_ps[3][:, :], ACT.Copy).then_inc(run.act_freed, 1)

            run_items(run0)
            sig = sig1
            act.wait_ge(slot_in[0], 16 * (L + 3))
            act.wait_ge(slot_in[1], 64)
            for i in range(2 * DC):
                go(gw1_hi[i][:, :], slot[i // DC][:, i % DC * N:(i % DC + 1) * N], ACT.Copy).then_inc(w_high, 1)

            def turned_highs(blocks, stage, to, function):
                for c in range(blocks):
                    if c % 2 == 0:
                        act.wait_ge(sig.to_act, ACT0[stage] + c // 2 + 1)
                    else:
                        act.wait_ge(sig.to_dve, DVE0[stage] + c // 2 + 1)
                    go(to[:, c, :], (act_ps if c % 2 == 0 else dve_ps)[c // 2][:, :], function).then_inc(turned_high, 1)

            turned_highs(DC, "xt2", xn2_hi, ACT.Copy)
            for t in range(NT):
                bank = bank_of(t, ACT0["h1"])
                go(h1x[:, t, 0:4, 0:GC], bank[:, :].rearrange("p (h c) -> p h c", h=4), ACT.Copy).then_inc(sig.act_freed, 1)

            act.wait_ge(slot_in[2], 16 * (L + 2))
            act.wait_ge(slot_in[3], 16 * (L + 2))
            act.wait_ge(sig.to_act, ACT0["mask"])
            act.wait_ge(sig.to_dve, DVE0["mask"])
            for k in range(GD // P):
                ks = slice(k % 4 * D, (k % 4 + 1) * D)
                go(part_slot[k // 4][:, ks], slot[2 + k // 4][:, ks], ACT.Copy).then_inc(w_high, 1)

            def graph_branches(g):
                b = g % 2
                act.wait_ge(g_rows, g + 1)
                for m in range(NT):
                    if g >= 2:
                        act.wait_ge(g_weight, NT * (g - 2) + m + 1)
                    go(branch[:, b, 0, m, :], act_ps[2 * b][:, :], ACT.Relu, bias=neg_src[:, 0, m, g % GH:g % GH + 1], scale=-1.0)
                    go(branch[:, b, 1, m, :], act_ps[2 * b + 1][:, :], ACT.Relu, bias=neg_src[:, 1, m, g % GH:g % GH + 1],
                       scale=-1.0).then_inc(g_low, 1)

            def graph_exps(g):
                for m in range(NT):
                    act.wait_ge(g_arg, NT * g + m + 1)
                    go(branch[:, g % 2, 0, m, :], branch[:, g % 2, 0, m, :], ACT.Exp, scale=-1.0).then_inc(g_exp, 1)

            graph_branches(0)
            for g in range(GH):
                if g + 1 < GH:
                    graph_branches(g + 1)
                graph_exps(g)
            turned_highs(GD // P, "o1t", out1_hi, ACT.Relu)
            for t in range(NT):
                bank = bank_of(t, ACT0["h2"])
                go(h2x[:, t, 0:HALF], bank[:, 0:HALF], ACT.Copy).then_inc(sig.act_freed, 1)
            graph_branches(GH)
            graph_exps(GH)
            for c in range(0, DC, 2):
                bank = bank_of(c // 2, ACT0["xt3"])
                go(xn3_t[:, c, :], bank[:, :], ACT.Copy).then_inc(sig.act_freed, 1)
            run_items(run1)

        @block.vector
        def _(dve):
            sig = sig0
            vv = nc.vector
            step = [0]

            def then(ins):
                step[0] = step[0] + 1
                ins.then_inc(dve_step, 1)

            def settle():
                dve.wait_ge(dve_step, step[0])

            def bank_of(j, before):
                dve.wait_ge(sig.to_dve, before + j + 1)
                return dve_ps[j % RING]

            def normalise(source, to, arrive):
                for t in range(NT):
                    for half in range(2):
                        arrive(t, half)
                        then(vv.bn_stats(bns[:, t, half, :], source[:, t, half * HALF:(half + 1) * HALF]))
                    if t < NT - 2:
                        continue
                    ts = range(NT - 1) if t == NT - 2 else range(t, NT)
                    cut = slice(ts[0], ts[-1] + 1)
                    v_eps, y, y2 = root[:, 0, cut], rstd[:, cut], root[:, 1, cut]
                    settle()
                    vv.memset(v_eps, 0.0)
                    for j in ts:
                        then(vv.bn_aggr(mv[:, j, :], bns[:, j, :, :]))
                    settle()
                    then(vv.tensor_scalar(v_eps, mv[:, cut, 1], EPS, None, ALU.add))
                    settle()
                    then(vv.tensor_scalar(y2.bitcast(I32), v_eps.bitcast(I32), 1, None, ALU.logical_shift_right))
                    settle()
                    then(vv.tensor_scalar(y.bitcast(I32), y2.bitcast(I32), -1.0, float(0x5F3759DF), ALU.mult, ALU.add))
                    settle()
                    for _ in range(NEWTON):
                        then(vv.tensor_tensor(y2, y, y, ALU.mult))
                        settle()
                        then(vv.scalar_tensor_tensor(y2, y2, -0.5, v_eps, ALU.mult, ALU.mult))
                        settle()
                        then(vv.scalar_tensor_tensor(y, y2, 1.5, y, ALU.add, ALU.mult))
                        settle()
                    for j in ts:
                        vv.tensor_scalar(to[:, j, :], source[:, j, :], mv[:, j, 0:1], rstd[:, j:j + 1],
                                         ALU.subtract, ALU.mult).then_inc(normed, 1)

            vv.memset(zrow[:, :], 0.0).then_inc(zrow_set, 1)
            vv.memset(ones[:, :], 1.0).then_inc(const_set, 1)
            def x_arrives(t, half):
                if half == 0:
                    dve.wait_ge(in_x[t], 16)

            normalise(xres, xn, x_arrives)
            for c in range(1, DC, 2):
                bank = bank_of(c // 2, DVE0["xt0"])
                vv.tensor_copy(xn_t[:, c, :], bank[:, :]).then_inc(sig.dve_freed, 1)
            dve.wait_ge(in_ends, 48)
            then(vv.tensor_copy(ends[:, :, :], ends_i[:, :, :]))
            vv.tensor_scalar(zero[:, :], iota[:, :], 0.0, None, ALU.mult).then_inc(const_set, 1)
            dve.wait_ge(in_par, 32)
            for c in range(1, DC, 2):
                bank = bank_of(c // 2, DVE0["wn"])
                vv.tensor_scalar(nodes_t[:, c, :], bank[:, :], col("bn", c), None, ALU.add).then_inc(sig.dve_freed, 1)
            for t in range(NT):
                bank = bank_of(t, DVE0["tok0"])
                vv.tensor_copy(nodes[:, t, HALF:D], bank[:, 0:HALF]).then_inc(sig.dve_freed, 1)

            settle()

            def low_part(g, b, half):
                dve.wait_ge(ea_high, g + 1)
                c = slice(half * GROUP // 2, (half + 1) * GROUP // 2)
                last = vv.tensor_tensor(ea_lo[:, b, c, :], ea_raw[:, b, c, :], ea_hi[:, b, c, :].bitcast(F32), ALU.subtract)
                last.then_inc(ea_split, 1)

            def hot_rows(g, b, more):
                for c in range(GROUP):
                    k = g * GROUP + c
                    dve.wait_ge(chunk_done, OPENED + k - 1)
                    vv.tensor_scalar(hot_d[:, c % 2, :], iota[:, :], ends[:, 1, bass.ds(k, 1)], None, ALU.is_equal)
                    vv.tensor_scalar(hot_s[:, c % 2, :], iota[:, :], ends[:, 0, bass.ds(k, 1)], None, ALU.is_equal
                                     ).then_inc(hots, 1)
                    if more and c in (2, 5):
                        low_part(g + 1, 1 - b, c // 4)

            for half in range(2):
                low_part(0, 0, half)
            with dve.Fori(0, GROUPS // 2 - 1) as i:
                hot_rows(2 * i, 0, True)
                hot_rows(2 * i + 1, 1, True)
            hot_rows(GROUPS - 2, 0, True)
            hot_rows(GROUPS - 1, 1, False)
            for m in range(2):
                bank = bank_of(m, DVE0["edges"])
                vv.tensor_copy(sea_t[:, m, :], bank[:, :]).then_inc(sig.dve_freed, 1)
            bank = bank_of(0, DVE0["deg"])
            vv.tensor_copy(deg[:, :], bank[:, :]).then_inc(sig.dve_freed, 1)
            dve.wait_ge(sig.dve_freed, DVE0["base"])
            then(vv.tensor_copy(cpt[:, :, :], ct[:, :, :]))
            settle()
            for t in range(NT):
                then(vv.tensor_tensor(iota[:, t * P:(t + 1) * P], ident[:, :], deg[:, t * P:(t + 1) * P], ALU.mult))
            settle()
            for t in range(NT):
                own = cpt[:, t, t * P:(t + 1) * P]
                last = vv.tensor_tensor(own, own, iota[:, t * P:(t + 1) * P], ALU.add)
                if t < NT - 1:
                    then(last)
                else:
                    last.then_inc(cpt_set, 1)
            settle()
            for c in range(DC):
                bank = bank_of(c, DVE0["base"])
                vv.scalar_tensor_tensor(base_t[:, c, :], deg[:, :], col("be", c), bank[:, :], ALU.mult, ALU.add).then_inc(sig.dve_freed, 1)
            dve.wait_ge(sig.dve_freed, DVE0["rounds"])

            before = step[0]
            with dve.Fori(0, L) as l:
                v0 = DVE0["rounds"] + 24 * l
                step[0] = before + NORM_STEPS * l
                dve.wait_ge(sig.dve_freed, v0)
                for c in range(DC):
                    dve.wait_ge(nt_high, DC * l + c + 1)
                    vv.tensor_tensor(nt_lo[:, c, :], nodes_t[:, c, :], nt_hi[:, c, :].bitcast(F32), ALU.subtract).then_inc(nt_low, 1)

                def low_weights(s, k, high, done):
                    dve.wait_ge(w_high, 3 * DC * l + done + 1)
                    ks = slice(k * D, (k + 1) * D)
                    vv.tensor_tensor(part_slot[s][:, ks], slot[s][:, ks], high.bitcast(F32), ALU.subtract).then_inc(w_low, 1)

                for c in range(DC):
                    for b in (2 * c, 2 * c + 1):
                        k = b % DC
                        low_weights(2 + b // DC, k, w1_hi[k][:, :] if b < DC else part_slot[1][:, k * D:(k + 1) * D], b)
                    bank = bank_of(c, v0)
                    vv.tensor_tensor(agg_t[:, c, :], bank[:, :], base_t[:, c, :], ALU.add).then_inc(sig.dve_freed, 1)
                for c in range(DC):
                    dve.wait_ge(agg_high, DC * l + c + 1)
                    vv.tensor_tensor(agg_lo[:, c, :], agg_t[:, c, :], agg_hi[:, c, :].bitcast(F32), ALU.subtract).then_inc(agg_low, 1)
                dve.wait_ge(in_row[0], 16 * (l + 1))

                def h_arrives(t, half):
                    u = 2 * t + half
                    bank = bank_of(u, v0 + 6)
                    vv.tensor_tensor(h[:, t, half * HALF:(half + 1) * HALF], bank[:, 0:HALF],
                                     brow[:, 0, half * HALF:(half + 1) * HALF], ALU.add).then_inc(sig.dve_freed, 1)
                    dve.wait_ge(sig.dve_freed, v0 + 6 + u + 1)
                    vv.memset(root[:, 1, :], 0.0)

                normalise(h, h, h_arrives)
                for c in range(DC):
                    dve.wait_ge(sig.act_freed, ACT0["rounds"] + 10 * l + c + 1)
                    vv.tensor_tensor(h_lo[:, c, :], h_t[:, c, :], h_hi[:, c, :].bitcast(F32), ALU.subtract).then_inc(h_low, 1)
                for c in range(DC):
                    bank = bank_of(c, v0 + 14)
                    vv.scalar_tensor_tensor(nodes_t[:, c, :], bank[:, :], par[:, bass.ds(COLS["b2"] + DC * l + c, 1)],
                                            nodes_t[:, c, :], ALU.add, ALU.add).then_inc(sig.dve_freed, 1)
                for t in range(NT):
                    bank = bank_of(t, v0 + 20)
                    vv.tensor_copy(nodes[:, t, HALF:D], bank[:, 0:HALF]).then_inc(sig.dve_freed, 1)
            step[0] = before + NORM_STEPS * L

            dve.wait_ge(sig.to_act, ACT0["heads"])
            dve.wait_ge(sig.dve_freed, DVE0["v"])
            for c in range(DC):
                dve.wait_ge(nt_high, DC * L + c + 1)
                vv.tensor_tensor(na_lo[:, c, :], nodes_t[:, c, :], na_hi[c][:, :].bitcast(F32), ALU.subtract).then_inc(nt_low, 1)

            def low_of(s, k, high, done):
                dve.wait_ge(w_high, 3 * DC * L + done + 1)
                ks = slice(k * D, (k + 1) * D)
                vv.tensor_tensor(part_slot[s][:, ks], slot[s][:, ks], high.bitcast(F32), ALU.subtract).then_inc(w_low, 1)

            for k in range(DC):
                low_of(3, k, wv_hi[:, k * D:(k + 1) * D], k)
            dve.wait_ge(sig.act_freed, ACT0["heads"])
            dve.wait_ge(in_row[0], 16 * (L + 1))
            dve.wait_ge(in_x_again, 16)
            then(vv.tensor_tensor(xres[:, :, :], xres[:, :, :], nodes[:, :, :], ALU.add))
            dve.wait_ge(in_row[1], 16)
            for u in range(8):
                t, half = u // 2, u % 2
                bank = bank_of(u, DVE0["v"])
                vv.tensor_tensor(v[:, t, half * HALF:(half + 1) * HALF], bank[:, 0:HALF],
                                 brow[:, 1, half * HALF:(half + 1) * HALF], ALU.add).then_inc(sig.dve_freed, 1)
                if u == 1:
                    settle()
                    for j in range(NT):
                        then(vv.tensor_tensor(xres[:, j, :], xres[:, j, :], brow[:, 0, :], ALU.add))
                    settle()
                    vv.memset(root[:, 0, :], 0.0).then_inc(x_added, 1)
                if u >= 2:
                    low_of(1, u - 2, wq_hi[u - 2][:, :], DC + u - 2)
            for k in range(DC):
                low_of(2, k, part_slot[3][:, k * D:(k + 1) * D], 2 * DC + k)

            a0, v0 = ACT0["heads"], DVE0["heads"]

            def query(hd):
                bank = bank_of(q_unit(hd), v0)
                vv.tensor_scalar(q_t[:, hd % 2, :], bank[0:DH, :], par[0:DH, COLS["bq"] + hd:COLS["bq"] + hd + 1],
                                 float(DH) ** -0.5, ALU.add, ALU.mult).then_inc(sig.dve_freed, 1)

            def maxima(hd):
                for t in range(NT):
                    dve.wait_ge(sig.to_act, a0 + score_unit(hd) + t + 1)
                    vv.tensor_reduce(nbias[:, hd % 2, t:t + 1], act_ps[(score_unit(hd) + t) % RING][:, :], AX_X, ALU.max,
                                     negate=True).then_inc(row_max, 1)

            def divide(hd):
                dve.wait_ge(sig.act_freed, a0 + score_unit(hd) + NT)
                then(vv.reciprocal(rinv[:, hd % 2, :], rsum[:, hd % 2, :]))
                settle()
                for t in range(NT):
                    vv.tensor_scalar(prb[:, hd % 2, t, :], prb[:, hd % 2, t, :], rinv[:, hd % 2, t:t + 1], None,
                                     ALU.mult).then_inc(prob_set, 1)

            query(0)
            maxima(0)
            for hd in range(NH):
                divide(hd)
                if hd + 1 < NH:
                    query(hd + 1)
                for j in range(2):
                    bank = bank_of(turn_unit_v(hd) + j, v0)
                    wait(dve, sig.to_dve, v0 + pv_unit(hd - 1) + 1 if hd else 0)
                    vv.tensor_copy(prb_t[:, 2 * j + 1, :], bank[:, :]).then_inc(sig.dve_freed, 1)
                if hd + 1 < NH:
                    maxima(hd + 1)
                bank = bank_of(pv_unit(hd), v0)
                vv.tensor_copy(attn_t[:, hd, :], bank[0:DH, :]).then_inc(sig.dve_freed, 1)

            def add_to_x(stage, t, half):
                u = 2 * t + half
                bank = bank_of(u, DVE0[stage])
                part = xres[:, t, half * HALF:(half + 1) * HALF]
                vv.tensor_tensor(part, bank[:, 0:HALF], part, ALU.add).then_inc(sig.dve_freed, 1)
                dve.wait_ge(sig.dve_freed, DVE0[stage] + u + 1)

            def low_up(j, i):
                s = run0.up_slots[j]
                for k in range(DC):
                    ks = slice(k * D, (k + 1) * D)
                    dve.wait_ge(up_high[j], DC * i + k + 1)
                    vv.tensor_tensor(part_slot[s][:, ks], slot[s][:, ks], up_hi[j][k][:, :].bitcast(F32), ALU.subtract
                                     ).then_inc(up_low[j], 1)

            def attention_arrives(t, half):
                add_to_x("wo", t, half)
                if half == 1 and t < 2:
                    low_up(t, 0)

            settle()
            normalise(xres, xn1, attention_arrives)

            def pick_top(values, ne, to, tmp):
                shape = [P, NT, ne]
                then(vv.tensor_reduce(top4[:, :], values, AX_X, ALU.max))
                settle()
                then(vv.tensor_tensor(tmp, values, top4[:, :].unsqueeze(2).to_broadcast(shape), ALU.is_equal))
                settle()
                then(vv.tensor_tensor(tmp, tmp, prio(ne), ALU.mult))
                settle()
                then(vv.tensor_reduce(top4[:, :], tmp, AX_X, ALU.max))
                settle()
                then(vv.tensor_tensor(to, tmp, top4[:, :].unsqueeze(2).to_broadcast(shape), ALU.is_equal))
                settle()

            def prio(ne):
                return col("prio", 0, NT * 8).rearrange("p (t e) -> p t e", t=NT)[:, :, 0:ne]

            def logits(stage, ne, b0):
                bank = bank_of(0, DVE0[stage])
                vv.tensor_tensor(logit[:, :, 0:ne], bank[:, 0:NT * ne].rearrange("p (t e) -> p t e", t=NT),
                                 bg[:, b0:b0 + ne].unsqueeze(1).to_broadcast([P, NT, ne]), ALU.add).then_inc(sig.dve_freed, 1)
                dve.wait_ge(sig.dve_freed, DVE0[stage] + 1)

            def gates_turned(stage, ne):
                bank = bank_of(2, DVE0[stage])
                vv.tensor_copy(gate_t[0:ne, :], bank[0:ne, :]).then_inc(sig.dve_freed, 1)

            for c in range(1, DC, 2):
                bank = bank_of(c // 2, DVE0["xt1"])
                vv.tensor_copy(xn1_t[:, c, :], bank[:, :]).then_inc(sig.dve_freed, 1)
            dve.wait_ge(in_gate, 48)
            logits("gate0", NE0, 0)
            then(vv.tensor_reduce(top4[:, :], logit[:, :, :], AX_X, ALU.max))
            settle()
            vv.tensor_tensor(logit[:, :, :], logit[:, :, :], top4[:, :].unsqueeze(2).to_broadcast([P, NT, NE0]),
                             ALU.subtract).then_inc(logit_set, 1)
            dve.wait_ge(prob_exp, 1)
            pick_top(prob[:, :, :], NE0, pick[0][:, :, :], pick[3][:, :, :])
            then(vv.scalar_tensor_tensor(pick[1][:, :, :], pick[0][:, :, :], -2.0, prob[:, :, :], ALU.mult, ALU.add))
            settle()
            pick_top(pick[1][:, :, :], NE0, pick[2][:, :, :], pick[3][:, :, :])
            vv.tensor_tensor(sel[:, :, :], pick[2][:, :, :], pick[0][:, :, :], ALU.add).then_inc(run0.sel_set, 1)
            dve.wait_ge(run0.sel_set, 1)
            then(vv.tensor_tensor(pick[1][:, :, :], sel[:, :, :], prob[:, :, :], ALU.mult))
            settle()
            then(vv.tensor_reduce(top4[:, :], pick[1][:, :, :], AX_X, ALU.add))
            settle()
            then(vv.reciprocal(top4[:, :], top4[:, :]))
            settle()
            vv.tensor_tensor(gate[:, :, :], pick[1][:, :, :], top4[:, :].unsqueeze(2).to_broadcast([P, NT, NE0]),
                             ALU.mult).then_inc(run0.gate_set, 1)
            dve.wait_ge(run0.gate_set, 1)

            def make_plan(run, stage, choices):
                ne = run.ne
                bank = bank_of(1, DVE0[stage])
                vv.tensor_copy(count[:, :, 0:ne], bank[:, 0:(NT + 1) * ne].rearrange("p (t e) -> p t e", e=ne)).then_inc(sig.dve_freed, 1)
                dve.wait_ge(sig.dve_freed, DVE0[stage] + 2)
                then(vv.tensor_scalar(count[:, NT, 0:1], count[:, NT, 0:1], 1.0, None, ALU.max))
                settle()
                total, n, end, begin = count[:, NT, 0:ne], chunks[:, 0, 0:ne], chunks[:, 1, 0:ne], chunks[:, 2, 0:ne]
                then(vv.tensor_scalar(n, total, 0.0, None, ALU.is_gt))
                for k in range(1, NT):
                    settle()
                    then(vv.scalar_tensor_tensor(n, total, float(P * k), n, ALU.is_gt, ALU.add))
                settle()
                tri8 = col("tri8", 0, 64).rearrange("p (a b) -> p a b", a=8)[:, 0:ne, 0:ne]
                then(vv.tensor_tensor(low8[:, 0:ne, 0:ne], n.unsqueeze(1).to_broadcast([P, ne, ne]), tri8, ALU.mult))
                settle()
                then(vv.tensor_reduce(end, low8[:, 0:ne, 0:ne], AX_X, ALU.add))
                settle()
                then(vv.tensor_tensor(begin, end, n, ALU.subtract))
                iota16 = col("iota16", 0, 16)
                then(vv.tensor_tensor(low16[:, :, 0:ne], iota16.unsqueeze(2).to_broadcast([P, 16, ne]),
                                      end.unsqueeze(1).to_broadcast([P, 16, ne]), ALU.is_ge))
                settle()
                then(vv.tensor_reduce(plan[:, 0:16], low16[:, :, 0:ne], AX_X, ALU.add))
                then(vv.tensor_scalar(plan[:, 16:17], chunks[:, 1, ne - 1:ne], -1.0, None, ALU.add))
                then(vv.tensor_scalar(begin, begin, float(P), None, ALU.mult))
                settle()
                then(vv.tensor_tensor(slot_of[:, :, 0:ne], count[:, 0:NT, 0:ne], begin.unsqueeze(1).to_broadcast([P, NT, ne]), ALU.add))
                settle()
                for j, choice in enumerate(choices):
                    then(vv.tensor_tensor(pick[3][:, :, 0:ne], slot_of[:, :, 0:ne], choice[:, :, 0:ne], ALU.mult))
                    settle()
                    then(vv.tensor_reduce(pos[:, j, :], pick[3][:, :, 0:ne], AX_X, ALU.add))
                    settle()
                n = len(choices)
                then(vv.tensor_copy(pos_i[:, 0:n, :], pos[:, 0:n, :]))
                settle()
                vv.tensor_copy(plan_i[:, :], plan[:, :]).then_inc(run.plan_set, 1)
                dve.wait_ge(run.plan_set, 1)
                dve.wait_ge(in_tri, 32)
                for t in range(NT):
                    then(vv.tensor_scalar(first_sel[:, t, :], slot_iota[:, :], pos[:, 0, t:t + 1], None, ALU.is_equal))
                if run.picks == 2:
                    settle()
                    for t in range(NT):
                        then(vv.scalar_tensor_tensor(first_sel[:, t, :], slot_iota[:, :], pos[:, 1, t:t + 1], first_sel[:, t, :],
                                                     ALU.is_equal, ALU.add))
                settle()
                then(vv.scalar_tensor_tensor(pos_last[:, 0:n, :], plan[:, 16:17].unsqueeze(2).to_broadcast([P, n, NT]), -float(P),
                                             pos[:, 0:n, :], ALU.mult, ALU.add))
                settle()
                vv.memset(root[:, 0, :], 0.0).then_inc(run.first_set, 1)

            make_plan(run0, "gate0", (pick[0], pick[2]))
            for j, choice in enumerate((pick[0], pick[2])):
                then(vv.tensor_tensor(pick[3][:, :, :], gate[:, :, :], choice[:, :, :], ALU.mult))
                settle()
                then(vv.tensor_reduce(share[:, j, :], pick[3][:, :, :], AX_X, ALU.add))
                settle()
            gates_turned("gate0", NE0)
            for u in range(8):
                add_to_x("bias0", u // 2, u % 2)

            def run_items(run):
                last = dve.value_load(plan_i[0:1, 16:17], min_val=run.items_min - 1, max_val=run.items_max - 1)

                def x_in(v, i, a):
                    dve.wait_ge(run.to_dve, v + 1)
                    if run.layer == 0:
                        vv.tensor_copy(x_hi[:, HALF:D], dve_ps[2][:, 0:HALF]).then_inc(x_high, 1)
                        dve.wait_ge(x_high, i + 1)
                        vv.tensor_tensor(x_lo[:, HALF:D], dve_ps[2][:, 0:HALF], x_hi[:, HALF:D].bitcast(F32), ALU.subtract
                                         ).then_inc(run.dve_freed, 1)
                        dve.wait_ge(run.act_freed, a + 1)
                        vv.tensor_tensor(x_lo[:, 0:HALF], act_ps[3][:, 0:HALF], x_hi[:, 0:HALF].bitcast(F32), ALU.subtract
                                         ).then_inc(x_low, 1)
                        return
                    vv.tensor_copy(item_xt[:, 3:6, :].rearrange("p c n -> p (c n)"), dve_ps[2][:, 0:HALF]).then_inc(run.dve_freed, 1)

                def hidden(v):
                    for u in range(run.n_up):
                        dve.wait_ge(run.to_dve, v + 2 + u)
                        vv.tensor_copy(hid[:, u * HALF:(u + 1) * HALF], dve_ps[(3 + u) % 4][:, 0:HALF]).then_inc(run.dve_freed, 1)

                def result(v, stored, halves=(0, 1)):
                    if 0 in halves:
                        wait(dve, run.y_out, 16 * stored)
                    for half in halves:
                        dve.wait_ge(run.to_dve, v + 1 + half)
                        vv.tensor_copy(item_y[:, half * HALF:(half + 1) * HALF],
                                       dve_ps[run.down_banks[half]][:, 0:HALF]).then_inc(run.dve_freed, 1)

                def share_last():
                    for t in range(NT):
                        if run.picks == 1:
                            then(vv.tensor_scalar(last_sel[:, t, :], slot_iota[:, :], pos_last[:, 0, t:t + 1], None, ALU.is_equal))
                        else:
                            for j, to in enumerate((last_sel, last_tmp)):
                                then(vv.tensor_scalar(to[:, t, :], slot_iota[:, :], pos_last[:, j, t:t + 1], share[:, j, t:t + 1],
                                                      ALU.is_equal, ALU.mult))
                    settle()
                    if run.picks == 2:
                        then(vv.tensor_tensor(last_sel[:, :, :], last_sel[:, :, :], last_tmp[:, :, :], ALU.add))
                        settle()
                    vv.memset(root[:, 0, :], 0.0).then_inc(run.last_set, 1)

                x_in(0, 0, 0)
                share_last()
                hidden(0)

                def result_after(k, halves):
                    result(run.dve_after(k) + 1 + run.n_up, k, halves)

                def iteration(k, first=False):
                    v = run.dve_after(k)
                    if run.layer == 0:
                        low_up(0, k + 1)
                    if not first:
                        result_after(k - 1, (1,))
                    x_in(v, k + 1, run.act_after(k))
                    if run.layer == 0:
                        low_up(1, k + 1)
                    hidden(v)
                    result_after(k, (0,))

                iteration(0, True)
                with dve.Fori(1, last) as k:
                    iteration(k)
                result_after(last - 1, (1,))
                return last, lambda: result(run.dve_after(last), last)

            def add_last(run, last, t, half):
                u = 2 * t + half
                v = run.dve_after(last) + 2
                dve.wait_ge(run.to_dve, v + u + 1)
                part = xres[:, t, half * HALF:(half + 1) * HALF]
                return vv.tensor_tensor(part, dve_ps[u % RING][:, 0:HALF], part, ALU.add)

            last, last_result = run_items(run0)

            def add_gathered(t):
                dve.wait_ge(run0.gathered[t], 32)
                for j in range(2):
                    then(vv.scalar_tensor_tensor(xres[:, t, :], got[:, t, j, :], share[:, j, t:t + 1], xres[:, t, :], ALU.mult, ALU.add))
                    settle()

            def results_arrive(t, half):
                if t == NT - 1 and half == 0:
                    add_gathered(t)
                add_last(run0, last, t, half).then_inc(run0.dve_freed, 1)
                dve.wait_ge(run0.dve_freed, run0.dve_after(last) + 2 + 2 * t + half + 1)
                vv.memset(root[:, 1, :], 0.0)

            for t in range(NT - 1):
                add_gathered(t)
            last_result()
            normalise(xres, xn2, results_arrive)
            sig = sig1
            def turned_lows(c, before):
                dve.wait_ge(turned_high, before + c + 1)
                return ((act_ps[c // 2], sig.act_freed), (dve_ps[c // 2], sig.dve_freed))[c % 2]

            for c in range(DC):
                bank, freed = turned_lows(c, 0)
                vv.tensor_tensor(xn2_lo[:, c, :], bank[:, :], xn2_hi[:, c, :].bitcast(F32), ALU.subtract).then_inc(freed, 1)
            then(vv.memset(h1x[:, :, :, GC:GC + 2], 1.0))
            dve.wait_ge(in_att1, 16)

            def by_head(row):
                return row.rearrange("p (h c) -> p h c", h=GH)

            for t in range(NT):
                bank = bank_of(t, DVE0["h1"])
                vv.tensor_copy(h1x[:, t, 4:8, 0:GC], bank[:, :].rearrange("p (h c) -> p h c", h=4)).then_inc(sig.dve_freed, 1)
                dve.wait_ge(sig.act_freed, ACT0["h1"] + t + 1)
                dve.wait_ge(sig.dve_freed, DVE0["h1"] + t + 1)
                settle()
                for which in range(2):
                    then(vv.tensor_tensor(by_head(scr[:, which, :]), h1x[:, t, :, 0:GC], by_head(att1[:, which, :]), ALU.mult))
                settle()
                for which in range(2):
                    then(vv.tensor_reduce(att[:, which, t, :], by_head(scr[:, which, :]), AX_X, ALU.add))
            settle()
            then(vv.tensor_scalar(neg_src[:, 0, :, :], att[:, 0, :, :], -1.0, None, ALU.mult))
            vv.tensor_scalar(neg_src[:, 1, :, :], att[:, 0, :, :], -0.2, None, ALU.mult).then_inc(att_set, 1)
            settle()
            for t in range(NT):
                bank = bank_of(t, DVE0["mask"])
                vv.tensor_scalar(mask[:, t, :], bank[:, :], 0.0, NONE, ALU.is_equal, ALU.mult).then_inc(sig.dve_freed, 1)
            dve.wait_ge(sig.dve_freed, DVE0["gat1"])
            dve.wait_ge(att_set, 1)

            def graph_front(g, unit, v0, a_dst):
                b = g % 2
                bank = bank_of(unit, v0)
                for t in range(NT):
                    last = vv.tensor_tensor_reduce(out=unread[t][:, :], in0=bank[:, :], in1=mask[:, t, :], scale=1.0, scalar=NONE,
                                                   op0=ALU.add, op1=ALU.max, accum_out=gmax[:, b, t:t + 1])
                    if t < NT - 1:
                        then(last)
                last.then_inc(sig.dve_freed, 1)
                dve.wait_ge(sig.dve_freed, v0 + unit + 1)
                settle()
                wait(dve, g_rows, g - 1)
                then(vv.scalar_tensor_tensor(gdec[:, b, 0, :], gmax[:, b, :], FLOOR, a_dst, ALU.max, ALU.add))
                settle()
                then(vv.scalar_tensor_tensor(gdec[:, b, 1, :], gdec[:, b, 0, :], 0.2, gdec[:, b, 0, :], ALU.mult, ALU.max))
                settle()
                then(vv.tensor_tensor(gdec[:, b, 2, :], a_dst, gdec[:, b, 1, :], ALU.subtract))
                settle()
                vv.scalar_tensor_tensor(gdec[:, b, 3, :], a_dst, 0.2, gdec[:, b, 1, :], ALU.mult, ALU.subtract).then_inc(g_dec, 1)

            def graph_args(g):
                for m in range(NT):
                    dve.wait_ge(g_low, NT * g + m + 1)
                    one = branch[:, g % 2, 0, m, :]
                    vv.tensor_tensor(one, one, branch[:, g % 2, 1, m, :], ALU.min).then_inc(g_arg, 1)

            def graph_out(hd):
                w = GC + 2
                settle()
                for pair in range(2):
                    bank = bank_of(out_unit(hd) + pair, v0)
                    den = bank[:, 0:2 * w].rearrange("p (t c) -> p t c", t=2)[:, :, GC]
                    then(vv.tensor_scalar(rinv[:, 0, 2 * pair:2 * pair + 2], den, DEN_EPS, None, ALU.add))
                settle()
                then(vv.reciprocal(rinv[:, 1, :], rinv[:, 0, :]))
                settle()
                for t in range(NT):
                    bank = dve_ps[(out_unit(hd) + t // 2) % RING]
                    last = vv.scalar_tensor_tensor(out1[:, t, hd * GC:(hd + 1) * GC], bank[:, t % 2 * w:t % 2 * w + GC],
                                                   rinv[:, 1, t:t + 1], g_b1[:, hd * GC:(hd + 1) * GC], ALU.mult, ALU.add)
                    if t % 2 == 0:
                        then(last)
                    else:
                        last.then_inc(sig.dve_freed, 1)

            v0 = DVE0["gat1"]
            graph_front(0, row_unit(0), v0, att[:, 1, :, 0])
            graph_front(1, row_unit(1), v0, att[:, 1, :, 1])
            dve.wait_ge(in_gb, 32)
            for hd in range(GH):
                graph_args(hd)
                if hd + 2 < GH:
                    graph_front(hd + 2, row_unit(hd + 2), v0, att[:, 1, :, hd + 2])
                if hd:
                    graph_out(hd - 1)
            graph_out(GH - 1)
            for t in range(NT):
                then(vv.tensor_tensor(xres[:, t, :], xres[:, t, :], g_b2[:, :], ALU.add))
            for c in range(GD // P):
                bank, freed = turned_lows(c, DC)
                vv.scalar_tensor_tensor(out1_lo[:, c, :], bank[:, :], 0.0, out1_hi[:, c, :].bitcast(F32), ALU.max, ALU.subtract
                                        ).then_inc(freed, 1)
            dve.wait_ge(sig.to_dve, DVE0["h2"])
            then(vv.memset(h2x[:, :, D:D + 2], 1.0))
            dve.wait_ge(in_row[0], 16 * (L + 2))
            for t in range(NT):
                bank = bank_of(t, DVE0["h2"])
                vv.tensor_copy(h2x[:, t, HALF:D], bank[:, 0:HALF]).then_inc(sig.dve_freed, 1)
                dve.wait_ge(sig.act_freed, ACT0["h2"] + t + 1)
                dve.wait_ge(sig.dve_freed, DVE0["h2"] + t + 1)
                settle()
                for which in range(2):
                    then(vv.tensor_tensor_reduce(out=unread_sum[which][:, :],
                                                 in0=h2x[:, t, 0:D], in1=brow[:, which, :], scale=1.0, scalar=0.0,
                                                 op0=ALU.mult, op1=ALU.add, accum_out=att[:, which, t, 0:1]))
            settle()
            then(vv.tensor_scalar(neg_src[:, 0, :, 0:1], att[:, 0, :, 0:1], -1.0, None, ALU.mult))
            vv.tensor_scalar(neg_src[:, 1, :, 0:1], att[:, 0, :, 0:1], -0.2, None, ALU.mult).then_inc(att_set, 1)
            settle()
            dve.wait_ge(att_set, 2)
            dve.wait_ge(sig.dve_freed, DVE0["gat2"])
            v0 = DVE0["gat2"]
            graph_front(GH, 0, v0, att[:, 1, :, 0])
            graph_args(GH)
            for m in range(1, NT, 2):
                dve.wait_ge(g_exp, NT * GH + m + 1)
                vv.tensor_tensor(gp_t[:, GH % 2, m, :], branch[:, GH % 2, 0, m, :], ct[:, m, :], ALU.mult).then_inc(g_weight, 1)

            def graph_arrives(t, turn):
                if turn == 1:
                    return
                for half in (1, 0):
                    u = 2 * t + 1 - half
                    bank = bank_of(1 + u, v0)
                    if half == 1:
                        then(vv.tensor_scalar(rinv[:, 0, t:t + 1], bank[:, HALF:HALF + 1], DEN_EPS, None, ALU.add))
                        settle()
                        then(vv.reciprocal(rinv[:, 1, t:t + 1], rinv[:, 0, t:t + 1]))
                        settle()
                    part = xres[:, t, half * HALF:(half + 1) * HALF]
                    vv.scalar_tensor_tensor(part, bank[:, 0:HALF], rinv[:, 1, t:t + 1], part, ALU.mult, ALU.add).then_inc(sig.dve_freed, 1)
                    dve.wait_ge(sig.dve_freed, v0 + 2 + u)

            normalise(xres, xn3, graph_arrives)
            for c in range(1, DC, 2):
                bank = bank_of(c // 2, DVE0["xt3"])
                vv.tensor_copy(xn3_t[:, c, :], bank[:, :]).then_inc(sig.dve_freed, 1)
            logits("gate1", NE1, 8)
            pick_top(logit[:, :, 0:NE1], NE1, pick[0][:, :, 0:NE1], pick[3][:, :, 0:NE1])
            vv.tensor_copy(sel[:, :, 0:NE1], pick[0][:, :, 0:NE1]).then_inc(run1.sel_set, 1)
            vv.tensor_copy(gate[:, :, 0:NE1], pick[0][:, :, 0:NE1]).then_inc(run1.gate_set, 1)
            dve.wait_ge(run1.gate_set, 1)
            make_plan(run1, "gate1", (pick[0],))
            gates_turned("gate1", NE1)
            for u in range(8):
                add_to_x("bias1", u // 2, u % 2)
            last, last_result = run_items(run1)
            last_result()
            for t in range(NT):
                dve.wait_ge(run1.gathered[t], 16)
                then(vv.tensor_tensor(xres[:, t, :], xres[:, t, :], got[:, t, 0, :], ALU.add))
                settle()
                for half in range(2):
                    done = add_last(run1, last, t, half)
                    done.then_inc(run1.dve_freed, 1)
                dve.wait_ge(run1.dve_freed, run1.dve_after(last) + 2 + 2 * t + 2)
                vv.memset(root[:, 0, :], 0.0).then_inc(final, 1)

        @block.gpsimd
        def _(pool):
            pool.wait_ge(zrow_set, 1)
            pool.wait_ge(sig0.to_dve, DVE0["deg"])
            for run in (run0, run1):
                for table, first in ((run.scattered, 0), (run.results, run.items_min - 1)):
                    for half in range(2):
                        pool.dma_start(table[first * P:run.items_max * P, half * HALF:(half + 1) * HALF].rearrange("(i p) d -> p i d", p=P),
                                       zrow[:, :].unsqueeze(1).to_broadcast([P, run.items_max - first, HALF])).then_inc(run.filled, 16)

            def run_items(run, nodes_in, normed_by):
                pool.wait_ge(run.filled, 64)
                pool.wait_ge(normed, normed_by)
                pool.wait_ge(run.plan_set, 1)
                last = pool.value_load(plan_i[0:1, 16:17], min_val=run.items_min - 1, max_val=run.items_max - 1)
                for t in range(NT):
                    for j in range(run.picks):
                        pool.indirect_dma_start(out=run.scattered, out_offset=bass.IndirectOffsetOnAxis(pos_i[:, j, t:t + 1], 0),
                                                in_=nodes_in[:, t, :], in_offset=None).then_inc(run.scattered_in, 16)

                def store(i, v):
                    pool.wait_ge(run.dve_freed, v)
                    pool.dma_start(run.results[bass.ds(i * P, P), :], item_y[:, :]).then_inc(run.y_out, 16)

                store(0, run.dve_after(1))
                with pool.Fori(1, last) as k:
                    store(k, run.dve_after(k + 1))
                pool.wait_ge(run.y_out, 16 * last)
                pool.sem_inc(stood, 1)
                for t in range(NT):
                    for j in range(run.picks):
                        pool.indirect_dma_start(out=got[:, t, j, :], out_offset=None, in_=run.results,
                                                in_offset=bass.IndirectOffsetOnAxis(pos_i[:, j, t:t + 1], 0)
                                                ).then_inc(run.gathered[t], 16)

            with pool.Fori(0, L) as l:
                for k in range(DC):
                    ks = slice(k * D, (k + 1) * D)
                    pool.wait_ge(w_high, 3 * DC * l + 2 * DC + k + 1)
                    nc.gpsimd.tensor_tensor(part_slot[0][:, ks], slot[0][:, ks], part_slot[1][:, ks].bitcast(F32), ALU.subtract
                                            ).then_inc(w_low, 1)
            run_items(run0, xn1, NT * (L + 2))
            def low_of(s, block, high, done):
                pool.wait_ge(w_high, 3 * DC * L + 3 * DC + done + 1)
                nc.gpsimd.tensor_tensor(part_slot[s][:, block], slot[s][:, block], high.bitcast(F32), ALU.subtract).then_inc(w_low, 1)

            for i in range(2 * DC):
                low_of(i // DC, slice(i % DC * N, (i % DC + 1) * N), gw1_hi[i][:, :], i)
            for k in range(GD // P):
                ks = slice(k % 4 * D, (k % 4 + 1) * D)
                low_of(2 + k // 4, ks, part_slot[k // 4][:, ks], 2 * DC + k)
            for g in range(GH + 1):
                for m in range(0, NT, 2 if g == GH else 1):
                    if 2 <= g < GH:
                        pool.wait_ge(sig1.to_dve, DVE0["gat1"] + out_unit(g - 2) + 2)
                    pool.wait_ge(g_exp, NT * g + m + 1)
                    nc.gpsimd.tensor_tensor(gp_t[:, g % 2, m, :], branch[:, g % 2, 0, m, :], ct[:, m, :], ALU.mult).then_inc(g_weight, 1)
            run_items(run1, xn3, NT * (L + 4))


_OUT = ((N, D), "float32")


def kernel(**inputs):
    import numpy as np
    import concourse.bacc as bacc
    from concourse.bass_utils import run_bass_kernel_spmd

    a = {k: np.asarray(w) for k, w in inputs.items()}
    g0, e0, g1, e1 = "L0_gnn_", "L0_ffn_", "L1_gnn_", "L1_ffn_"

    def blocks(vec):
        return vec.reshape(-1, P).T

    def heads(vec):
        m = np.zeros((P, NH), np.float32)
        m[0:DH] = vec.reshape(NH, DH).T
        return m

    bqkv = a[g0 + "bqkv"]
    prio = np.tile(np.arange(8, 0, -1, dtype=np.float32), (P, NT))
    cols = np.concatenate([
        blocks(a[g0 + "bn"]), blocks(a[g0 + "be"]), blocks(a[g0 + "ln_g"]), blocks(a[g0 + "ln_b"]),
        blocks(a[g0 + "b2"]), heads(bqkv[0:D]), heads(bqkv[D:2 * D]), blocks(a[e0 + "b1"]), blocks(a[e1 + "b1"]), prio,
        np.tile(np.tril(np.ones((8, 8), np.float32)).reshape(-1), (P, 1)), np.tile(np.arange(16, dtype=np.float32), (P, 1))], axis=1)
    rows = np.concatenate([w.reshape(-1) for w in (
        a[g0 + "b1"], bqkv[2 * D:], a[g0 + "bo"], a[g1 + "b1"], a[g1 + "att_src1"], a[g1 + "att_dst1"],
        a[g1 + "b2"], a[g1 + "att_src2"], a[g1 + "att_dst2"], a[e0 + "bg"], a[e1 + "bg"])])
    arrays = {
        "x": a["x"], "src": a["src"].reshape(E // P, P).T, "dst": a["dst"].reshape(E // P, P).T,
        "edge": a["edge_attr_256"], "cols": cols, "rows": rows,
        "ident_d": np.eye(P, dtype=np.float32), "iota_d": np.arange(N, dtype=np.float32),
        "tri_d": np.triu(np.ones((P, P), np.float32), 1),
        "wn": a[g0 + "Wn"].T, "we": a[g0 + "We"].T, "w1": a[g0 + "W1"].transpose(0, 2, 1),
        "w2": a[g0 + "W2"].transpose(0, 2, 1), "wqkv": a[g0 + "Wqkv"].T, "wo": a[g0 + "Wo"].T,
        "wg0": a[e0 + "Wg"], "e0w1": a[e0 + "W1"], "e0w2": a[e0 + "W2"], "e0b2": a[e0 + "b2"],
        "gw1": a[g1 + "W1"].T, "gw2": a[g1 + "W2"].T,
        "wg1": a[e1 + "Wg"], "e1w1": a[e1 + "W1"], "e1w2": a[e1 + "W2"], "e1b2": a[e1 + "b2"],
    }
    nc = bacc.Bacc("TRN2", target_bir_lowering=False, num_devices=1)
    args, feed = [], {}
    for name, w in arrays.items():
        w = np.ascontiguousarray(w)
        feed[f"in_{name}"] = w
        args.append(nc.dram_tensor(f"in_{name}", w.shape, mybir.dt.from_np(w.dtype), kind="ExternalInput").ap())
    for name, slots in (("xs0", 15 * P), ("ys0", 15 * P), ("xs1", 7 * P), ("ys1", 7 * P)):
        args.append(nc.dram_tensor(name, (slots, D), F32, kind="Internal").ap())
    args.append(nc.dram_tensor("out_0", _OUT[0], F32, kind="ExternalOutput").ap())
    build(nc, *args)
    r = run_bass_kernel_spmd(nc, [feed], core_ids=[0])
    return r.results[0]["out_0"]
```
